# Optimizing a Trainium2 kernel written in Bass

```python
import numpy as np
import jax
import jax.numpy as jnp

def _softmax(x, axis=-1):
    return jax.nn.softmax(x, axis=axis)

def _gelu(x):
    return jax.nn.gelu(x, approximate=True)

def _silu(x):
    return jax.nn.silu(x)

def _sigmoid(x):
    return jax.nn.sigmoid(x)

def _layernorm(x, axis=-1, eps=1e-05):
    m = jnp.mean(x, axis=axis, keepdims=True)
    v = jnp.var(x, axis=axis, keepdims=True)
    return (x - m) / jnp.sqrt(v + eps)

def _scatter_add(tgt, idx, src, axis=0):
    return tgt.at[idx].add(src)

def _segment_sum(src, seg, n):
    return jax.ops.segment_sum(src, seg, n)
kernel_name = 'mk_lm_tower_d1_tok_ids1024_r4_bc403d'

def setup_inputs(seed: int=0):
    np.random.seed(seed)
    _w = jnp.asarray

    def _rec_inputs():
        import jax
        import jax.numpy as jnp
        _rk = jax.random.key(seed)
        x = jax.random.randint(jax.random.fold_in(_rk, 1), (32, 256), 0, 256, jnp.int32)
        return x
    x = _rec_inputs()

    def _L0_tok_setup():
        import jax, jax.numpy as jnp
        import numpy as np
        V, D, H, L, S, B = (256, 128, 8, 2, 256, 8)
        HD = D // H
        EPS = 1e-05

        def _make_pos_enc():
            position = np.arange(S)[:, None]
            div = np.exp(np.arange(0, D, 2) * (-np.log(10000.0) / D))
            pe = np.zeros((S, D), dtype=np.float32)
            pe[:, 0::2] = np.sin(position * div)
            pe[:, 1::2] = np.cos(position * div)
            return jnp.asarray(pe)
        _PE = _make_pos_enc()

        def _ln(x, s, b, eps=1e-06):
            m = x.mean(-1, keepdims=True)
            v = ((x - m) ** 2).mean(-1, keepdims=True)
            return (x - m) / jnp.sqrt(v + eps) * s + b

        def _causal_fft_conv(filters, x):
            n = 2 * S
            f_f = jnp.fft.rfft(filters.T, n=n, axis=-1)
            x_f = jnp.fft.rfft(x, n=n, axis=2)
            y = jnp.fft.irfft(x_f * f_f[None, :, :, None], n=n, axis=2)
            return y[:, :, :S, :].astype(x.dtype)

        def _scan_attn(x, sb, qk, qb, kk, kb, vk, vb, ok, ob, gk, gb):
            Bx, Sx, Dx = x.shape
            q = (x @ qk + qb).reshape(Bx, Sx, H, HD).transpose(0, 2, 1, 3)
            k = (x @ kk + kb).reshape(Bx, Sx, H, HD).transpose(0, 2, 1, 3) / jnp.sqrt(float(HD))
            v = (x @ vk + vb).reshape(Bx, Sx, H, HD).transpose(0, 2, 1, 3)
            k = _causal_fft_conv(sb, k)
            v = _causal_fft_conv(sb, v)
            Z = jnp.einsum('bhsd,bhse->bhsde', v, k)
            gl = Z.reshape(Bx, H, Sx, HD * HD) @ gk + gb
            gates = (jax.nn.relu(gl) ** 2 + EPS)[..., None]
            cum_gZ = jnp.cumsum(gates * Z, axis=2)
            cum_g = jnp.cumsum(gates, axis=2)
            attn = cum_gZ / (cum_g + EPS)
            o = jnp.einsum('bhsd,bhsde->bhse', q, attn)
            nrm = jnp.linalg.norm(o, axis=3, keepdims=True)
            o = o / jnp.maximum(nrm, EPS)
            o = o.transpose(0, 2, 1, 3).reshape(Bx, Sx, Dx)
            return o @ ok + ob

        def _forward(tokens, spectral_basis, embed, ln1_s, ln1_b, wq_k, wq_b, wk_k, wk_b, wv_k, wv_b, wo_k, wo_b, gate_k, gate_b, ln2_s, ln2_b, ff1_k, ff1_b, ff2_k, ff2_b, lnf_s, lnf_b, out_k, out_b):
            x = embed[tokens] + _PE[None, :, :]
            for i in range(L):
                h = _ln(x, ln1_s[i], ln1_b[i])
                h = _scan_attn(h, spectral_basis, wq_k[i], wq_b[i], wk_k[i], wk_b[i], wv_k[i], wv_b[i], wo_k[i], wo_b[i], gate_k[i], gate_b[i])
                x = x + h
                h = _ln(x, ln2_s[i], ln2_b[i])
                h = jax.nn.gelu(h @ ff1_k[i] + ff1_b[i]) @ ff2_k[i] + ff2_b[i]
                x = x + h
            x = _ln(x, lnf_s, lnf_b)
            return x @ out_k + out_b
        key = jax.random.key(seed)
        ks = jax.random.split(key, 16)

        def rn(i, shape, scale):
            return jax.random.normal(ks[i], shape, dtype=jnp.float32) * scale
        sd = 1.0 / np.sqrt(D)
        sf = 1.0 / np.sqrt(4 * D)
        return {'tokens': jax.random.randint(ks[0], (B, S), 0, V, dtype=jnp.int32), 'spectral_basis': rn(1, (S, H), 1.0 / np.sqrt(S)), 'embed': rn(2, (V, D), 0.02), 'ln1_s': jnp.ones((L, D)), 'ln1_b': jnp.zeros((L, D)), 'wq_k': rn(3, (L, D, D), sd), 'wq_b': jnp.zeros((L, D)), 'wk_k': rn(4, (L, D, D), sd), 'wk_b': jnp.zeros((L, D)), 'wv_k': rn(5, (L, D, D), sd), 'wv_b': jnp.zeros((L, D)), 'wo_k': rn(6, (L, D, D), sd), 'wo_b': jnp.zeros((L, D)), 'gate_k': rn(7, (L, HD * HD, 1), 1.0 / HD), 'gate_b': jnp.zeros((L, 1)), 'ln2_s': jnp.ones((L, D)), 'ln2_b': jnp.zeros((L, D)), 'ff1_k': rn(8, (L, D, 4 * D), sd), 'ff1_b': jnp.zeros((L, 4 * D)), 'ff2_k': rn(9, (L, 4 * D, D), sf), 'ff2_b': jnp.zeros((L, D)), 'lnf_s': jnp.ones((D,)), 'lnf_b': jnp.zeros((D,)), 'out_k': rn(10, (D, V), sd), 'out_b': jnp.zeros((V,))}
    _L0_tok_all = _L0_tok_setup()
    _L0_tok_in = {k: v for k, v in _L0_tok_all.items() if k in ('spectral_basis', 'embed', 'ln1_s', 'ln1_b', 'wq_k', 'wq_b', 'wk_k', 'wk_b', 'wv_k', 'wv_b', 'wo_k', 'wo_b', 'gate_k', 'gate_b', 'ln2_s', 'ln2_b', 'ff1_k', 'ff1_b', 'ff2_k', 'ff2_b', 'lnf_s', 'lnf_b', 'out_k', 'out_b')}
    del _L0_tok_all

    def _L0_attn_setup():
        import jax, jax.numpy as jnp
        import numpy as np
        D_MODEL = 256
        N_HEADS = 16
        D_K = 64
        key = jax.random.key(seed)
        k0, k1, k2, k3, k4 = jax.random.split(key, 5)
        B, S = (4, 1024)
        std = 0.02
        x = jax.random.normal(k0, (B, S, D_MODEL), dtype=jnp.float32)
        W_q = std * jax.random.normal(k1, (N_HEADS * D_K, D_MODEL), dtype=jnp.float32)
        W_k = std * jax.random.normal(k2, (N_HEADS * D_K, D_MODEL), dtype=jnp.float32)
        W_v = std * jax.random.normal(k3, (N_HEADS * D_K, D_MODEL), dtype=jnp.float32)
        W_o = std * jax.random.normal(k4, (D_MODEL, N_HEADS * D_K), dtype=jnp.float32)
        return {'x': x, 'W_q': W_q, 'W_k': W_k, 'W_v': W_v, 'W_o': W_o}
    _L0_attn_all = _L0_attn_setup()
    _L0_attn_in = {k: v for k, v in _L0_attn_all.items() if k in ('W_q', 'W_k', 'W_v', 'W_o')}
    del _L0_attn_all

    def _L0_ffn_setup():
        import jax, jax.numpy as jnp
        import numpy as np
        DIM = 256
        HIDDEN = 768
        SCALE = 1.0 / 127.0

        def _dequant(w_int, dtype):
            return w_int.astype(dtype) * jnp.asarray(SCALE, dtype)
        key = jax.random.key(seed)
        k_x, k_g, k_u, k_d = jax.random.split(key, 4)
        x = jax.random.normal(k_x, (4, 512, DIM), dtype=jnp.float32)
        w_gate = jax.random.randint(k_g, (HIDDEN, DIM), -127, 128, dtype=jnp.int32)
        w_up = jax.random.randint(k_u, (HIDDEN, DIM), -127, 128, dtype=jnp.int32)
        w_down = jax.random.randint(k_d, (DIM, HIDDEN), -127, 128, dtype=jnp.int32)
        return {'x': x, 'w_gate': w_gate, 'w_up': w_up, 'w_down': w_down}
    _L0_ffn_all = _L0_ffn_setup()
    _L0_ffn_in = {k: v for k, v in _L0_ffn_all.items() if k in ('w_gate', 'w_up', 'w_down')}
    del _L0_ffn_all
    return {'x': x, 'L0_tok_spectral_basis': _L0_tok_in['spectral_basis'], 'L0_tok_embed': _L0_tok_in['embed'], 'L0_tok_ln1_s': _L0_tok_in['ln1_s'], 'L0_tok_ln1_b': _L0_tok_in['ln1_b'], 'L0_tok_wq_k': _L0_tok_in['wq_k'], 'L0_tok_wq_b': _L0_tok_in['wq_b'], 'L0_tok_wk_k': _L0_tok_in['wk_k'], 'L0_tok_wk_b': _L0_tok_in['wk_b'], 'L0_tok_wv_k': _L0_tok_in['wv_k'], 'L0_tok_wv_b': _L0_tok_in['wv_b'], 'L0_tok_wo_k': _L0_tok_in['wo_k'], 'L0_tok_wo_b': _L0_tok_in['wo_b'], 'L0_tok_gate_k': _L0_tok_in['gate_k'], 'L0_tok_gate_b': _L0_tok_in['gate_b'], 'L0_tok_ln2_s': _L0_tok_in['ln2_s'], 'L0_tok_ln2_b': _L0_tok_in['ln2_b'], 'L0_tok_ff1_k': _L0_tok_in['ff1_k'], 'L0_tok_ff1_b': _L0_tok_in['ff1_b'], 'L0_tok_ff2_k': _L0_tok_in['ff2_k'], 'L0_tok_ff2_b': _L0_tok_in['ff2_b'], 'L0_tok_lnf_s': _L0_tok_in['lnf_s'], 'L0_tok_lnf_b': _L0_tok_in['lnf_b'], 'L0_tok_out_k': _L0_tok_in['out_k'], 'L0_tok_out_b': _L0_tok_in['out_b'], 'L0_attn_W_q': _L0_attn_in['W_q'], 'L0_attn_W_k': _L0_attn_in['W_k'], 'L0_attn_W_v': _L0_attn_in['W_v'], 'L0_attn_W_o': _L0_attn_in['W_o'], 'L0_ffn_w_gate': _L0_ffn_in['w_gate'], 'L0_ffn_w_up': _L0_ffn_in['w_up'], 'L0_ffn_w_down': _L0_ffn_in['w_down']}

def reference(x, L0_tok_spectral_basis, L0_tok_embed, L0_tok_ln1_s, L0_tok_ln1_b, L0_tok_wq_k, L0_tok_wq_b, L0_tok_wk_k, L0_tok_wk_b, L0_tok_wv_k, L0_tok_wv_b, L0_tok_wo_k, L0_tok_wo_b, L0_tok_gate_k, L0_tok_gate_b, L0_tok_ln2_s, L0_tok_ln2_b, L0_tok_ff1_k, L0_tok_ff1_b, L0_tok_ff2_k, L0_tok_ff2_b, L0_tok_lnf_s, L0_tok_lnf_b, L0_tok_out_k, L0_tok_out_b, L0_attn_W_q, L0_attn_W_k, L0_attn_W_v, L0_attn_W_o, L0_ffn_w_gate, L0_ffn_w_up, L0_ffn_w_down):
    import jax
    import jax.numpy as jnp

    def _L0_tok_ref(tokens, spectral_basis, embed, ln1_s, ln1_b, wq_k, wq_b, wk_k, wk_b, wv_k, wv_b, wo_k, wo_b, gate_k, gate_b, ln2_s, ln2_b, ff1_k, ff1_b, ff2_k, ff2_b, lnf_s, lnf_b, out_k, out_b):
        import jax, jax.numpy as jnp
        import numpy as np
        V, D, H, L, S, B = (256, 128, 8, 2, 256, 8)
        HD = D // H
        EPS = 1e-05

        def _make_pos_enc():
            position = np.arange(S)[:, None]
            div = np.exp(np.arange(0, D, 2) * (-np.log(10000.0) / D))
            pe = np.zeros((S, D), dtype=np.float32)
            pe[:, 0::2] = np.sin(position * div)
            pe[:, 1::2] = np.cos(position * div)
            return jnp.asarray(pe)
        _PE = _make_pos_enc()

        def _ln(x, s, b, eps=1e-06):
            m = x.mean(-1, keepdims=True)
            v = ((x - m) ** 2).mean(-1, keepdims=True)
            return (x - m) / jnp.sqrt(v + eps) * s + b

        def _causal_fft_conv(filters, x):
            n = 2 * S
            f_f = jnp.fft.rfft(filters.T, n=n, axis=-1)
            x_f = jnp.fft.rfft(x, n=n, axis=2)
            y = jnp.fft.irfft(x_f * f_f[None, :, :, None], n=n, axis=2)
            return y[:, :, :S, :].astype(x.dtype)

        def _scan_attn(x, sb, qk, qb, kk, kb, vk, vb, ok, ob, gk, gb):
            Bx, Sx, Dx = x.shape
            q = (x @ qk + qb).reshape(Bx, Sx, H, HD).transpose(0, 2, 1, 3)
            k = (x @ kk + kb).reshape(Bx, Sx, H, HD).transpose(0, 2, 1, 3) / jnp.sqrt(float(HD))
            v = (x @ vk + vb).reshape(Bx, Sx, H, HD).transpose(0, 2, 1, 3)
            k = _causal_fft_conv(sb, k)
            v = _causal_fft_conv(sb, v)
            Z = jnp.einsum('bhsd,bhse->bhsde', v, k)
            gl = Z.reshape(Bx, H, Sx, HD * HD) @ gk + gb
            gates = (jax.nn.relu(gl) ** 2 + EPS)[..., None]
            cum_gZ = jnp.cumsum(gates * Z, axis=2)
            cum_g = jnp.cumsum(gates, axis=2)
            attn = cum_gZ / (cum_g + EPS)
            o = jnp.einsum('bhsd,bhsde->bhse', q, attn)
            nrm = jnp.linalg.norm(o, axis=3, keepdims=True)
            o = o / jnp.maximum(nrm, EPS)
            o = o.transpose(0, 2, 1, 3).reshape(Bx, Sx, Dx)
            return o @ ok + ob

        def _forward(tokens, spectral_basis, embed, ln1_s, ln1_b, wq_k, wq_b, wk_k, wk_b, wv_k, wv_b, wo_k, wo_b, gate_k, gate_b, ln2_s, ln2_b, ff1_k, ff1_b, ff2_k, ff2_b, lnf_s, lnf_b, out_k, out_b):
            x = embed[tokens] + _PE[None, :, :]
            for i in range(L):
                h = _ln(x, ln1_s[i], ln1_b[i])
                h = _scan_attn(h, spectral_basis, wq_k[i], wq_b[i], wk_k[i], wk_b[i], wv_k[i], wv_b[i], wo_k[i], wo_b[i], gate_k[i], gate_b[i])
                x = x + h
                h = _ln(x, ln2_s[i], ln2_b[i])
                h = jax.nn.gelu(h @ ff1_k[i] + ff1_b[i]) @ ff2_k[i] + ff2_b[i]
                x = x + h
            x = _ln(x, lnf_s, lnf_b)
            return x @ out_k + out_b
        return _forward(tokens, spectral_basis, embed, ln1_s, ln1_b, wq_k, wq_b, wk_k, wk_b, wv_k, wv_b, wo_k, wo_b, gate_k, gate_b, ln2_s, ln2_b, ff1_k, ff1_b, ff2_k, ff2_b, lnf_s, lnf_b, out_k, out_b)

    def _L0_attn_ref(x, W_q, W_k, W_v, W_o):
        import jax, jax.numpy as jnp
        import numpy as np
        D_MODEL = 256
        N_HEADS = 16
        D_K = 64
        B, S, _ = x.shape
        H, Dk = (N_HEADS, D_K)
        q = (x @ W_q.T).reshape(B, S, H, Dk)
        k = (x @ W_k.T).reshape(B, S, H, Dk)
        v = (x @ W_v.T).reshape(B, S, H, Dk)
        scale = 1.0 / jnp.sqrt(jnp.float32(Dk))
        kv = jnp.einsum('bshd,bshe->bhde', k, v)
        attn = jnp.einsum('bshd,bhde->bshe', q, kv) * scale
        out = attn.reshape(B, S, H * Dk) @ W_o.T
        return out

    def _L0_ffn_ref(x, w_gate, w_up, w_down):
        import jax, jax.numpy as jnp
        import numpy as np
        DIM = 256
        HIDDEN = 768
        SCALE = 1.0 / 127.0

        def _dequant(w_int, dtype):
            return w_int.astype(dtype) * jnp.asarray(SCALE, dtype)
        wg = _dequant(w_gate, x.dtype)
        wu = _dequant(w_up, x.dtype)
        wd = _dequant(w_down, x.dtype)
        gate = jnp.einsum('bsd,hd->bsh', x, wg)
        up = jnp.einsum('bsd,hd->bsh', x, wu)
        h = jax.nn.silu(gate) * up
        return jnp.einsum('bsh,dh->bsd', h, wd)
    h = _L0_tok_ref(x, L0_tok_spectral_basis, L0_tok_embed, L0_tok_ln1_s, L0_tok_ln1_b, L0_tok_wq_k, L0_tok_wq_b, L0_tok_wk_k, L0_tok_wk_b, L0_tok_wv_k, L0_tok_wv_b, L0_tok_wo_k, L0_tok_wo_b, L0_tok_gate_k, L0_tok_gate_b, L0_tok_ln2_s, L0_tok_ln2_b, L0_tok_ff1_k, L0_tok_ff1_b, L0_tok_ff2_k, L0_tok_ff2_b, L0_tok_lnf_s, L0_tok_lnf_b, L0_tok_out_k, L0_tok_out_b)
    h = h + _L0_attn_ref(_layernorm(h, axis=-1), L0_attn_W_q, L0_attn_W_k, L0_attn_W_v, L0_attn_W_o)
    h = h + _L0_ffn_ref(_layernorm(h, axis=-1), L0_ffn_w_gate, L0_ffn_w_up, L0_ffn_w_down)
    return h

_drawn_inputs = setup_inputs


def setup_inputs(seed=0):
    import zlib

    import numpy as np

    out = dict(_drawn_inputs(seed))
    spreads = {'L0_tok_ln1_s': (1.0, 0.2),
     'L0_tok_ln1_b': (0.0, 0.1),
     'L0_tok_wq_b': (0.0, 0.1),
     'L0_tok_wk_b': (0.0, 0.1),
     'L0_tok_wv_b': (0.0, 0.1),
     'L0_tok_wo_b': (0.0, 0.1),
     'L0_tok_gate_b': (0.0, 0.1),
     'L0_tok_ln2_s': (1.0, 0.2),
     'L0_tok_ln2_b': (0.0, 0.1),
     'L0_tok_ff1_b': (0.0, 0.1),
     'L0_tok_ff2_b': (0.0, 0.1),
     'L0_tok_lnf_s': (1.0, 0.2),
     'L0_tok_lnf_b': (0.0, 0.1),
     'L0_tok_out_b': (0.0, 0.1)}
    factors = {}
    for name, (base, spread) in spreads.items():
        noise = np.random.default_rng([zlib.crc32(name.encode()), seed]).standard_normal(out[name].shape)
        drawn = base * np.exp(spread * noise) if base else spread * noise
        out[name] = jnp.asarray(drawn.astype(out[name].dtype))
    for name, factor in factors.items():
        out[name] = (out[name] * factor).astype(out[name].dtype)
    return out
```

```python
from contextlib import ExitStack

import concourse.bass as bass
from concourse import mybir

F32 = mybir.dt.float32
F32R = mybir.dt.float32r
I32 = mybir.dt.int32
ALU = mybir.AluOpType
ACT = mybir.ActivationFunctionType
AX_X = mybir.AxisListType.X

P = 128
BATCH, SEQ = 32, 256
C = SEQ // P
NB = 2
J = C * NB
TOK = J * P
GROUPS = BATCH // NB
STREAMS = 2
BODIES = GROUPS // STREAMS
D, V, LAYERS, HEADS = 128, 256, 2, 8
HD = D // HEADS
FF = 4 * D
FC = FF // P
EPS_LN, EPS_LN_B, EPS_NORM, EPS = 1e-6, 1e-5, 1e-5, 1e-5
HALF = HEADS // 2
FIRST, LAST = -1, BODIES - 1
RSQRT_SEED = float(0x5F3759DF)


class Signal:

    def __init__(self, sem, base, per_turn, ahead):
        self.sem, self.base, self.per_turn, self.ahead = sem, base, per_turn, ahead

    def at(self, i, k):
        return i * self.per_turn + (self.base + k)


class Semaphores:

    def __init__(self, ctx, nc):
        self.ctx, self.nc, self.live, self.retired = ctx, nc, [], []

    def one(self, name):
        return self.ctx.enter_context(self.nc.semaphore(name))

    def counted(self, name, per_turn, ahead=0, base=1):
        sem, base = self.retired.pop() if self.retired else (self.one(name), base)
        sig = Signal(sem, base, per_turn, ahead)
        self.live.append(sig)
        return sig

    def raise_new(self, eng):
        for sig in self.live:
            if sig.base == 1:
                eng.sem_inc(sig.sem)

    def retire(self, turns):
        self.retired = [(sig.sem, sig.at(turns, sig.ahead)) for sig in self.live]
        self.live = []


class Banks:

    def __init__(self, ring, products):
        self.bank, self.position = {}, {}
        self.occupants = {b: [] for b in range(8)}
        n = 0
        for name, fixed, signal, k, ahead in products:
            b = fixed
            if b is None:
                b = ring[n % len(ring)]
                n += 1
            self.bank[name] = b
            self.position[name] = len(self.occupants[b])
            self.occupants[b].append((signal, k, ahead))

    def last_reads(self, name, i):
        occupants, n = self.occupants[self.bank[name]], self.position[name]
        before = [(sig, k, ahead) for sig, k, ahead in occupants[n:]]
        earlier = [(sig, k, 0) if ahead else (sig, 0, 0) for sig, k, ahead in before] + occupants[:n]
        if i is FIRST:
            earlier = [(sig, k, shift) for sig, k, shift in occupants[:n] if shift == 1]
        elif i is LAST:
            earlier = [read for read in earlier if read[2] <= 0]
        return earlier[-1:]


def wait(eng, i, needs):
    last = {}
    for sig, k, shift in needs:
        last[sig] = max((shift, k), last.get(sig, (shift, k)))
    for sig, (shift, k) in last.items():
        value = sig.at(i, shift * sig.per_turn + k)
        if not (isinstance(value, int) and value <= sig.base):
            eng.wait_ge(sig.sem, value)


def turns(eng, order, body):
    body(FIRST, [step for step in order if step[-1]])
    with eng.Fori(0, LAST) as i:
        body(i, order)
    body(LAST, [step for step in order if not step[-1]])


def token_tower(nc, semaphores, a, h_rows):
    with ExitStack() as ctx:
        def sb(name, shape, dt=F32):
            return ctx.enter_context(nc.sbuf_tensor(name, shape, dt))

        def each(name, shape, dt=F32):
            return [sb(f"{name}{s}", shape, dt) for s in range(STREAMS)]

        def signals(name, per_turn, ahead=0, base=1):
            return [semaphores.counted(f"{name}{s}", per_turn, ahead, base) for s in range(STREAMS)]

        def sem(name):
            return semaphores.one(name)

        ident = sb("ident", [P, P])
        causal = sb("causal", [P, P])
        same_head = sb("same_head", [P, P])
        ones = sb("ones", [P, P])
        pos = sb("pos", [P, C, D])
        taps = sb("taps", [P, HEADS, SEQ])
        w_q = [[sb(f"w_q{l}{h}", [P, D], F32R) for h in "hl"] for l in range(LAYERS)]
        w_kv = [[sb(f"w_kv{l}{h}", [P, 2 * D], F32R) for h in "hl"] for l in range(LAYERS)]
        w_f1 = [[sb(f"w_f1{l}{h}", [P, FF], F32R) for h in "hl"] for l in range(LAYERS)]
        w_head = [sb(f"w_head{h}", [P, V], F32R) for h in "hl"]
        w_o = [sb(f"w_o{l}", [P, D]) for l in range(LAYERS)]
        w_f2 = [sb(f"w_f2{l}", [P, FC, D]) for l in range(LAYERS)]
        w_gate = [sb(f"w_gate{l}", [P, D]) for l in range(LAYERS)]
        b_q = sb("b_q", [P, LAYERS])
        b_kv = sb("b_kv", [P, LAYERS, 2 * D])
        b_f1 = sb("b_f1", [P, LAYERS, FC])
        b_head = sb("b_head", [P, V])
        b_o = sb("b_o", [P, LAYERS, D])
        b_f2 = sb("b_f2", [P, LAYERS, D])
        b_gate = sb("b_gate", [P, LAYERS])
        minus_half = sb("minus_half", [P, J])

        idx = each("idx", [P, J], I32)
        emb = each("emb", [P, J, D])
        x = each("x", [P, J, D])
        xn = each("xn", [P, J, D])
        stats = each("stats", [P, J, 6])
        mv = each("mv", [P, J, 2])
        var = each("var", [P, J])
        rstd = each("rstd", [P, J])
        xT = [[sb(f"xT{s}{h}", [P, TOK], F32R) for h in "hl"] for s in range(STREAMS)]
        qT = each("qT", [P, 2, TOK], F32R)
        qT_last = each("qT_last", [P, NB * P])
        kv = each("kv", [P, HEADS, C, NB, 2, HD])
        vc = each("vc", [P, J, D])
        kc = each("kc", [P, J, D])
        vT = each("vT", [P, TOK])
        vTs = [[sb(f"vTs{s}{h}", [P, TOK], F32R) for h in "hl"] for s in range(STREAMS)]
        gate = each("gate", [P, J * HEADS])
        state = each("state", [P, NB, D])
        floor = each("floor", [P, J * HEADS])
        oT = each("oT", [P, TOK])
        sq = each("sq", [P, J * HEADS, HD])
        m2 = each("m2", [P, J * HEADS])
        mh = each("mh", [P, J * HEADS])
        y = each("y", [P, J * HEADS])
        yy = each("yy", [P, J * HEADS])
        oTn = each("oTn", [P, TOK])
        gl = each("gl", [P, FC, TOK])
        h_out = each("h_out", [P, J, V])
        q_split = sb("q_split", [P, 2, HEADS, TOK], F32R)
        gk = sb("gk", [P, J, HEADS, D])
        att = sb("att", [P, 2, HEADS, P])
        gk_heads = gk[:].rearrange("p j h (g e) -> p j (h g) e", e=HD)[:, :, ::HEADS + 1, :]

        ps = [ctx.enter_context(nc.psum_tensor(f"ps{n}", [P, 512], F32)) for n in range(8)]

        loaded, prep, ready = sem("loaded"), sem("prep"), sem("ready")
        passed = sem("passed")
        L = LAYERS
        LN = 2 * L + 1
        idx_in = signals("idx_in", 16, ahead=16)
        emb_in = signals("emb_in", 16 * J, ahead=16 * J, base=0)
        q_spread = signals("q_spread", 16 * HEADS * L)
        h_stored = signals("h_stored", 16)
        x_step = signals("x_step", 1 + 4 * L)
        ln_step = signals("ln_step", 3 * LN)
        ln_rstd = signals("ln_rstd", LN)
        xn_made = signals("xn_made", LN)
        xT_low = signals("xT_low", LN)
        q_low = signals("q_low", L)
        kv_made = signals("kv_made", 2 * L)
        kc_made = signals("kc_made", 2 * L)
        vT_low = signals("vT_low", 2 * L)
        gate_step = signals("gate_step", 6 * L)
        state_step = signals("state_step", 3 * L)
        att_made = signals("att_made", 2 * J * L)
        NORM = 14
        norm_step = signals("norm_step", NORM * L)
        h_made = signals("h_made", 2)
        xT_high = signals("xT_high", LN)
        q_high = signals("q_high", 2 * L)
        vc_made = signals("vc_made", 2 * L)
        vT_made = signals("vT_made", L)
        oT_made = signals("oT_made", L)
        sq_made = signals("sq_made", L)
        oTn_made = signals("oTn_made", L)
        gl_made = signals("gl_made", FC * L)
        p_xT = signals("p_xT", LN)
        p_q = signals("p_q", L)
        p_kv = signals("p_kv", 2 * L)
        p_conv = signals("p_conv", 2 * L)
        p_vT = signals("p_vT", L)
        p_vg = signals("p_vg", L)
        p_state = signals("p_state", L)
        p_qk = signals("p_qk", 2 * J * L)
        p_av = signals("p_av", J * L)
        p_norm = signals("p_norm", L)
        p_unit = signals("p_unit", L)
        p_wo = signals("p_wo", L)
        p_f1 = signals("p_f1", FC * L)
        p_f2 = signals("p_f2", L)
        p_head = signals("p_head", 2)

        def front(s, l, ahead=0):
            return [(step, s, 2 * l if step == "ln" else l, 0, ahead)
                    for step in ("ln", "qkv", "conv", "turn_v", "gate", "state")]

        def back(s, l):
            return [("qk", s, l, 0, 0), ("qk", s, l, 1, 0), ("av", s, l, 0, 0), ("qk", s, l, 2, 0),
                    ("av", s, l, 1, 0), ("qk", s, l, 3, 0), ("av", s, l, 2, 0), ("av", s, l, 3, 0),
                    ("norm", s, l, 0, 0), ("unit", s, l, 0, 0), ("wo", s, l, 0, 0), ("ln", s, 2 * l + 1, 0, 0),
                    ("f1", s, l, 0, 0), ("f2", s, l, 0, 0)]

        def woven(long, short, after):
            out = []
            for n, step in enumerate(long):
                out.append(step)
                out += [short[k] for k in range(len(short)) if after[k] == n]
            return out

        def head(s):
            return [("ln", s, 2 * L, 0, 0), ("head", s, 0, 0, 0)]

        SIX = [1, 8, 9, 10, 11, 12]
        order = [("embed", 1, 0, 0, 0)]
        order += woven(back(0, 0), front(1, 0), SIX)
        order += woven(back(1, 0), front(0, 1), SIX)
        order += woven(back(0, 1), front(1, 1), SIX)
        order += woven(back(1, 1), head(0) + [("embed", 0, 0, 0, 1)] + front(0, 0, 1), [0, 2, 3, 4, 8, 9, 10, 11, 12])
        order += head(1)

        products = []
        for step, s, l, j, ahead in order:
            if step == "ln":
                products.append((("xT", s, l), None, xT_low[s], l + 1, ahead))
            elif step == "qkv":
                products.append((("q", s, l), None, q_low[s], l + 1, ahead))
                for n in range(2):
                    products.append((("kv", s, l, n), None, kv_made[s], 2 * l + n + 1, ahead))
            elif step == "conv":
                for n in range(2):
                    products.append((("conv", s, l, n), None,
                                     kc_made[s], 2 * l + n + 1, ahead))
            elif step == "turn_v":
                products.append((("vT", s, l), None, vT_made[s], l + 1, ahead))
            elif step == "gate":
                products.append((("vg", s, l), None, gate_step[s], 6 * l + 1, ahead))
            elif step == "state":
                products.append((("state", s, l), None, state_step[s], 3 * l + 3, ahead))
            elif step == "qk":
                for n in range(2):
                    products.append((("qk", s, l, j, n), None, att_made[s], 2 * (J * l + j) + n + 1, ahead))
            elif step == "av" and j == 0:
                products.append((("av", s, l), 7, oT_made[s], l + 1, ahead))
            elif step == "norm":
                products.append((("norm", s, l), 7, norm_step[s], NORM * (l + 1), ahead))
            elif step == "unit":
                products.append((("unit", s, l), 7, oTn_made[s], l + 1, ahead))
            elif step == "wo":
                products.append((("wo", s, l), 7, x_step[s], 4 * l + 3, ahead))
            elif step == "f1":
                for f in range(FC):
                    products.append((("f1", s, l, f), None, gl_made[s], FC * l + f + 1, ahead))
            elif step == "f2":
                products.append((("f2", s, l), None, x_step[s], 4 * l + 5, ahead))
            elif step == "head":
                for n in range(2):
                    products.append((("head", s, n), None, h_made[s], n + 1, ahead))
        banks = Banks(range(7), products)

        def bank(*name):
            return ps[banks.bank[name]]

        raw_q = xn[0][:].rearrange("p j d -> p (j d)")[:, 0:L * D].rearrange("p (l d) -> p l d", l=L)
        raw_kv = kv[0][:].rearrange("p h c b v e -> p (h c b v e)")[:, 0:L * 2 * D].rearrange("p (l d) -> p l d", l=L)
        raw_f1 = gl[0][:].rearrange("p f t -> p (f t)")[:, 0:L * FF].rearrange("p (l d) -> p l d", l=L)
        raw_head = sq[0][:].rearrange("p a e -> p (a e)")[:, 0:V]
        ln_s = sb("ln_s", [P, LN])
        ln_b = sb("ln_b", [P, LN])
        ln_b_rows = sb("ln_b_rows", [P, LN, P])

        block = ctx.enter_context(nc.Block())
        loads = [(ident[:], a["ident"]), (causal[:], a["causal"]), (same_head[:], a["same_head"]),
                 (pos[:], a["pos"].rearrange("(c p) d -> p c d", p=P)),
                 (raw_q, a["wq_k"].rearrange("l c n -> c l n")),
                 (raw_kv[:, :, 0:D], a["wk_k"].rearrange("l c n -> c l n")),
                 (raw_kv[:, :, D:2 * D], a["wv_k"].rearrange("l c n -> c l n")),
                 (raw_f1, a["ff1_k"].rearrange("l c n -> c l n")),
                 (raw_head, a["out_k"]),
                 (ln_s[:], a["ln_s"]), (ln_b[:], a["ln_b"]), (b_q[:], a["b_q"]), (b_f1[:], a["b_f1"])]
        for l in range(L):
            loads += [(w_o[l][:], a["wo_k"][l]),
                      (w_f2[l][:], a["ff2_k"][l].rearrange("(f p) n -> p f n", p=P))]
        rows = [(b_kv[:, :, 0:D], a["wk_b"]), (b_kv[:, :, D:2 * D], a["wv_b"]),
                (b_o[:], a["wo_b"]), (b_f2[:], a["ff2_b"])]
        for out, src in rows:
            loads.append((out, src.unsqueeze(0).to_broadcast([P, L, D])))
        loads.append((b_head[:], a["out_b"].unsqueeze(0).to_broadcast([P, V])))
        loads.append((b_gate[:], a["gate_b"].rearrange("l o -> o l").to_broadcast([P, L])))
        flt = a["filters"]
        delayed = att[:].rearrange("p n h t -> p (n h t)")
        flip = oTn[0][:, 0:P]
        loads.append((delayed.rearrange("p (h t) -> p h t", h=HEADS),
                      bass.AP(tensor=flt.tensor, offset=flt.offset,
                              ap=[[1, P], [P - 1 + SEQ, HEADS], [1, SEQ]])))
        loads.append((flip, a["flip"]))
        gate_loads = [(w_gate[l][HD * h:HD * h + HD, HD * h:HD * h + HD],
                       a["gate_k"][l].rearrange("(d e) o -> d (e o)", e=HD))
                      for l in range(L) for h in range(HEADS)]

        @block.sync
        def _(sp):
            semaphores.raise_new(sp)
            for out, src in loads:
                sp.dma_start(out, src).then_inc(loaded, 16)
            for s in range(STREAMS):
                sp.dma_start(idx[s][:], a["token_ids"][s]).then_inc(idx_in[s].sem, 16)
            sp.wait_ge(prep, 1)
            for out, src in gate_loads:
                sp.dma_start(out, src).then_inc(loaded, 16)
            def body(i, steps):
                for step, s, l, j, ahead in steps:
                    t = i + ahead
                    if step == "embed":
                        sp.wait_ge(emb_in[s].sem, emb_in[s].at(t, 16 * J))
                        sp.sem_inc(passed)
                        sp.dma_start(idx[s][:], a["token_ids"][t * STREAMS + (STREAMS + s)])\
                            .then_inc(idx_in[s].sem, 16)
                    elif step == "qkv":
                        sp.wait_ge(q_low[s].sem, q_low[s].at(t, l + 1))
                        sp.sem_inc(passed)
                        o = 1 - s
                        used = J * 2 * (l + 1 if s else l)
                        wait(sp, t, [(p_qk[o], used, 0)])
                        sp.sem_inc(passed)
                        for h in range(HEADS):
                            r = slice(HD * h, HD * h + HD)
                            sp.dma_start(q_split[r, :, h, :].bitcast(F32), qT[s][r, :, :].bitcast(F32)).then_inc(q_spread[s].sem, 16)
                    elif step == "head":
                        sp.wait_ge(h_made[s].sem, h_made[s].at(t, 2))
                        sp.sem_inc(passed)
                        sp.dma_start(h_rows[t * STREAMS + s], h_out[s][:]).then_inc(h_stored[s].sem, 16)
            turns(sp, order, body)
            for s in range(STREAMS):
                sp.wait_ge(h_stored[s].sem, h_stored[s].at(BODIES, 0))
                sp.wait_ge(idx_in[s].sem, idx_in[s].at(BODIES, 16))

        N_LOADS = 16 * len(loads)
        N_ALL = N_LOADS + 16 * len(gate_loads)

        @block.gpsimd
        def _(pool):
            for l in range(L):
                pool.memset(w_gate[l][:], 0.0)
            pool.memset(ones[:], 1.0)
            pool.memset(minus_half[:], -0.5)
            pool.memset(gk[:], 0.0)
            pool.memset(q_split[:].bitcast(F32), 0.0).then_inc(prep, 1)

            def gather(s):
                for j in range(J):
                    pool.indirect_dma_start(emb[s][:, j, :], None, a["embed"],
                                            bass.IndirectOffsetOnAxis(ap=idx[s][:, j:j + 1], axis=0))\
                        .then_inc(emb_in[s].sem, 16)

            for s in range(STREAMS):
                pool.wait_ge(idx_in[s].sem, idx_in[s].at(0, 16))
                gather(s)
            pool.wait_ge(ready, 1)
            def body(i, steps):
                for step, s, l, j, ahead in steps:
                    t = i + ahead
                    if step == "ln":
                        pool.wait_ge(ln_step[s].sem, ln_step[s].at(t, 3 * l + 3))
                        pool.tensor_tensor(rstd[s][:], var[s][:], minus_half[:], ALU.pow)\
                            .then_inc(ln_rstd[s].sem, 1)
                        if l < 2 * L:
                            pool.wait_ge(xn_made[s].sem, xn_made[s].at(t, l + 1))
                            bias = (b_f2 if l % 2 else b_o)[:, l // 2, :]
                            pool.tensor_tensor(x[s][:], x[s][:], bias.unsqueeze(1).to_broadcast([P, J, D]),
                                               ALU.add).then_inc(x_step[s].sem, 1)
                    elif step == "turn_v":
                        pool.wait_ge(vT_made[s].sem, vT_made[s].at(t, l + 1))
                        pool.sem_inc(passed)
                        pool.tensor_scalar(vTs[s][0][:], vT[s][:], 1.0, 0.0, ALU.mult, ALU.add)\
                            .then_inc(vT_low[s].sem, 1)
                        pool.wait_ge(vT_low[s].sem, vT_low[s].at(t, 2 * l + 1))
                        pool.tensor_tensor(vTs[s][1][:], vT[s][:], vTs[s][0][:].bitcast(F32), ALU.subtract)\
                            .then_inc(vT_low[s].sem, 1)
                    elif step == "f2" and l == 0:
                        pool.wait_ge(idx_in[s].sem, idx_in[s].at(t, 32))
                        pool.wait_ge(x_step[s].sem, x_step[s].at(t, 1))
                        pool.sem_inc(passed)
                        gather(s)
            turns(pool, order, body)
            for s in range(STREAMS):
                pool.wait_ge(emb_in[s].sem, emb_in[s].at(BODIES, 16 * J))

        @block.vector
        def _(dve):
            done = [1]

            def link(ins):
                done[0] += 1
                ins.then_inc(prep, 1)
                dve.wait_ge(prep, done[0])

            def split(pair, src):
                link(dve.tensor_copy(pair[0][:], src))
                link(dve.tensor_tensor(pair[1][:], src, pair[0][:].bitcast(F32), ALU.subtract))

            dve.wait_ge(loaded, N_ALL)
            dve.wait_ge(prep, 1)
            for u in range(LN):
                link(dve.tensor_copy(ln_b_rows[:, u, :], ln_b[:, u:u + 1].to_broadcast([P, P])))
            for l in range(L):
                link(dve.tensor_scalar(raw_kv[:, l, 0:D], raw_kv[:, l, 0:D], HD ** -0.5, None, ALU.mult))
                link(dve.tensor_scalar(b_kv[:, l, 0:D], b_kv[:, l, 0:D], HD ** -0.5, None, ALU.mult))
            dve.wait_ge(ready, 1)
            for n in range(4):
                link(dve.tensor_copy(taps[:].rearrange("p h t -> p (h t)")[:, 512 * n:512 * n + 512], ps[3 + n][:]))
            link(dve.tensor_tensor(b_q[:], b_q[:], ps[0][:, 0:L], ALU.add))
            link(dve.tensor_tensor(b_f1[:], b_f1[:], ps[0][:, L:L + L * FC].rearrange("p (l f) -> p l f", l=L),
                                   ALU.add))
            link(dve.tensor_tensor(b_kv[:], b_kv[:], ps[1][:].rearrange("p (l d) -> p l d", l=L), ALU.add))
            link(dve.tensor_tensor(b_head[:], b_head[:], ps[2][:, 0:V], ALU.add))
            for l in range(L):
                for raw, pair, u in ((raw_q, w_q[l], 2 * l), (raw_kv, w_kv[l], 2 * l), (raw_f1, w_f1[l], 2 * l + 1)):
                    link(dve.tensor_scalar(raw[:, l, :], raw[:, l, :], ln_s[:, u:u + 1], None, ALU.mult))
                    split(pair, raw[:, l, :])
            link(dve.tensor_scalar(raw_head, raw_head, ln_s[:, 2 * L:2 * L + 1], None, ALU.mult))
            split(w_head, raw_head)
            dve.tensor_copy(b_gate[:], b_gate[:]).then_inc(ready, 1)
            dve.wait_ge(ready, 2)

            def body(i, steps):
                for step, s, l, j, ahead in steps:
                    t = i + ahead
                    if step == "embed":
                        dve.wait_ge(emb_in[s].sem, emb_in[s].at(t, 16 * J))
                        for c in range(C):
                            ins = dve.tensor_tensor(x[s][:, NB * c:NB * c + NB, :], emb[s][:, NB * c:NB * c + NB, :],
                                                    pos[:, c, :].unsqueeze(1).to_broadcast([P, NB, D]), ALU.add)
                        ins.then_inc(x_step[s].sem, 1)

                    elif step == "ln":
                        dve.wait_ge(x_step[s].sem, x_step[s].at(t, 2 * l + 1))
                        for j in range(J):
                            ins = dve.bn_stats(stats[s][:, j, :], x[s][:, j, :])
                        ins.then_inc(ln_step[s].sem, 1)
                        dve.wait_ge(ln_step[s].sem, ln_step[s].at(t, 3 * l + 1))
                        dve.sem_inc(passed)
                        for j in range(J):
                            ins = dve.bn_aggr(mv[s][:, j, :], stats[s][:, j, :])
                        ins.then_inc(ln_step[s].sem, 1)
                        dve.wait_ge(ln_step[s].sem, ln_step[s].at(t, 3 * l + 2))
                        dve.tensor_scalar(var[s][:], mv[s][:, :, 1], EPS_LN, None, ALU.add)\
                            .then_inc(ln_step[s].sem, 1)
                        dve.wait_ge(ln_rstd[s].sem, ln_rstd[s].at(t, l + 1))
                        for j in range(J):
                            ins = dve.tensor_scalar(xn[s][:, j, :], x[s][:, j, :], mv[s][:, j, 0:1],
                                                    rstd[s][:, j:j + 1], ALU.subtract, ALU.mult)
                        ins.then_inc(xn_made[s].sem, 1)
                        dve.wait_ge(p_xT[s].sem, p_xT[s].at(t, l + 1))
                        dve.wait_ge(xT_high[s].sem, xT_high[s].at(t, l + 1))
                        dve.tensor_tensor(xT[s][1][:], bank("xT", s, l)[:], xT[s][0][:].bitcast(F32), ALU.subtract)\
                            .then_inc(xT_low[s].sem, 1)

                    elif step == "qkv":
                        dve.wait_ge(q_high[s].sem, q_high[s].at(t, 2 * l + 2))
                        dve.scalar_tensor_tensor(out=qT[s][:, 1, :], in0=bank("q", s, l)[:], scalar=b_q[:, l:l + 1],
                                                 in1=qT[s][:, 0, :].bitcast(F32), op0=ALU.add, op1=ALU.subtract)\
                            .then_inc(q_low[s].sem, 1)
                        for n in range(2):
                            dve.wait_ge(p_kv[s].sem, p_kv[s].at(t, 2 * l + n + 1))
                            for b in range(NB):
                                ins = dve.tensor_tensor(
                                    kv[s][:, :, n, b, :, :],
                                    bank("kv", s, l, n)[:, 2 * D * b:2 * D * b + 2 * D].rearrange(
                                        "p (v h e) -> p h v e", v=2, h=HEADS),
                                    b_kv[:, l, :].rearrange("p (v h e) -> p h v e", v=2, h=HEADS), ALU.add)
                            ins.then_inc(kv_made[s].sem, 1)

                    elif step == "conv":
                        for n in range(2):
                            dve.wait_ge(vc_made[s].sem, vc_made[s].at(t, 2 * l + n + 1))
                            src = bank("conv", s, l, n)[:].rearrange("p (h j v e) -> p h j v e", h=HALF, j=J, v=2)
                            dve.tensor_copy(kc[s][:].rearrange("p j (h e) -> p h j e", h=HEADS)[:, HALF * n:HALF * n + HALF],
                                            src[:, :, :, 0, :]).then_inc(kc_made[s].sem, 1)

                    elif step == "gate":
                        k = 6 * l
                        g = gate_step[s]
                        dve.wait_ge(p_vg[s].sem, p_vg[s].at(t, l + 1))
                        dve.wait_ge(kc_made[s].sem, kc_made[s].at(t, 2 * l + 2))
                        dve.tensor_tensor(sq[s][:].rearrange("p a e -> p (a e)"), bank("vg", s, l)[:],
                                          kc[s][:].rearrange("p j d -> p (j d)"), ALU.mult).then_inc(g.sem, 1)
                        dve.wait_ge(g.sem, g.at(t, k + 1))
                        dve.tensor_reduce(gate[s][:], sq[s][:], AX_X, ALU.add).then_inc(g.sem, 1)
                        dve.wait_ge(g.sem, g.at(t, k + 2))
                        dve.tensor_scalar(gate[s][:], gate[s][:], b_gate[:, l:l + 1], 0.0, ALU.add, ALU.max)\
                            .then_inc(g.sem, 1)
                        dve.wait_ge(g.sem, g.at(t, k + 3))
                        dve.tensor_tensor(gate[s][:], gate[s][:], gate[s][:], ALU.mult).then_inc(g.sem, 1)
                        dve.wait_ge(g.sem, g.at(t, k + 4))
                        dve.tensor_scalar(gate[s][:], gate[s][:], EPS, None, ALU.add).then_inc(g.sem, 1)
                        dve.wait_ge(g.sem, g.at(t, k + 5))
                        o = 1 - s
                        wait(dve, t, [(p_av[o], J * (l + 1 if s else l), 0)])
                        for j in range(J):
                            ins = dve.tensor_tensor(
                                gk_heads[:, j], kc[s][:, j, :].rearrange("p (h e) -> p h e", h=HEADS),
                                gate[s][:, HEADS * j:HEADS * j + HEADS].unsqueeze(2).to_broadcast([P, HEADS, HD]),
                                ALU.mult)
                        ins.then_inc(g.sem, 1)

                    elif step == "state":
                        g = state_step[s]
                        dve.wait_ge(p_state[s].sem, p_state[s].at(t, l + 1))
                        dve.tensor_scalar(floor[s][:], bank("state", s, l)[:, NB * D:NB * D + J * HEADS], EPS,
                                          EPS_NORM, ALU.add, ALU.mult).then_inc(g.sem, 1)
                        dve.wait_ge(g.sem, g.at(t, 3 * l + 1))
                        dve.tensor_tensor(floor[s][:], floor[s][:], floor[s][:], ALU.mult).then_inc(g.sem, 1)
                        dve.tensor_tensor(state[s][:], bank("state", s, l)[:, 0:NB * D].rearrange(
                            "p (b d) -> p b d", b=NB), same_head[:].unsqueeze(1).to_broadcast([P, NB, D]),
                            ALU.mult).then_inc(g.sem, 1)

                    elif step == "qk":
                        if j < 2:
                            o = 1 - s
                            wait(dve, t, [(p_av[o], J * (l + 1 if s else l), 0)])
                        else:
                            dve.wait_ge(p_av[s].sem, p_av[s].at(t, J * l + j - 1))
                        for n in range(2):
                            k = 2 * (J * l + j) + n + 1
                            dve.wait_ge(p_qk[s].sem, p_qk[s].at(t, k))
                            dve.tensor_tensor(att[:, j % 2, HALF * n:HALF * n + HALF, :],
                                              bank("qk", s, l, j, n)[:].rearrange("p (h t) -> p h t", h=HALF),
                                              causal[:].unsqueeze(1).to_broadcast([P, HALF, P]), ALU.mult)\
                                .then_inc(att_made[s].sem, 1)

                    elif step == "norm":
                        g, k = norm_step[s], NORM * l
                        dve.wait_ge(sq_made[s].sem, sq_made[s].at(t, l + 1))
                        dve.tensor_reduce(m2[s][:], sq[s][:], AX_X, ALU.add).then_inc(g.sem, 1)
                        dve.wait_ge(g.sem, g.at(t, k + 1))
                        dve.tensor_tensor(m2[s][:], m2[s][:], floor[s][:], ALU.max).then_inc(g.sem, 1)
                        dve.wait_ge(g.sem, g.at(t, k + 2))
                        dve.tensor_scalar(mh[s][:], m2[s][:], -0.5, None, ALU.mult).then_inc(g.sem, 1)
                        dve.tensor_scalar(y[s][:].bitcast(I32), m2[s][:].bitcast(I32), -0.5, RSQRT_SEED,
                                          ALU.mult, ALU.add).then_inc(g.sem, 1)
                        for n in range(3):
                            dve.wait_ge(g.sem, g.at(t, k + 4 + 3 * n))
                            dve.tensor_tensor(yy[s][:], y[s][:], y[s][:], ALU.mult).then_inc(g.sem, 1)
                            dve.wait_ge(g.sem, g.at(t, k + 5 + 3 * n))
                            dve.tensor_tensor(yy[s][:], yy[s][:], mh[s][:], ALU.mult).then_inc(g.sem, 1)
                            dve.wait_ge(g.sem, g.at(t, k + 6 + 3 * n))
                            dve.scalar_tensor_tensor(out=y[s][:], in0=yy[s][:], scalar=1.5, in1=y[s][:],
                                                     op0=ALU.add, op1=ALU.mult).then_inc(g.sem, 1)
                        dve.wait_ge(g.sem, g.at(t, k + 13))
                        dve.tensor_tensor(sq[s][:], bank("norm", s, l)[:].rearrange("p (a e) -> p a e", e=HD),
                                          y[s][:].unsqueeze(2).to_broadcast([P, J * HEADS, HD]), ALU.mult)\
                            .then_inc(g.sem, 1)

                    elif step == "wo":
                        dve.wait_ge(p_wo[s].sem, p_wo[s].at(t, l + 1))
                        dve.wait_ge(x_step[s].sem, x_step[s].at(t, 4 * l + 2))
                        dve.tensor_tensor(x[s][:], x[s][:], bank("wo", s, l)[:].rearrange("p (j d) -> p j d", j=J),
                                          ALU.add).then_inc(x_step[s].sem, 1)

                    elif step == "f2":
                        dve.wait_ge(p_f2[s].sem, p_f2[s].at(t, l + 1))
                        dve.wait_ge(x_step[s].sem, x_step[s].at(t, 4 * l + 4))
                        dve.tensor_tensor(x[s][:], x[s][:], bank("f2", s, l)[:].rearrange("p (j d) -> p j d", j=J),
                                          ALU.add).then_inc(x_step[s].sem, 1)

                    elif step == "head":
                        wait(dve, t, [(h_stored[s], 0, 0)])
                        for n in range(2):
                            dve.wait_ge(p_head[s].sem, p_head[s].at(t, n + 1))
                            dve.tensor_tensor(h_out[s][:, 2 * n:2 * n + 2, :],
                                              bank("head", s, n)[:].rearrange("p (j v) -> p j v", j=2),
                                              b_head[:].unsqueeze(1).to_broadcast([P, 2, V]), ALU.add)\
                                .then_inc(h_made[s].sem, 1)

            turns(dve, order, body)

        @block.scalar
        def _(act):
            act.wait_ge(ready, 2)
            def body(i, steps):
                for step, s, l, j, ahead in steps:
                    t = i + ahead
                    if step == "ln":
                        act.wait_ge(p_xT[s].sem, p_xT[s].at(t, l + 1))
                        act.activation(xT[s][0][:], bank("xT", s, l)[:], ACT.Copy).then_inc(xT_high[s].sem, 1)

                    elif step == "qkv":
                        act.wait_ge(p_q[s].sem, p_q[s].at(t, l + 1))
                        wait(act, t, [(q_spread[s], 16 * HEADS * l, 0)])
                        act.activation(qT[s][:, 0, :], bank("q", s, l)[:], ACT.Identity, bias=b_q[:, l:l + 1])\
                            .then_inc(q_high[s].sem, 1)
                        act.activation(qT_last[s][:], bank("q", s, l)[:, NB * P:J * P], ACT.Identity,
                                       bias=b_q[:, l:l + 1]).then_inc(q_high[s].sem, 1)

                    elif step == "conv":
                        for n in range(2):
                            act.wait_ge(p_conv[s].sem, p_conv[s].at(t, 2 * l + n + 1))
                            src = bank("conv", s, l, n)[:].rearrange("p (h j v e) -> p h j v e", h=HALF, j=J, v=2)
                            act.activation(vc[s][:].rearrange("p j (h e) -> p h j e", h=HEADS)[:, HALF * n:HALF * n + HALF],
                                           src[:, :, :, 1, :], ACT.Copy).then_inc(vc_made[s].sem, 1)

                    elif step == "turn_v":
                        act.wait_ge(p_vT[s].sem, p_vT[s].at(t, l + 1))
                        act.activation(vT[s][:], bank("vT", s, l)[:], ACT.Copy).then_inc(vT_made[s].sem, 1)

                    elif step == "norm":
                        act.wait_ge(p_av[s].sem, p_av[s].at(t, J * (l + 1)))
                        act.activation(oT[s][:], bank("av", s, l)[:], ACT.Copy).then_inc(oT_made[s].sem, 1)
                        act.wait_ge(p_norm[s].sem, p_norm[s].at(t, l + 1))
                        act.activation(sq[s][:].rearrange("p a e -> p (a e)"), bank("norm", s, l)[:], ACT.Square)\
                            .then_inc(sq_made[s].sem, 1)

                    elif step == "unit":
                        act.wait_ge(p_unit[s].sem, p_unit[s].at(t, l + 1))
                        act.activation(oTn[s][:], bank("unit", s, l)[:], ACT.Copy).then_inc(oTn_made[s].sem, 1)

                    elif step == "f1":
                        for f in range(FC):
                            act.wait_ge(p_f1[s].sem, p_f1[s].at(t, FC * l + f + 1))
                            act.activation(gl[s][:, f, :], bank("f1", s, l, f)[:], ACT.Gelu_apprx_tanh,
                                           bias=b_f1[:, l, f:f + 1]).then_inc(gl_made[s].sem, 1)

            turns(act, order, body)

        @block.tensor
        def _(pe):
            pe.wait_ge(loaded, N_ALL)
            pe.wait_ge(prep, 1 + LN + 2 * L)
            for l in range(L):
                pe.matmul(ps[0][:, l:l + 1], raw_q[:, l, :], ln_b[:, 2 * l:2 * l + 1], start=(l == 0), stop=True,
                          skip_group_check=True)
            for l in range(L):
                for f in range(FC):
                    n = L + FC * l + f
                    pe.matmul(ps[0][:, n:n + 1], raw_f1[:, l, P * f:P * f + P], ln_b[:, 2 * l + 1:2 * l + 2],
                              start=False, stop=True, skip_group_check=True)
            for l in range(L):
                pe.matmul(ps[1][:, 2 * D * l:2 * D * l + 2 * D], ln_b_rows[:, 2 * l, :], raw_kv[:, l, :],
                          start=(l == 0), stop=True, skip_group_check=True)
            pe.matmul(ps[2][:, 0:V], ln_b_rows[:, 2 * L, :], raw_head, start=True, stop=True)
            for n in range(4):
                ins = pe.matmul(ps[3 + n][:], flip, delayed[:, 512 * n:512 * n + 512], start=True, stop=True)
            ins.then_inc(ready, 1)
            pe.wait_ge(ready, 2)

            def product(out, lhsT, rhs, start=True, stop=True, **kw):
                pe.matmul(out, lhsT[0], rhs[0], start=start, stop=False, **kw)
                pe.matmul(out, lhsT[0], rhs[1], start=False, stop=False, **kw)
                return pe.matmul(out, lhsT[1], rhs[0], start=False, stop=stop, **kw)

            def body(i, steps):
                if i is not FIRST and i is not LAST:
                    pe.wait_ge(state_step[0].sem, state_step[0].at(i, 3))
                    pe.wait_ge(q_low[0].sem, q_low[0].at(i, 1))

                def claim(*name):
                    wait(pe, i, banks.last_reads(name, i))
                    return bank(*name)

                for step, s, l, j, ahead in steps:
                    t = i + ahead
                    if step == "ln":
                        pe.wait_ge(xn_made[s].sem, xn_made[s].at(t, l + 1))
                        out = claim("xT", s, l)
                        for j in range(J):
                            ins = pe.transpose(out[:, P * j:P * j + P], xn[s][:, j, :], ident[:])
                        ins.then_inc(p_xT[s].sem, 1)

                    elif step == "qkv":
                        pe.wait_ge(xT_low[s].sem, xT_low[s].at(t, 2 * l + 1))
                        out = claim("q", s, l)
                        product(out[:], [w[:] for w in w_q[l]], [t[:] for t in xT[s]]).then_inc(p_q[s].sem, 1)
                        for n in range(2):
                            out = claim("kv", s, l, n)
                            for b in range(NB):
                                c = slice(P * (NB * n + b), P * (NB * n + b) + P)
                                ins = product(out[:, 2 * D * b:2 * D * b + 2 * D], [t[:, c] for t in xT[s]],
                                              [w[:] for w in w_kv[l]])
                            ins.then_inc(p_kv[s].sem, 1)

                    elif step == "conv":
                        pe.wait_ge(kv_made[s].sem, kv_made[s].at(t, 2 * l + 2))
                        for n in range(2):
                            out = claim("conv", s, l, n)[:].rearrange("p (h w) -> p h w", h=HALF)
                            w = 2 * HD * NB
                            for h in range(HALF):
                                hh = HALF * n + h
                                src = kv[s][:, hh].rearrange("p c b v e -> p (c b v e)")
                                pe.matmul(out[:, h, :], taps[:, hh, 0:P], src, start=(h == 0), stop=True,
                                          skip_group_check=True)
                                ins = pe.matmul(out[:, h, w:2 * w], taps[:, hh, P:2 * P], src[:, 0:w], start=False,
                                                stop=True, skip_group_check=True)
                            ins.then_inc(p_conv[s].sem, 1)

                    elif step == "turn_v":
                        pe.wait_ge(vc_made[s].sem, vc_made[s].at(t, 2 * l + 2))
                        out = claim("vT", s, l)
                        for j in range(J):
                            ins = pe.transpose(out[:, P * j:P * j + P], vc[s][:, j, :], ident[:])
                        ins.then_inc(p_vT[s].sem, 1)

                    elif step == "gate":
                        pe.wait_ge(vT_made[s].sem, vT_made[s].at(t, l + 1))
                        out = claim("vg", s, l)
                        for j in range(J):
                            ins = pe.matmul(out[:, P * j:P * j + P], vT[s][:, P * j:P * j + P], w_gate[l][:],
                                            start=True, stop=True)
                        ins.then_inc(p_vg[s].sem, 1)

                    elif step == "state":
                        out = claim("state", s, l)
                        pe.wait_ge(gate_step[s].sem, gate_step[s].at(t, 6 * l + 6))
                        for b in range(NB):
                            pe.matmul(out[:, D * b:D * b + D], vc[s][:, b, :], gk_heads[:, b], start=(b == 0),
                                      stop=True, skip_group_check=True)
                        z, w = NB * D, NB * HEADS
                        pe.matmul(out[:, z:z + 2 * w], causal[:], gate[s][:], start=False, stop=False,
                                  skip_group_check=True)
                        pe.matmul(out[:, z + w:z + 2 * w], ones[:], gate[s][:, 0:w], start=False, stop=True,
                                  skip_group_check=True).then_inc(p_state[s].sem, 1)

                    elif step == "qk":
                        if j == 0:
                            pe.wait_ge(q_spread[s].sem, q_spread[s].at(t, 16 * HEADS * (l + 1)))
                            pe.wait_ge(vT_low[s].sem, vT_low[s].at(t, 2 * l + 2))
                        c = slice(P * j, P * j + P)
                        for n in range(2):
                            out = claim("qk", s, l, j, n)
                            product(out[:].rearrange("p (h t) -> p h t", h=HALF), [t[:, c] for t in vTs[s]],
                                    [q_split[:, k, HALF * n:HALF * n + HALF, c] for k in range(2)])\
                                .then_inc(p_qk[s].sem, 1)

                    elif step == "av":
                        if j == 0:
                            claim("av", s, l)
                        if j == NB:
                            pe.wait_ge(state_step[s].sem, state_step[s].at(t, 3 * l + 3))
                            pe.wait_ge(q_high[s].sem, q_high[s].at(t, 2 * l + 2))
                        out = bank("av", s, l)[:, P * j:P * j + P]
                        if j >= NB:
                            b = j - NB
                            pe.matmul(out, state[s][:, b, :], qT_last[s][:, P * b:P * b + P], start=True, stop=False)
                        for h in range(HEADS):
                            if h % HALF == 0:
                                k = 2 * (J * l + j) + h // HALF + 1
                                pe.wait_ge(att_made[s].sem, att_made[s].at(t, k))
                            ins = pe.matmul(out, gk[:, j, h, :], att[:, j % 2, h, :], start=(h == 0 and j < NB),
                                            stop=(h == HEADS - 1))
                        ins.then_inc(p_av[s].sem, 1)

                    elif step == "norm":
                        pe.wait_ge(oT_made[s].sem, oT_made[s].at(t, l + 1))
                        out = claim("norm", s, l)
                        for j in range(J):
                            ins = pe.transpose(out[:, P * j:P * j + P], oT[s][:, P * j:P * j + P], ident[:])
                        ins.then_inc(p_norm[s].sem, 1)

                    elif step == "unit":
                        pe.wait_ge(norm_step[s].sem, norm_step[s].at(t, NORM * (l + 1)))
                        out = claim("unit", s, l)
                        for j in range(J):
                            o = sq[s][:, HEADS * j:HEADS * j + HEADS, :].rearrange("p h e -> p (h e)")
                            ins = pe.transpose(out[:, P * j:P * j + P], o, ident[:])
                        ins.then_inc(p_unit[s].sem, 1)

                    elif step == "wo":
                        pe.wait_ge(oTn_made[s].sem, oTn_made[s].at(t, l + 1))
                        out = claim("wo", s, l)
                        for j in range(J):
                            ins = pe.matmul(out[:, D * j:D * j + D], oTn[s][:, P * j:P * j + P], w_o[l][:],
                                            start=True, stop=True)
                        ins.then_inc(p_wo[s].sem, 1)

                    elif step == "f1":
                        pe.wait_ge(xT_low[s].sem, xT_low[s].at(t, 2 * l + 2))
                        for f in range(FC):
                            out = claim("f1", s, l, f)
                            product(out[:], [w[:, P * f:P * f + P] for w in w_f1[l]], [t[:] for t in xT[s]])\
                                .then_inc(p_f1[s].sem, 1)

                    elif step == "f2":
                        out = claim("f2", s, l)
                        for f in range(FC):
                            pe.wait_ge(gl_made[s].sem, gl_made[s].at(t, FC * l + f + 1))
                            for j in range(J):
                                ins = pe.matmul(out[:, D * j:D * j + D], gl[s][:, f, P * j:P * j + P],
                                                w_f2[l][:, f, :], start=(f == 0 and j == 0), stop=(f == FC - 1),
                                                skip_group_check=True)
                        ins.then_inc(p_f2[s].sem, 1)

                    elif step == "head":
                        pe.wait_ge(xT_low[s].sem, xT_low[s].at(t, LN))
                        for n in range(2):
                            out = claim("head", s, n)
                            for b in range(2):
                                c = slice(P * (2 * n + b), P * (2 * n + b) + P)
                                ins = product(out[:, V * b:V * b + V], [t[:, c] for t in xT[s]],
                                              [w[:] for w in w_head])
                            ins.then_inc(p_head[s].sem, 1)

            turns(pe, order, body)


DM = V
KC = DM // P
AH, DK = 16, 64
PAIRS = AH * DK // P
HID = 768
HC = HID // P
DEQUANT = 1.0 / 127.0
STAGE = 1024


def attention_and_mlp(nc, semaphores, a, h_rows, out_rows):
    with ExitStack() as ctx:
        def sb(name, shape, dt=F32):
            return ctx.enter_context(nc.sbuf_tensor(name, shape, dt))

        def pair(name, shape):
            return [sb(name + h, shape, F32R) for h in ("_high", "_low")]

        def each(name, shape, dt=F32):
            return [sb(f"{name}{s}", shape, dt) for s in range(STREAMS)]

        def signals(name, per_turn):
            return [semaphores.counted(f"b_{name}{s}", per_turn) for s in range(STREAMS)]

        def sem(name):
            return semaphores.one(name)

        ident = sb("ident_b", [P, P])
        minus_half = sb("minus_half_b", [P, J])
        wv = pair("wv", [P, KC, AH * DK])
        wk = sb("wk", [P, KC, AH * DK])
        wo = pair("wo", [P, PAIRS, DM])
        wq = pair("wq", [P, PAIRS, DM])
        wg = pair("wg", [P, KC, HID])
        wu = pair("wu", [P, KC, HID])
        wd = pair("wd", [P, HC, DM])

        h = each("h", [P, J, DM])
        xn = each("bxn", [P, J, DM])
        xns = [pair(f"xns{s}", [P, J, DM]) for s in range(STREAMS)]
        xT = [pair(f"bxT{s}", [P, KC, TOK]) for s in range(STREAMS)]
        stats = each("bstats", [P, J, 6])
        mv = each("bmv", [P, J, 2])
        var = each("bvar", [P, J])
        rstd = each("brstd", [P, J])
        gram = [pair(f"gram{b}", [P, KC, DM]) for b in range(NB)]
        t1 = sb("t1", [P, KC, AH * DK])
        kvs = pair("kvs", [P, PAIRS, P])
        r = pair("r", [P, PAIRS, DM])
        m = [pair(f"m{b}", [P, KC, DM]) for b in range(NB)]
        silu = sb("silu", [P, 2, TOK])
        hid = sb("hid", [P, 2, TOK])
        hids = pair("hids", [P, 2, TOK])

        ps = [ctx.enter_context(nc.psum_tensor(f"bps{n}", [P, 512], F32)) for n in range(8)]

        direct, cleared = sem("b_direct"), sem("b_cleared")
        passed = sem("b_passed")
        scaled, split_high, split_low = sem("b_scaled"), sem("b_split_high"), sem("b_split_low")
        h_in = signals("h_in", 16)
        out_sent = signals("out_sent", 16 * NB)
        h_step = signals("h_step", NB + 2)
        ln_step = signals("ln_step", 6)
        ln_rstd = signals("ln_rstd", 2)
        xn_made = signals("xn_made", 2)
        xn_high = signals("xn_high", 1)
        xn_low = signals("xn_low", 1)
        xT_high = signals("xT_high", 2 * KC)
        xT_low = signals("xT_low", 2 * KC)
        gram_high, gram_low = signals("gram_high", NB), signals("gram_low", NB)
        t1_even, t1_odd = signals("t1_even", 2 * NB), signals("t1_odd", 2 * NB)
        kvs_high, kvs_low = signals("kvs_high", 2 * NB), signals("kvs_low", 2 * NB)
        r_high, r_low = signals("r_high", 4 * NB), signals("r_low", 4 * NB)
        m_high, m_low = signals("m_high", NB), signals("m_low", NB)
        silu_made = signals("silu_made", HC)
        hid_made, hid_high, hid_low = signals("hid_made", HC), signals("hid_high", HC), signals("hid_low", HC)
        p_xT = signals("p_xT", 2 * KC)
        p_gram = signals("p_gram", NB)
        p_t1 = signals("p_t1", 4 * NB)
        p_kv = signals("p_kv", 2 * NB)
        p_r = signals("p_r", 4 * NB)
        p_m = signals("p_m", NB)
        p_attn = signals("p_attn", NB)
        p_gate, p_up, p_down = signals("p_gate", HC), signals("p_up", HC), signals("p_down", HC)

        def attention(s):
            steps = [("ln", s, 0)]
            for b in range(NB):
                steps += [("gram", s, b)]
            for b in range(NB):
                steps += [("t1", s, b), ("kv", s, b), ("r", s, b), ("m", s, b), ("attn", s, b)]
            return steps

        def mlp(s):
            steps = [("ln", s, 1), ("up", s, 0)]
            for f in range(1, HC):
                steps += [("up", s, f), ("down", s, f - 1)]
            return steps + [("down", s, HC - 1), ("add", s, 0)]

        def woven(long, short):
            out, n = [], 0
            for k, step in enumerate(long):
                out.append(step)
                want = (k + 1) * len(short) // len(long)
                out += short[n:want]
                n = want
            return out

        order = attention(0) + woven(attention(1), mlp(0)) + mlp(1)

        products = []
        for step, s, b in order:
            if step == "ln":
                for k in range(KC):
                    products.append((("xT", s, b, k), None, xT_low[s], KC * b + k + 1, 0))
            elif step == "gram":
                products.append((("gram", s, b), None, gram_low[s], b + 1, 0))
            elif step == "t1":
                for n in range(2):
                    products.append((("t1", s, b, n, 0), None, t1_even[s], 2 * b + n + 1, 0))
                    products.append((("t1", s, b, n, 1), None, t1_odd[s], 2 * b + n + 1, 0))
            elif step == "kv":
                for n in range(2):
                    products.append((("kv", s, b, n), None, kvs_low[s], 2 * b + n + 1, 0))
            elif step == "r":
                for n in range(4):
                    products.append((("r", s, b, n), None, r_low[s], 4 * b + n + 1, 0))
            elif step == "m":
                products.append((("m", s, b), None, m_low[s], b + 1, 0))
            elif step == "attn":
                products.append((("attn", s, b), None, h_step[s], b + 1, 0))
            elif step == "up":
                products.append((("gate", s, b), None, silu_made[s], b + 1, 0))
                products.append((("up", s, b), None, hid_made[s], b + 1, 0))
            elif step == "down" and b == 0:
                for n in range(2):
                    products.append((("down", s, n), 6 + n, h_step[s], NB + n + 1, 0))
        banks = Banks(range(6), products)

        def bank(*name):
            return ps[banks.bank[name]]

        stages = [t[:].rearrange("p j d -> p (j d)") for t in (h[0], h[1], xn[0], xn[1])]
        stages += [t1[:, k, :] for k in range(KC)]
        landed = [sem(f"b_landed{n}") for n in range(len(stages))]
        pieces = []
        for w, src, is_int in ((wv, "W_vT", False), (wg, "w_gateT", True), (wu, "w_upT", True),
                               (wo, "W_oT", False), (wq, "W_q", False), (wd, "w_downT", True)):
            K, N = w[0].shape[1], w[0].shape[2]
            per = STAGE // N
            view = a[src].rearrange("(k p) n -> p k n", p=P)
            for k in range(0, K, per):
                pieces.append((w, k, min(per, K - k), N, view, is_int))

        def stage(n, dt=F32):
            _, _, cnt, N, _, _ = pieces[n]
            t = stages[n % len(stages)][:, 0:cnt * N]
            if dt != F32:
                t = t.bitcast(dt)
            return t.rearrange("p (k n) -> p k n", n=N)

        block = ctx.enter_context(nc.Block())

        @block.sync
        def _(sp):
            sp.dma_start(ident[:], a["ident"]).then_inc(direct, 16)
            for n, (w, k, cnt, N, view, is_int) in enumerate(pieces):
                if n >= len(stages):
                    sp.wait_ge(split_low, n - len(stages) + 1)
                sp.dma_start(stage(n, I32 if is_int else F32), view[:, k:k + cnt, :]).then_inc(landed[n % len(stages)], 16)
            sp.dma_start(wk[:], a["W_kT"].rearrange("(k p) n -> p k n", p=P)).then_inc(direct, 16)
            sp.wait_ge(split_low, len(pieces))
            with sp.Fori(0, BODIES) as i:
                for s in range(STREAMS):
                    sp.wait_ge(out_sent[s].sem, out_sent[s].at(i, 0))
                    sp.sem_inc(passed)
                    sp.dma_start(h[s][:], h_rows[i * STREAMS + s]).then_inc(h_in[s].sem, 16)
                for step, s, b in order:
                    if step == "add":
                        sp.wait_ge(h_step[s].sem, h_step[s].at(i, NB + 2))
                        sp.sem_inc(passed)
                        for b in range(NB):
                            sp.dma_start(out_rows[i * STREAMS + s, b], h[s][:, b::NB, :])\
                                .then_inc(out_sent[s].sem, 16)
            for s in range(STREAMS):
                sp.wait_ge(out_sent[s].sem, out_sent[s].at(BODIES, 0))

        @block.gpsimd
        def _(pool):
            pool.memset(minus_half[:], -0.5)
            pool.memset(kvs[0][:].bitcast(F32), 0.0)
            pool.memset(kvs[1][:].bitcast(F32), 0.0).then_inc(cleared, 1)
            with pool.Fori(0, BODIES) as i:
                for step, s, b in order:
                    if step == "ln":
                        pool.wait_ge(ln_step[s].sem, ln_step[s].at(i, 3 * b + 3))
                        pool.tensor_tensor(rstd[s][:], var[s][:], minus_half[:], ALU.pow)\
                            .then_inc(ln_rstd[s].sem, 1)
                        if b == 0:
                            pool.wait_ge(xn_made[s].sem, xn_made[s].at(i, 1))
                            pool.sem_inc(passed)
                            pool.tensor_scalar(xns[s][0][:], xn[s][:], 1.0, 0.0, ALU.mult, ALU.add)\
                                .then_inc(xn_high[s].sem, 1)
                    elif step == "up":
                        f = b
                        pool.wait_ge(hid_high[s].sem, hid_high[s].at(i, f + 1))
                        pool.tensor_tensor(hids[1][:, f % 2, :], hid[:, f % 2, :], hids[0][:, f % 2, :].bitcast(F32),
                                           ALU.subtract).then_inc(hid_low[s].sem, 1)

        @block.vector
        def _(dve):
            for n, (w, k, cnt, N, view, is_int) in enumerate(pieces):
                if is_int:
                    dve.wait_ge(landed[n % len(stages)], 16 * (n // len(stages) + 1))
                    dve.tensor_scalar(stage(n), stage(n, I32), DEQUANT, None, ALU.mult).then_inc(scaled, 1)
                dve.wait_ge(split_high, n + 1)
                dve.tensor_tensor(w[1][:, k:k + cnt, :], stage(n), w[0][:, k:k + cnt, :].bitcast(F32),
                                  ALU.subtract).then_inc(split_low, 1)
            dve.wait_ge(split_low, len(pieces))
            dve.wait_ge(cleared, 1)

            with dve.Fori(0, BODIES) as i:
                for step, s, b in order:
                    if step == "ln":
                        if b == 0:
                            dve.wait_ge(h_in[s].sem, h_in[s].at(i, 16))
                        else:
                            dve.wait_ge(h_step[s].sem, h_step[s].at(i, NB))
                        for j in range(J):
                            ins = dve.bn_stats(stats[s][:, j, :], h[s][:, j, :])
                        ins.then_inc(ln_step[s].sem, 1)
                        dve.wait_ge(ln_step[s].sem, ln_step[s].at(i, 3 * b + 1))
                        dve.sem_inc(passed)
                        for j in range(J):
                            ins = dve.bn_aggr(mv[s][:, j, :], stats[s][:, j, :])
                        ins.then_inc(ln_step[s].sem, 1)
                        dve.wait_ge(ln_step[s].sem, ln_step[s].at(i, 3 * b + 2))
                        dve.tensor_scalar(var[s][:], mv[s][:, :, 1], EPS_LN_B, None, ALU.add)\
                            .then_inc(ln_step[s].sem, 1)
                        dve.wait_ge(ln_rstd[s].sem, ln_rstd[s].at(i, b + 1))
                        for j in range(J):
                            ins = dve.tensor_scalar(xn[s][:, j, :], h[s][:, j, :], mv[s][:, j, 0:1],
                                                    rstd[s][:, j:j + 1], ALU.subtract, ALU.mult)
                        ins.then_inc(xn_made[s].sem, 1)
                        for k in range(KC):
                            dve.wait_ge(xT_high[s].sem, xT_high[s].at(i, KC * b + k + 1))
                            dve.tensor_tensor(xT[s][1][:, k, :], bank("xT", s, b, k)[:],
                                              xT[s][0][:, k, :].bitcast(F32), ALU.subtract)\
                                .then_inc(xT_low[s].sem, 1)
                        if b == 0:
                            dve.wait_ge(xn_high[s].sem, xn_high[s].at(i, 1))
                            dve.tensor_tensor(xns[s][1][:], xn[s][:], xns[s][0][:].bitcast(F32), ALU.subtract)\
                                .then_inc(xn_low[s].sem, 1)

                    elif step == "gram":
                        dve.wait_ge(gram_high[s].sem, gram_high[s].at(i, b + 1))
                        dve.tensor_tensor(gram[b][1][:].rearrange("p k n -> p (k n)"), bank("gram", s, b)[:],
                                          gram[b][0][:].rearrange("p k n -> p (k n)").bitcast(F32), ALU.subtract)\
                            .then_inc(gram_low[s].sem, 1)

                    elif step == "t1":
                        for n in range(2):
                            dve.wait_ge(p_t1[s].sem, p_t1[s].at(i, 4 * b + 2 * n + 2))
                            dve.tensor_copy(t1[:, 1, 512 * n:512 * n + 512], bank("t1", s, b, n, 1)[:])\
                                .then_inc(t1_odd[s].sem, 1)

                    elif step == "kv":
                        for n in range(2):
                            dve.wait_ge(kvs_high[s].sem, kvs_high[s].at(i, 2 * b + n + 1))
                            src = bank("kv", s, b, n)[:].rearrange("p (q d) -> p q d", d=P)
                            for e in range(2):
                                r_, c_ = slice(DK * e, DK * e + DK), slice(DK * e, DK * e + DK)
                                ins = dve.scalar_tensor_tensor(
                                    out=kvs[1][r_, 4 * n:4 * n + 4, c_], in0=src[r_, :, c_], scalar=DK ** -0.5,
                                    in1=kvs[0][r_, 4 * n:4 * n + 4, c_].bitcast(F32), op0=ALU.mult,
                                    op1=ALU.subtract)
                            ins.then_inc(kvs_low[s].sem, 1)

                    elif step == "r":
                        for n in range(4):
                            dve.wait_ge(r_high[s].sem, r_high[s].at(i, 4 * b + n + 1))
                            dve.tensor_tensor(r[1][:, 2 * n:2 * n + 2, :].rearrange("p k n -> p (k n)"),
                                              bank("r", s, b, n)[:],
                                              r[0][:, 2 * n:2 * n + 2, :].rearrange("p k n -> p (k n)").bitcast(F32),
                                              ALU.subtract).then_inc(r_low[s].sem, 1)

                    elif step == "m":
                        dve.wait_ge(m_high[s].sem, m_high[s].at(i, b + 1))
                        dve.tensor_tensor(m[b][1][:].rearrange("p k n -> p (k n)"), bank("m", s, b)[:],
                                          m[b][0][:].rearrange("p k n -> p (k n)").bitcast(F32), ALU.subtract)\
                            .then_inc(m_low[s].sem, 1)

                    elif step == "attn":
                        dve.wait_ge(p_attn[s].sem, p_attn[s].at(i, b + 1))
                        dve.tensor_tensor(h[s][:, b::NB, :], h[s][:, b::NB, :],
                                          bank("attn", s, b)[:].rearrange("p (c n) -> p c n", c=C), ALU.add)\
                            .then_inc(h_step[s].sem, 1)

                    elif step == "up":
                        f = b
                        dve.wait_ge(p_up[s].sem, p_up[s].at(i, f + 1))
                        dve.wait_ge(silu_made[s].sem, silu_made[s].at(i, f + 1))
                        o = 1 - s
                        if f < 2:
                            dve.wait_ge(hid_low[o].sem, hid_low[o].at(i, HC * s))
                        else:
                            dve.wait_ge(hid_low[s].sem, hid_low[s].at(i, f - 1))
                        dve.tensor_tensor(hid[:, f % 2, :], silu[:, f % 2, :], bank("up", s, f)[:], ALU.mult)\
                            .then_inc(hid_made[s].sem, 1)

                    elif step == "add":
                        dve.wait_ge(p_down[s].sem, p_down[s].at(i, HC))
                        for n in range(2):
                            dve.tensor_tensor(h[s][:, 2 * n:2 * n + 2, :], h[s][:, 2 * n:2 * n + 2, :],
                                              bank("down", s, n)[:].rearrange("p (j n) -> p j n", j=2), ALU.add)\
                                .then_inc(h_step[s].sem, 1)

        @block.scalar
        def _(act):
            n_int = 0
            for n, (w, k, cnt, N, view, is_int) in enumerate(pieces):
                if is_int:
                    n_int += 1
                    act.wait_ge(scaled, n_int)
                else:
                    act.wait_ge(landed[n % len(stages)], 16 * (n // len(stages) + 1))
                act.activation(w[0][:, k:k + cnt, :], stage(n), ACT.Copy).then_inc(split_high, 1)
            act.wait_ge(cleared, 1)
            act.wait_ge(split_low, len(pieces))
            with act.Fori(0, BODIES) as i:
                for step, s, b in order:
                    if step == "ln":
                        for k in range(KC):
                            act.wait_ge(p_xT[s].sem, p_xT[s].at(i, KC * b + k + 1))
                            act.activation(xT[s][0][:, k, :], bank("xT", s, b, k)[:], ACT.Copy)\
                                .then_inc(xT_high[s].sem, 1)

                    elif step == "gram":
                        act.wait_ge(p_gram[s].sem, p_gram[s].at(i, b + 1))
                        act.activation(gram[b][0][:].rearrange("p k n -> p (k n)"), bank("gram", s, b)[:], ACT.Copy)\
                            .then_inc(gram_high[s].sem, 1)

                    elif step == "t1":
                        for n in range(2):
                            act.wait_ge(p_t1[s].sem, p_t1[s].at(i, 4 * b + 2 * n + 1))
                            act.activation(t1[:, 0, 512 * n:512 * n + 512], bank("t1", s, b, n, 0)[:], ACT.Copy)\
                                .then_inc(t1_even[s].sem, 1)

                    elif step == "kv":
                        for n in range(2):
                            act.wait_ge(p_kv[s].sem, p_kv[s].at(i, 2 * b + n + 1))
                            src = bank("kv", s, b, n)[:].rearrange("p (q d) -> p q d", d=P)
                            for e in range(2):
                                r_, c_ = slice(DK * e, DK * e + DK), slice(DK * e, DK * e + DK)
                                ins = act.activation(kvs[0][r_, 4 * n:4 * n + 4, c_], src[r_, :, c_], ACT.Copy,
                                                     scale=DK ** -0.5)
                            ins.then_inc(kvs_high[s].sem, 1)

                    elif step == "r":
                        for n in range(4):
                            act.wait_ge(p_r[s].sem, p_r[s].at(i, 4 * b + n + 1))
                            act.activation(r[0][:, 2 * n:2 * n + 2, :].rearrange("p k n -> p (k n)"),
                                           bank("r", s, b, n)[:], ACT.Copy).then_inc(r_high[s].sem, 1)

                    elif step == "m":
                        act.wait_ge(p_m[s].sem, p_m[s].at(i, b + 1))
                        act.activation(m[b][0][:].rearrange("p k n -> p (k n)"), bank("m", s, b)[:], ACT.Copy)\
                            .then_inc(m_high[s].sem, 1)

                    elif step == "up":
                        f, o = b, 1 - s
                        act.wait_ge(p_gate[s].sem, p_gate[s].at(i, f + 1))
                        if f < 2:
                            act.wait_ge(hid_made[o].sem, hid_made[o].at(i, HC * s))
                        else:
                            act.wait_ge(hid_made[s].sem, hid_made[s].at(i, f - 1))
                        act.activation(silu[:, f % 2, :], bank("gate", s, f)[:], ACT.Silu)\
                            .then_inc(silu_made[s].sem, 1)
                        act.wait_ge(hid_made[s].sem, hid_made[s].at(i, f + 1))
                        if f < 2:
                            act.wait_ge(p_down[o].sem, p_down[o].at(i, HC * s))
                        else:
                            act.wait_ge(p_down[s].sem, p_down[s].at(i, f - 1))
                        act.activation(hids[0][:, f % 2, :], hid[:, f % 2, :], ACT.Copy)\
                            .then_inc(hid_high[s].sem, 1)

        @block.tensor
        def _(pe):
            pe.wait_ge(direct, 32)
            pe.wait_ge(split_low, len(pieces))
            pe.wait_ge(cleared, 1)

            def product(out, lhsT, rhs, start=True, stop=True, **kw):
                pe.matmul(out, lhsT[0], rhs[0], start=start, stop=False, **kw)
                pe.matmul(out, lhsT[0], rhs[1], start=False, stop=False, **kw)
                return pe.matmul(out, lhsT[1], rhs[0], start=False, stop=stop, **kw)

            with pe.Fori(0, BODIES) as i:
                def claim(*name, inputs=()):
                    wait(pe, i, [*inputs, *banks.last_reads(name, i)])
                    return bank(*name)

                for step, s, b in order:
                    if step == "ln":
                        pe.wait_ge(xn_made[s].sem, xn_made[s].at(i, b + 1))
                        for k in range(KC):
                            out = claim("xT", s, b, k)
                            for j in range(J):
                                ins = pe.transpose(out[:, P * j:P * j + P], xn[s][:, j, P * k:P * k + P], ident[:])
                            ins.then_inc(p_xT[s].sem, 1)

                    elif step == "gram":
                        pe.wait_ge(xn_low[s].sem, xn_low[s].at(i, 1))
                        out = claim("gram", s, b)
                        for k in range(KC):
                            for c in range(C):
                                j = NB * c + b
                                ins = product(out[:, DM * k:DM * k + DM], [t[:, j, P * k:P * k + P] for t in xns[s]],
                                              [t[:, j, :] for t in xns[s]], start=(c == 0), stop=(c == C - 1))
                        ins.then_inc(p_gram[s].sem, 1)

                    elif step == "t1":
                        for n in range(2):
                            for k in range(KC):
                                out = claim("t1", s, b, n, k, inputs=[(gram_low[s], b + 1, 0)])
                                for q in range(KC):
                                    ins = product(out[:], [t[:, q, P * k:P * k + P] for t in gram[b]],
                                                  [w[:, q, 512 * n:512 * n + 512] for w in wv],
                                                  start=(q == 0), stop=(q == KC - 1))
                                ins.then_inc(p_t1[s].sem, 1)

                    elif step == "kv":
                        for n in range(2):
                            out = claim("kv", s, b, n, inputs=[(t1_even[s], 2 * b + n + 1, 0), (t1_odd[s], 2 * b + n + 1, 0)])
                            for q in range(PAIRS // 2):
                                c = slice(P * (4 * n + q), P * (4 * n + q) + P)
                                for k in range(KC):
                                    ins = pe.matmul(out[:, P * q:P * q + P], t1[:, k, c], wk[:, k, c],
                                                    start=(k == 0), stop=(k == KC - 1))
                            ins.then_inc(p_kv[s].sem, 1)

                    elif step == "r":
                        for n in range(4):
                            out = claim("r", s, b, n, inputs=[(kvs_low[s], 2 * b + n // 2 + 1, 0)])
                            for q in range(2):
                                ins = product(out[:, DM * q:DM * q + DM], [t[:, 2 * n + q, :] for t in kvs],
                                              [w[:, 2 * n + q, :] for w in wo])
                            ins.then_inc(p_r[s].sem, 1)

                    elif step == "m":
                        out = claim("m", s, b, inputs=[(r_low[s], 4 * b + 1, 0)])
                        for k in range(KC):
                            for q in range(PAIRS):
                                if k == 0 and q % 2 == 0 and q > 0:
                                    pe.wait_ge(r_low[s].sem, r_low[s].at(i, 4 * b + q // 2 + 1))
                                ins = product(out[:, DM * k:DM * k + DM], [w[:, q, P * k:P * k + P] for w in wq],
                                              [t[:, q, :] for t in r], start=(q == 0), stop=(q == PAIRS - 1))
                        ins.then_inc(p_m[s].sem, 1)

                    elif step == "attn":
                        out = claim("attn", s, b, inputs=[(m_low[s], b + 1, 0), (xT_low[s], KC, 0)])
                        for c in range(C):
                            j = NB * c + b
                            for k in range(KC):
                                ins = product(out[:, DM * c:DM * c + DM], [t[:, k, P * j:P * j + P] for t in xT[s]],
                                              [t[:, k, :] for t in m[b]], start=(k == 0), stop=(k == KC - 1))
                        ins.then_inc(p_attn[s].sem, 1)

                    elif step == "up":
                        f = b
                        for w, name, sig in ((wg, "gate", p_gate), (wu, "up", p_up)):
                            out = claim(name, s, f, inputs=[(xT_low[s], 2 * KC, 0)] if f == 0 else [])
                            for k in range(KC):
                                ins = product(out[:], [t[:, k, P * f:P * f + P] for t in w],
                                              [t[:, k, :] for t in xT[s]], start=(k == 0), stop=(k == KC - 1))
                            ins.then_inc(sig[s].sem, 1)

                    elif step == "down":
                        f = b
                        pe.wait_ge(hid_low[s].sem, hid_low[s].at(i, f + 1))
                        for j in range(J):
                            if f == 0 and j % 2 == 0:
                                claim("down", s, j // 2)
                            out = bank("down", s, j // 2)
                            ins = product(out[:, DM * (j % 2):DM * (j % 2) + DM],
                                          [t[:, f % 2, P * j:P * j + P] for t in hids],
                                          [w[:, f, :] for w in wd], start=(f == 0 and j % 2 == 0),
                                          stop=(f == HC - 1), skip_group_check=True)
                        ins.then_inc(p_down[s].sem, 1)


def layout(t):
    import numpy as np
    g = {k[len("L0_tok_"):]: np.asarray(v) for k, v in t.items() if k.startswith("L0_tok_")}
    ids = np.asarray(t["x"]).reshape(GROUPS, NB, C, P).transpose(0, 3, 2, 1).reshape(GROUPS, P, J)
    position = np.arange(SEQ)[:, None]
    div = np.exp(np.arange(0, D, 2) * (-np.log(10000.0) / D))
    pe = np.zeros((SEQ, D), np.float32)
    pe[:, 0::2] = np.sin(position * div)
    pe[:, 1::2] = np.cos(position * div)
    r = np.arange(P)
    filters = np.concatenate([np.zeros((HEADS, P - 1), np.float32), g["spectral_basis"].T], 1)
    ln = lambda k: np.stack([g[f"ln1_{k}"][0], g[f"ln2_{k}"][0], g[f"ln1_{k}"][1], g[f"ln2_{k}"][1],
                             g[f"lnf_{k}"]], 1)
    out = {
        "token_ids": np.concatenate([ids, np.zeros((STREAMS, P, J), ids.dtype)]),
        "pos": pe, "ident": np.eye(P, dtype=np.float32), "flip": np.eye(P, dtype=np.float32)[::-1],
        "causal": (r[:, None] <= r[None, :]).astype(np.float32),
        "same_head": (r[:, None] // HD == r[None, :] // HD).astype(np.float32),
        "filters": filters, "ln_s": ln("s"), "ln_b": ln("b"),
        "b_q": g["wq_b"].T, "b_f1": g["ff1_b"].reshape(LAYERS, FC, P).transpose(2, 0, 1),
    }
    for k in ("embed", "wq_k", "wk_k", "wv_k", "wo_k", "wk_b", "wv_b", "wo_b", "gate_k", "gate_b", "ff1_k", "ff2_k",
              "ff2_b", "out_k", "out_b"):
        out[k] = g[k]
    at, ff = "L0_attn_", "L0_ffn_"
    out["W_q"] = np.asarray(t[at + "W_q"])
    for k in ("W_k", "W_v", "W_o"):
        out[k + "T"] = np.asarray(t[at + k]).T
    for k in ("w_gate", "w_up", "w_down"):
        out[k + "T"] = np.asarray(t[ff + k]).T
    return {k: np.ascontiguousarray(v) for k, v in out.items()}


def kernel(**inputs):
    import numpy as np
    import concourse.bacc as bacc
    from concourse.bass_utils import run_bass_kernel_spmd

    arrays = {f"in_{k}": v for k, v in layout(inputs).items()}
    nc = bacc.Bacc("TRN2", target_bir_lowering=False, num_devices=1)
    a = {k[3:]: nc.dram_tensor(k, v.shape, mybir.dt.from_np(v.dtype), kind="ExternalInput").ap()
         for k, v in arrays.items()}
    h_rows = nc.dram_tensor("h_rows", (GROUPS, P, J, V), F32).ap()
    out = nc.dram_tensor("out", (BATCH, SEQ, V), F32, kind="ExternalOutput").ap()
    with ExitStack() as ctx:
        semaphores = Semaphores(ctx, nc)
        token_tower(nc, semaphores, a, h_rows)
        semaphores.retire(BODIES)
        attention_and_mlp(nc, semaphores, a, h_rows, out.rearrange("(g b) (c p) n -> g b p c n", b=NB, p=P))
    r = run_bass_kernel_spmd(nc, [arrays], core_ids=[0])
    return r.results[0]["out"]
```

```python
from contextlib import ExitStack

import concourse.bass as bass
from concourse import mybir

F32 = mybir.dt.float32
F32R = mybir.dt.float32r
I32 = mybir.dt.int32
ALU = mybir.AluOpType
ACT = mybir.ActivationFunctionType
AX_X = mybir.AxisListType.X

P = 128
BATCH, SEQ = 32, 256
C = SEQ // P
NB = 2
J = C * NB
TOK = J * P
GROUPS = BATCH // NB
STREAMS = 2
BODIES = GROUPS // STREAMS
D, V, LAYERS, HEADS = 128, 256, 2, 8
HD = D // HEADS
FF = 4 * D
FC = FF // P
EPS_LN, EPS_LN_B, EPS_NORM, EPS = 1e-6, 1e-5, 1e-5, 1e-5
HALF = HEADS // 2
PAIR = 2
BLOCK = PAIR * HD
Q_PARTS, V_PARTS = (0, 1, 0), (0, 0, 1)
FIRST, LAST = -1, BODIES - 1
AFTER = [[1, 4, 5, 6, 6, 7, 7, 9, 9, 12, 14, 15, 19, 19],
         [0, 2, 3, 3, 4, 4, 6, 6, 7, 7, 7, 7, 9, 9, 9, 12, 15, 16, 16],
         [0, 2, 3, 3, 4, 4, 6, 6, 7, 7, 7, 7, 9, 9, 10, 12, 15, 16, 16],
         [1, 4, 5, 6, 6, 7, 7, 9, 9, 12, 14, 15, 19, 19]]
RSQRT_SEED = float(0x5F3759DF)


class Signal:

    def __init__(self, sem, base, per_turn, ahead):
        self.sem, self.base, self.per_turn, self.ahead = sem, base, per_turn, ahead

    def at(self, i, k):
        return i * self.per_turn + (self.base + k)


class Semaphores:

    def __init__(self, ctx, nc):
        self.ctx, self.nc, self.live, self.retired = ctx, nc, [], []

    def one(self, name):
        return self.ctx.enter_context(self.nc.semaphore(name))

    def counted(self, name, per_turn, ahead=0, base=1):
        sem, base = self.retired.pop() if self.retired else (self.one(name), base)
        sig = Signal(sem, base, per_turn, ahead)
        self.live.append(sig)
        return sig

    def raise_new(self, eng):
        for sig in self.live:
            if sig.base == 1:
                eng.sem_inc(sig.sem)

    def retire(self, turns):
        self.retired = [(sig.sem, sig.at(turns, sig.ahead)) for sig in self.live]
        self.live = []


class Banks:

    def __init__(self, ring, products):
        self.bank, self.position = {}, {}
        self.occupants = {b: [] for b in range(8)}
        n = 0
        for name, fixed, signal, k, ahead in products:
            b = fixed
            if b is None:
                b = ring[n % len(ring)]
                n += 1
            self.bank[name] = b
            self.position[name] = len(self.occupants[b])
            self.occupants[b].append((signal, k, ahead))

    def last_reads(self, name, i):
        occupants, n = self.occupants[self.bank[name]], self.position[name]
        before = [(sig, k, ahead) for sig, k, ahead in occupants[n:]]
        earlier = [(sig, k, 0) if ahead else (sig, 0, 0) for sig, k, ahead in before] + occupants[:n]
        if i is FIRST:
            earlier = [(sig, k, shift) for sig, k, shift in occupants[:n] if shift == 1]
        elif i is LAST:
            earlier = [read for read in earlier if read[2] <= 0]
        return earlier[-1:]

    def reads_ahead(self):
        last = [[(sig, k, 0) for sig, k, ahead in occupants if ahead][-1:] for occupants in self.occupants.values()]
        return [read for reads in last for read in reads]


def wait(eng, i, needs):
    last = {}
    for sig, k, shift in needs:
        last[sig] = max((shift, k), last.get(sig, (shift, k)))
    for sig, (shift, k) in last.items():
        value = sig.at(i, shift * sig.per_turn + k)
        if not (isinstance(value, int) and value <= sig.base):
            eng.wait_ge(sig.sem, value)


def turns(eng, order, body):
    body(FIRST, [step for step in order if step[-1]])
    with eng.Fori(0, LAST) as i:
        body(i, order)
    body(LAST, [step for step in order if not step[-1]])


def token_tower(nc, semaphores, a, h_rows):
    with ExitStack() as ctx:
        def sb(name, shape, dt=F32):
            return ctx.enter_context(nc.sbuf_tensor(name, shape, dt))

        def each(name, shape, dt=F32):
            return [sb(f"{name}{s}", shape, dt) for s in range(STREAMS)]

        def signals(name, per_turn, ahead=0, base=1):
            return [semaphores.counted(f"{name}{s}", per_turn, ahead, base) for s in range(STREAMS)]

        def sem(name):
            return semaphores.one(name)

        ident = sb("ident", [P, P])
        causal = sb("causal", [P, P])
        same_head = sb("same_head", [P, P])
        ones = sb("ones", [P, P])
        pos = sb("pos", [P, C, D])
        taps = sb("taps", [P, HEADS, SEQ])
        w_q = [[sb(f"w_q{l}{h}", [P, D], F32R) for h in "hl"] for l in range(LAYERS)]
        w_kv = [[sb(f"w_kv{l}{h}", [P, 2 * D], F32R) for h in "hl"] for l in range(LAYERS)]
        w_f1 = [[sb(f"w_f1{l}{h}", [P, FF], F32R) for h in "hl"] for l in range(LAYERS)]
        w_head = [sb(f"w_head{h}", [P, V], F32R) for h in "hl"]
        w_o = [sb(f"w_o{l}", [P, D]) for l in range(LAYERS)]
        w_f2 = [sb(f"w_f2{l}", [P, FC, D]) for l in range(LAYERS)]
        w_gate = [sb(f"w_gate{l}", [P, D]) for l in range(LAYERS)]
        b_q = sb("b_q", [P, LAYERS])
        b_kv = sb("b_kv", [P, LAYERS, 2 * D])
        b_f1 = sb("b_f1", [P, LAYERS, FC])
        b_head = sb("b_head", [P, V])
        b_o = sb("b_o", [P, LAYERS, D])
        b_f2 = sb("b_f2", [P, LAYERS, D])
        b_gate = sb("b_gate", [P, LAYERS])
        minus_half = sb("minus_half", [P, J])

        idx = each("idx", [P, J], I32)
        emb = each("emb", [P, J, D])
        x = each("x", [P, J, D])
        xn = each("xn", [P, J, D])
        stats = each("stats", [P, J, 6])
        mv = each("mv", [P, J, 2])
        var = each("var", [P, J])
        rstd = each("rstd", [P, J])
        xT = [[sb(f"xT{s}{h}", [P, TOK], F32R) for h in "hl"] for s in range(STREAMS)]
        qT = each("qT", [P, 2, TOK], F32R)
        qT_last = each("qT_last", [P, NB * P])
        kv = each("kv", [P, HEADS, C, NB, 2, HD])
        vc = each("vc", [P, J, D])
        kc = each("kc", [P, J, D])
        vT = each("vT", [P, TOK])
        vTs = [[sb(f"vTs{s}{h}", [P, TOK], F32R) for h in "hl"] for s in range(STREAMS)]
        v_rows = each("v_rows", [P, HEADS // PAIR, TOK], F32R)
        gate = each("gate", [P, J * HEADS])
        state = each("state", [P, NB, D])
        floor = each("floor", [P, J * HEADS])
        oT = each("oT", [P, TOK])
        sq = each("sq", [P, J * HEADS, HD])
        m2 = each("m2", [P, J * HEADS])
        mh = each("mh", [P, J * HEADS])
        y = each("y", [P, J * HEADS])
        yy = each("yy", [P, J * HEADS])
        oTn = each("oTn", [P, TOK])
        gl = each("gl", [P, FC, TOK])
        h_out = each("h_out", [P, J, V])
        q_rows = sb("q_rows", [P, PAIR, HEADS // PAIR, TOK], F32R)
        gk = sb("gk", [P, J, HEADS, D])
        att = sb("att", [P, 2, HEADS, P])
        gk_heads = gk[:].rearrange("p j h (g e) -> p j (h g) e", e=HD)[:, :, ::HEADS + 1, :]

        ps = [ctx.enter_context(nc.psum_tensor(f"ps{n}", [P, 512], F32)) for n in range(8)]

        loaded, prep, ready = sem("loaded"), sem("prep"), sem("ready")
        passed = sem("passed")
        L = LAYERS
        LN = 2 * L + 1
        idx_in = signals("idx_in", 16, ahead=16)
        emb_in = signals("emb_in", 16 * J, ahead=16 * J, base=0)
        Q_DMAS, V_DMAS = 16 * len(Q_PARTS) * HEADS, 16 * len(V_PARTS) * HEADS // PAIR
        q_spread = signals("q_spread", Q_DMAS * L)
        v_spread = signals("v_spread", V_DMAS * L)
        h_stored = signals("h_stored", 16)
        x_step = signals("x_step", 1 + 4 * L)
        ln_step = signals("ln_step", 3 * LN)
        ln_rstd = signals("ln_rstd", LN)
        xn_made = signals("xn_made", LN)
        xT_low = signals("xT_low", LN)
        q_low = signals("q_low", L)
        kv_made = signals("kv_made", 2 * L)
        kc_made = signals("kc_made", 2 * L)
        vT_low = signals("vT_low", 2 * L)
        gate_step = signals("gate_step", 6 * L)
        state_step = signals("state_step", 3 * L)
        att_made = signals("att_made", 2 * J * L)
        NORM = 14
        norm_step = signals("norm_step", NORM * L)
        h_made = signals("h_made", 2)
        xT_high = signals("xT_high", LN)
        q_high = signals("q_high", 2 * L)
        vc_made = signals("vc_made", 2 * L)
        vT_made = signals("vT_made", L)
        oT_made = signals("oT_made", L)
        sq_made = signals("sq_made", L)
        oTn_made = signals("oTn_made", L)
        gl_made = signals("gl_made", FC * L)
        p_xT = signals("p_xT", LN)
        p_q = signals("p_q", L)
        p_kv = signals("p_kv", 2 * L)
        p_conv = signals("p_conv", 2 * L)
        p_vT = signals("p_vT", L)
        p_vg = signals("p_vg", L)
        p_state = signals("p_state", L)
        p_qk = signals("p_qk", 2 * J * L)
        p_av = signals("p_av", J * L)
        p_norm = signals("p_norm", L)
        p_unit = signals("p_unit", L)
        p_wo = signals("p_wo", L)
        p_f1 = signals("p_f1", FC * L)
        p_f2 = signals("p_f2", L)
        p_head = signals("p_head", 2)

        def norm(s, u, ahead):
            return [("stats", s, u, 0, ahead), ("ln", s, u, 0, ahead), ("low", s, u, 0, ahead)]

        def front(s, l, ahead):
            return norm(s, 2 * l, ahead) + [(step, s, l, n, ahead) for step, n in (
                ("q", 0), ("kv", 0), ("q_low", 0), ("kv", 1), ("conv", 0), ("conv", 1), ("turn_v", 0), ("gate", 0),
                ("gated", 0), ("state", 0), ("state_low", 0))]

        def back(s, l, ahead):
            steps = [("qk", 0), ("qk", 1), ("av", 0), ("qk", 2), ("av", 1), ("qk", 3), ("av", 2), ("av", 3),
                     ("norm", 0), ("chain", 0), ("unit", 0), ("wo", 0)]
            return [(step, s, l, j, ahead) for step, j in steps] + norm(s, 2 * l + 1, ahead) + \
                [(step, s, l, f, ahead) for step, f in [("f1", f) for f in range(FC)] + [("f2", 0)]]

        def head(s, ahead):
            return norm(s, 2 * L, ahead) + [("head", s, 0, 0, ahead)]

        def woven(long, short, after):
            out = []
            for n, step in enumerate(long):
                out.append(step)
                out += [short[k] for k in range(len(short)) if after[k] == n]
            return out

        def next_turn(s):
            stats, ln, low, out = head(s, 0)
            first = front(s, 0, 1)
            return [stats, ln, ("embed", s, 0, 0, 1), low, first[0], out] + first[1:]

        order = woven(back(0, 1, 0), front(1, 1, 0), AFTER[0])
        order += woven(back(1, 1, 0), next_turn(0), AFTER[1])
        order += woven(back(0, 0, 1), next_turn(1), AFTER[2])
        order += woven(back(1, 0, 1), front(0, 1, 1), AFTER[3])

        products = []
        for step, s, l, j, ahead in order:
            if step == "ln":
                products.append((("xT", s, l), None, xT_low[s], l + 1, ahead))
            elif step == "q":
                products.append((("q", s, l), None, q_low[s], l + 1, ahead))
            elif step == "kv":
                products.append((("kv", s, l, j), None, kv_made[s], 2 * l + j + 1, ahead))
            elif step == "conv":
                products.append((("conv", s, l, j), None, kc_made[s], 2 * l + j + 1, ahead))
            elif step == "turn_v":
                products.append((("vT", s, l), None, vT_made[s], l + 1, ahead))
            elif step == "gate":
                products.append((("vg", s, l), None, gate_step[s], 6 * l + 1, ahead))
            elif step == "state":
                products.append((("state", s, l), None, state_step[s], 3 * l + 3, ahead))
            elif step == "qk":
                for n in range(2):
                    products.append((("qk", s, l, j, n), None, att_made[s], 2 * (J * l + j) + n + 1, ahead))
            elif step == "av" and j == 0:
                products.append((("av", s, l), 7, oT_made[s], l + 1, ahead))
            elif step == "norm":
                products.append((("norm", s, l), 7, norm_step[s], NORM * (l + 1), ahead))
            elif step == "unit":
                products.append((("unit", s, l), 7, oTn_made[s], l + 1, ahead))
            elif step == "wo":
                products.append((("wo", s, l), 7, x_step[s], 4 * l + 3, ahead))
            elif step == "f1":
                products.append((("f1", s, l, j), None, gl_made[s], FC * l + j + 1, ahead))
            elif step == "f2":
                products.append((("f2", s, l), None, x_step[s], 4 * l + 5, ahead))
            elif step == "head":
                for n in range(2):
                    products.append((("head", s, n), None, h_made[s], n + 1, ahead))
        banks = Banks(range(7), products)

        def bank(*name):
            return ps[banks.bank[name]]

        raw_q = xn[0][:].rearrange("p j d -> p (j d)")[:, 0:L * D].rearrange("p (l d) -> p l d", l=L)
        raw_kv = kv[0][:].rearrange("p h c b v e -> p (h c b v e)")[:, 0:L * 2 * D].rearrange("p (l d) -> p l d", l=L)
        raw_f1 = gl[0][:].rearrange("p f t -> p (f t)")[:, 0:L * FF].rearrange("p (l d) -> p l d", l=L)
        raw_head = sq[0][:].rearrange("p a e -> p (a e)")[:, 0:V]
        ln_s = sb("ln_s", [P, LN])
        ln_b = sb("ln_b", [P, LN])
        ln_b_rows = sb("ln_b_rows", [P, LN, P])

        block = ctx.enter_context(nc.Block())
        loads = [(ident[:], a["ident"]), (causal[:], a["causal"]), (same_head[:], a["same_head"]),
                 (pos[:], a["pos"].rearrange("(c p) d -> p c d", p=P)),
                 (raw_q, a["wq_k"].rearrange("l c n -> c l n")),
                 (raw_kv[:, :, 0:D], a["wk_k"].rearrange("l c n -> c l n")),
                 (raw_kv[:, :, D:2 * D], a["wv_k"].rearrange("l c n -> c l n")),
                 (raw_f1, a["ff1_k"].rearrange("l c n -> c l n")),
                 (raw_head, a["out_k"]),
                 (ln_s[:], a["ln_s"]), (ln_b[:], a["ln_b"]), (b_q[:], a["b_q"]), (b_f1[:], a["b_f1"])]
        for l in range(L):
            loads += [(w_o[l][:], a["wo_k"][l]),
                      (w_f2[l][:], a["ff2_k"][l].rearrange("(f p) n -> p f n", p=P))]
        rows = [(b_kv[:, :, 0:D], a["wk_b"]), (b_kv[:, :, D:2 * D], a["wv_b"]),
                (b_o[:], a["wo_b"]), (b_f2[:], a["ff2_b"])]
        for out, src in rows:
            loads.append((out, src.unsqueeze(0).to_broadcast([P, L, D])))
        loads.append((b_head[:], a["out_b"].unsqueeze(0).to_broadcast([P, V])))
        loads.append((b_gate[:], a["gate_b"].rearrange("l o -> o l").to_broadcast([P, L])))
        flt = a["filters"]
        delayed = att[:].rearrange("p n h t -> p (n h t)")
        flip = oTn[0][:, 0:P]
        loads.append((delayed.rearrange("p (h t) -> p h t", h=HEADS),
                      bass.AP(tensor=flt.tensor, offset=flt.offset,
                              ap=[[1, P], [P - 1 + SEQ, HEADS], [1, SEQ]])))
        loads.append((flip, a["flip"]))
        gate_loads = [(w_gate[l][HD * h:HD * h + HD, HD * h:HD * h + HD],
                       a["gate_k"][l].rearrange("(d e) o -> d (e o)", e=HD))
                      for l in range(L) for h in range(HEADS)]

        @block.sync
        def _(sp):
            semaphores.raise_new(sp)
            for out, src in loads:
                sp.dma_start(out, src).then_inc(loaded, 16)
            for s in range(STREAMS):
                sp.dma_start(idx[s][:], a["token_ids"][s]).then_inc(idx_in[s].sem, 16)
            sp.wait_ge(prep, 1)
            for out, src in gate_loads:
                sp.dma_start(out, src).then_inc(loaded, 16)
            def body(i, steps):
                for step, s, l, j, ahead in steps:
                    t = i + ahead
                    if step == "embed":
                        sp.wait_ge(emb_in[s].sem, emb_in[s].at(t, 16 * J))
                        sp.sem_inc(passed)
                        sp.dma_start(idx[s][:], a["token_ids"][t * STREAMS + (STREAMS + s)])\
                            .then_inc(idx_in[s].sem, 16)
                    elif step == "q_low":
                        sp.wait_ge(q_low[s].sem, q_low[s].at(t, l + 1))
                        sp.sem_inc(passed)
                        o = 1 - s
                        used = J * 2 * (l + 1 if s else l)
                        wait(sp, t, [(p_qk[o], used, 0)])
                        sp.sem_inc(passed)
                        for h in range(HEADS):
                            src = slice(HD * h, HD * h + HD)
                            for n, part in enumerate(Q_PARTS):
                                r = BLOCK * n + HD * (h % PAIR)
                                sp.dma_start(q_rows[r:r + HD, h % PAIR, h // PAIR, :].bitcast(F32),
                                             qT[s][src, part, :].bitcast(F32)).then_inc(q_spread[s].sem, 16)
                    elif step == "turn_v":
                        sp.wait_ge(vT_low[s].sem, vT_low[s].at(t, 2 * l + 2))
                        sp.sem_inc(passed)
                        wait(sp, t, [(p_qk[s], J * 2 * l, 0)])
                        sp.sem_inc(passed)
                        for g in range(HEADS // PAIR):
                            for n, part in enumerate(V_PARTS):
                                sp.dma_start(v_rows[s][BLOCK * n:BLOCK * n + BLOCK, g, :].bitcast(F32),
                                             vTs[s][part][BLOCK * g:BLOCK * g + BLOCK, :].bitcast(F32))\
                                    .then_inc(v_spread[s].sem, 16)
                    elif step == "head":
                        sp.wait_ge(h_made[s].sem, h_made[s].at(t, 2))
                        sp.sem_inc(passed)
                        sp.dma_start(h_rows[t * STREAMS + s], h_out[s][:]).then_inc(h_stored[s].sem, 16)
            turns(sp, order, body)
            for s in range(STREAMS):
                sp.wait_ge(h_stored[s].sem, h_stored[s].at(BODIES, 0))
                sp.wait_ge(idx_in[s].sem, idx_in[s].at(BODIES, 16))

        N_LOADS = 16 * len(loads)
        N_ALL = N_LOADS + 16 * len(gate_loads)

        @block.gpsimd
        def _(pool):
            for l in range(L):
                pool.memset(w_gate[l][:], 0.0)
            pool.memset(ones[:], 1.0)
            pool.memset(minus_half[:], -0.5)
            pool.memset(gk[:], 0.0)
            pool.memset(q_rows[:].bitcast(F32), 0.0).then_inc(prep, 1)

            def gather(s):
                for j in range(J):
                    pool.indirect_dma_start(emb[s][:, j, :], None, a["embed"],
                                            bass.IndirectOffsetOnAxis(ap=idx[s][:, j:j + 1], axis=0))\
                        .then_inc(emb_in[s].sem, 16)

            for s in range(STREAMS):
                pool.wait_ge(idx_in[s].sem, idx_in[s].at(0, 16))
                gather(s)
            pool.wait_ge(ready, 1)
            def body(i, steps):
                for step, s, l, j, ahead in steps:
                    t = i + ahead
                    if step == "stats":
                        pool.wait_ge(ln_step[s].sem, ln_step[s].at(t, 3 * l + 3))
                        pool.tensor_tensor(rstd[s][:], var[s][:], minus_half[:], ALU.pow)\
                            .then_inc(ln_rstd[s].sem, 1)
                    elif step == "ln" and l < 2 * L:
                        pool.wait_ge(xn_made[s].sem, xn_made[s].at(t, l + 1))
                        bias = (b_f2 if l % 2 else b_o)[:, l // 2, :]
                        pool.tensor_tensor(x[s][:], x[s][:], bias.unsqueeze(1).to_broadcast([P, J, D]),
                                           ALU.add).then_inc(x_step[s].sem, 1)
                    elif step == "turn_v":
                        pool.wait_ge(vT_made[s].sem, vT_made[s].at(t, l + 1))
                        pool.sem_inc(passed)
                        wait(pool, t, [(v_spread[s], V_DMAS * l, 0)])
                        pool.sem_inc(passed)
                        pool.tensor_scalar(vTs[s][0][:], vT[s][:], 1.0, 0.0, ALU.mult, ALU.add)\
                            .then_inc(vT_low[s].sem, 1)
                        pool.wait_ge(vT_low[s].sem, vT_low[s].at(t, 2 * l + 1))
                        pool.tensor_tensor(vTs[s][1][:], vT[s][:], vTs[s][0][:].bitcast(F32), ALU.subtract)\
                            .then_inc(vT_low[s].sem, 1)
                    elif step == "f2" and l == 0:
                        pool.wait_ge(idx_in[s].sem, idx_in[s].at(t, 32))
                        pool.wait_ge(x_step[s].sem, x_step[s].at(t, 1))
                        pool.sem_inc(passed)
                        gather(s)
            turns(pool, order, body)
            for s in range(STREAMS):
                pool.wait_ge(emb_in[s].sem, emb_in[s].at(BODIES, 16 * J))

        @block.vector
        def _(dve):
            done = [1]

            def link(ins):
                done[0] += 1
                ins.then_inc(prep, 1)
                dve.wait_ge(prep, done[0])

            def split(pair, src):
                link(dve.tensor_copy(pair[0][:], src))
                link(dve.tensor_tensor(pair[1][:], src, pair[0][:].bitcast(F32), ALU.subtract))

            dve.wait_ge(loaded, N_ALL)
            dve.wait_ge(prep, 1)
            for u in range(LN):
                link(dve.tensor_copy(ln_b_rows[:, u, :], ln_b[:, u:u + 1].to_broadcast([P, P])))
            for l in range(L):
                link(dve.tensor_scalar(raw_kv[:, l, 0:D], raw_kv[:, l, 0:D], HD ** -0.5, None, ALU.mult))
                link(dve.tensor_scalar(b_kv[:, l, 0:D], b_kv[:, l, 0:D], HD ** -0.5, None, ALU.mult))
            dve.wait_ge(ready, 1)
            for n in range(4):
                link(dve.tensor_copy(taps[:].rearrange("p h t -> p (h t)")[:, 512 * n:512 * n + 512], ps[3 + n][:]))
            link(dve.tensor_tensor(b_q[:], b_q[:], ps[0][:, 0:L], ALU.add))
            link(dve.tensor_tensor(b_f1[:], b_f1[:], ps[0][:, L:L + L * FC].rearrange("p (l f) -> p l f", l=L),
                                   ALU.add))
            link(dve.tensor_tensor(b_kv[:], b_kv[:], ps[1][:].rearrange("p (l d) -> p l d", l=L), ALU.add))
            link(dve.tensor_tensor(b_head[:], b_head[:], ps[2][:, 0:V], ALU.add))
            for l in range(L):
                for raw, pair, u in ((raw_q, w_q[l], 2 * l), (raw_kv, w_kv[l], 2 * l), (raw_f1, w_f1[l], 2 * l + 1)):
                    link(dve.tensor_scalar(raw[:, l, :], raw[:, l, :], ln_s[:, u:u + 1], None, ALU.mult))
                    split(pair, raw[:, l, :])
            link(dve.tensor_scalar(raw_head, raw_head, ln_s[:, 2 * L:2 * L + 1], None, ALU.mult))
            split(w_head, raw_head)
            dve.tensor_copy(b_gate[:], b_gate[:]).then_inc(ready, 1)
            dve.wait_ge(ready, 2)

            def body(i, steps):
                for step, s, l, j, ahead in steps:
                    t = i + ahead
                    if step == "embed":
                        dve.wait_ge(emb_in[s].sem, emb_in[s].at(t, 16 * J))
                        dve.wait_ge(xn_made[s].sem, xn_made[s].at(t, 0))
                        for c in range(C):
                            ins = dve.tensor_tensor(x[s][:, NB * c:NB * c + NB, :], emb[s][:, NB * c:NB * c + NB, :],
                                                    pos[:, c, :].unsqueeze(1).to_broadcast([P, NB, D]), ALU.add)
                        ins.then_inc(x_step[s].sem, 1)

                    elif step == "stats":
                        dve.wait_ge(x_step[s].sem, x_step[s].at(t, 2 * l + 1))
                        for j in range(J):
                            ins = dve.bn_stats(stats[s][:, j, :], x[s][:, j, :])
                        ins.then_inc(ln_step[s].sem, 1)
                        dve.wait_ge(ln_step[s].sem, ln_step[s].at(t, 3 * l + 1))
                        dve.sem_inc(passed)
                        for j in range(J):
                            ins = dve.bn_aggr(mv[s][:, j, :], stats[s][:, j, :])
                        ins.then_inc(ln_step[s].sem, 1)
                        dve.wait_ge(ln_step[s].sem, ln_step[s].at(t, 3 * l + 2))
                        dve.tensor_scalar(var[s][:], mv[s][:, :, 1], EPS_LN, None, ALU.add)\
                            .then_inc(ln_step[s].sem, 1)

                    elif step == "ln":
                        dve.wait_ge(ln_rstd[s].sem, ln_rstd[s].at(t, l + 1))
                        for j in range(J):
                            ins = dve.tensor_scalar(xn[s][:, j, :], x[s][:, j, :], mv[s][:, j, 0:1],
                                                    rstd[s][:, j:j + 1], ALU.subtract, ALU.mult)
                        ins.then_inc(xn_made[s].sem, 1)

                    elif step == "low":
                        dve.wait_ge(p_xT[s].sem, p_xT[s].at(t, l + 1))
                        dve.wait_ge(xT_high[s].sem, xT_high[s].at(t, l + 1))
                        dve.tensor_tensor(xT[s][1][:], bank("xT", s, l)[:], xT[s][0][:].bitcast(F32), ALU.subtract)\
                            .then_inc(xT_low[s].sem, 1)

                    elif step == "q_low":
                        dve.wait_ge(q_high[s].sem, q_high[s].at(t, 2 * l + 2))
                        dve.scalar_tensor_tensor(out=qT[s][:, 1, :], in0=bank("q", s, l)[:], scalar=b_q[:, l:l + 1],
                                                 in1=qT[s][:, 0, :].bitcast(F32), op0=ALU.add, op1=ALU.subtract)\
                            .then_inc(q_low[s].sem, 1)

                    elif step == "kv":
                        dve.wait_ge(p_kv[s].sem, p_kv[s].at(t, 2 * l + j + 1))
                        for b in range(NB):
                            ins = dve.tensor_tensor(
                                kv[s][:, :, j, b, :, :],
                                bank("kv", s, l, j)[:, 2 * D * b:2 * D * b + 2 * D].rearrange(
                                    "p (v h e) -> p h v e", v=2, h=HEADS),
                                b_kv[:, l, :].rearrange("p (v h e) -> p h v e", v=2, h=HEADS), ALU.add)
                        ins.then_inc(kv_made[s].sem, 1)

                    elif step == "conv":
                        dve.wait_ge(vc_made[s].sem, vc_made[s].at(t, 2 * l + j + 1))
                        src = bank("conv", s, l, j)[:].rearrange("p (h j v e) -> p h j v e", h=HALF, j=J, v=2)
                        dve.tensor_copy(kc[s][:].rearrange("p j (h e) -> p h j e", h=HEADS)[:, HALF * j:HALF * j + HALF],
                                        src[:, :, :, 0, :]).then_inc(kc_made[s].sem, 1)

                    elif step == "gate":
                        k = 6 * l
                        g = gate_step[s]
                        dve.wait_ge(p_vg[s].sem, p_vg[s].at(t, l + 1))
                        dve.wait_ge(kc_made[s].sem, kc_made[s].at(t, 2 * l + 2))
                        dve.tensor_tensor(sq[s][:].rearrange("p a e -> p (a e)"), bank("vg", s, l)[:],
                                          kc[s][:].rearrange("p j d -> p (j d)"), ALU.mult).then_inc(g.sem, 1)

                    elif step == "gated":
                        k = 6 * l
                        g = gate_step[s]
                        dve.wait_ge(g.sem, g.at(t, k + 1))
                        dve.tensor_reduce(gate[s][:], sq[s][:], AX_X, ALU.add).then_inc(g.sem, 1)
                        dve.wait_ge(g.sem, g.at(t, k + 2))
                        dve.tensor_scalar(gate[s][:], gate[s][:], b_gate[:, l:l + 1], 0.0, ALU.add, ALU.max)\
                            .then_inc(g.sem, 1)
                        dve.wait_ge(g.sem, g.at(t, k + 3))
                        dve.tensor_tensor(gate[s][:], gate[s][:], gate[s][:], ALU.mult).then_inc(g.sem, 1)
                        dve.wait_ge(g.sem, g.at(t, k + 4))
                        dve.tensor_scalar(gate[s][:], gate[s][:], EPS, None, ALU.add).then_inc(g.sem, 1)
                        dve.wait_ge(g.sem, g.at(t, k + 5))
                        o = 1 - s
                        wait(dve, t, [(p_av[o], J * (l + 1 if s else l), 0)])
                        for j in range(J):
                            ins = dve.tensor_tensor(
                                gk_heads[:, j], kc[s][:, j, :].rearrange("p (h e) -> p h e", h=HEADS),
                                gate[s][:, HEADS * j:HEADS * j + HEADS].unsqueeze(2).to_broadcast([P, HEADS, HD]),
                                ALU.mult)
                        ins.then_inc(g.sem, 1)

                    elif step == "state_low":
                        g = state_step[s]
                        dve.wait_ge(p_state[s].sem, p_state[s].at(t, l + 1))
                        dve.tensor_scalar(floor[s][:], bank("state", s, l)[:, NB * D:NB * D + J * HEADS], EPS,
                                          EPS_NORM, ALU.add, ALU.mult).then_inc(g.sem, 1)
                        dve.wait_ge(g.sem, g.at(t, 3 * l + 1))
                        dve.tensor_tensor(floor[s][:], floor[s][:], floor[s][:], ALU.mult).then_inc(g.sem, 1)
                        dve.tensor_tensor(state[s][:], bank("state", s, l)[:, 0:NB * D].rearrange(
                            "p (b d) -> p b d", b=NB), same_head[:].unsqueeze(1).to_broadcast([P, NB, D]),
                            ALU.mult).then_inc(g.sem, 1)

                    elif step == "qk":
                        if j < 2:
                            o = 1 - s
                            wait(dve, t, [(p_av[o], J * (l + 1 if s else l), 0)])
                        else:
                            dve.wait_ge(p_av[s].sem, p_av[s].at(t, J * l + j - 1))
                        for n in range(2):
                            k = 2 * (J * l + j) + n + 1
                            dve.wait_ge(p_qk[s].sem, p_qk[s].at(t, k))
                            dve.tensor_tensor(att[:, j % 2, HALF * n:HALF * n + HALF, :],
                                              bank("qk", s, l, j, n)[:].rearrange("p (h t) -> p h t", h=HALF),
                                              causal[:].unsqueeze(1).to_broadcast([P, HALF, P]), ALU.mult)\
                                .then_inc(att_made[s].sem, 1)

                    elif step == "chain":
                        g, k = norm_step[s], NORM * l
                        dve.wait_ge(sq_made[s].sem, sq_made[s].at(t, l + 1))
                        dve.tensor_reduce(m2[s][:], sq[s][:], AX_X, ALU.add).then_inc(g.sem, 1)
                        dve.wait_ge(g.sem, g.at(t, k + 1))
                        dve.tensor_tensor(m2[s][:], m2[s][:], floor[s][:], ALU.max).then_inc(g.sem, 1)
                        dve.wait_ge(g.sem, g.at(t, k + 2))
                        dve.tensor_scalar(mh[s][:], m2[s][:], -0.5, None, ALU.mult).then_inc(g.sem, 1)
                        dve.tensor_scalar(y[s][:].bitcast(I32), m2[s][:].bitcast(I32), -0.5, RSQRT_SEED,
                                          ALU.mult, ALU.add).then_inc(g.sem, 1)
                        for n in range(3):
                            dve.wait_ge(g.sem, g.at(t, k + 4 + 3 * n))
                            dve.tensor_tensor(yy[s][:], y[s][:], y[s][:], ALU.mult).then_inc(g.sem, 1)
                            dve.wait_ge(g.sem, g.at(t, k + 5 + 3 * n))
                            dve.tensor_tensor(yy[s][:], yy[s][:], mh[s][:], ALU.mult).then_inc(g.sem, 1)
                            dve.wait_ge(g.sem, g.at(t, k + 6 + 3 * n))
                            dve.scalar_tensor_tensor(out=y[s][:], in0=yy[s][:], scalar=1.5, in1=y[s][:],
                                                     op0=ALU.add, op1=ALU.mult).then_inc(g.sem, 1)
                        dve.wait_ge(g.sem, g.at(t, k + 13))
                        dve.tensor_tensor(sq[s][:], bank("norm", s, l)[:].rearrange("p (a e) -> p a e", e=HD),
                                          y[s][:].unsqueeze(2).to_broadcast([P, J * HEADS, HD]), ALU.mult)\
                            .then_inc(g.sem, 1)

                    elif step == "wo":
                        dve.wait_ge(p_wo[s].sem, p_wo[s].at(t, l + 1))
                        dve.wait_ge(x_step[s].sem, x_step[s].at(t, 4 * l + 2))
                        dve.tensor_tensor(x[s][:], x[s][:], bank("wo", s, l)[:].rearrange("p (j d) -> p j d", j=J),
                                          ALU.add).then_inc(x_step[s].sem, 1)

                    elif step == "f2":
                        dve.wait_ge(p_f2[s].sem, p_f2[s].at(t, l + 1))
                        dve.wait_ge(x_step[s].sem, x_step[s].at(t, 4 * l + 4))
                        dve.tensor_tensor(x[s][:], x[s][:], bank("f2", s, l)[:].rearrange("p (j d) -> p j d", j=J),
                                          ALU.add).then_inc(x_step[s].sem, 1)

                    elif step == "head":
                        wait(dve, t, [(h_stored[s], 0, 0)])
                        for n in range(2):
                            dve.wait_ge(p_head[s].sem, p_head[s].at(t, n + 1))
                            dve.tensor_tensor(h_out[s][:, 2 * n:2 * n + 2, :],
                                              bank("head", s, n)[:].rearrange("p (j v) -> p j v", j=2),
                                              b_head[:].unsqueeze(1).to_broadcast([P, 2, V]), ALU.add)\
                                .then_inc(h_made[s].sem, 1)

            turns(dve, order, body)

        @block.scalar
        def _(act):
            act.wait_ge(ready, 2)
            def body(i, steps):
                for step, s, l, j, ahead in steps:
                    t = i + ahead
                    if step == "ln":
                        act.wait_ge(p_xT[s].sem, p_xT[s].at(t, l + 1))
                        act.activation(xT[s][0][:], bank("xT", s, l)[:], ACT.Copy).then_inc(xT_high[s].sem, 1)

                    elif step == "q":
                        act.wait_ge(p_q[s].sem, p_q[s].at(t, l + 1))
                        wait(act, t, [(q_spread[s], Q_DMAS * l, 0)])
                        act.activation(qT[s][:, 0, :], bank("q", s, l)[:], ACT.Identity, bias=b_q[:, l:l + 1])\
                            .then_inc(q_high[s].sem, 1)
                        act.activation(qT_last[s][:], bank("q", s, l)[:, NB * P:J * P], ACT.Identity,
                                       bias=b_q[:, l:l + 1]).then_inc(q_high[s].sem, 1)

                    elif step == "conv":
                        act.wait_ge(p_conv[s].sem, p_conv[s].at(t, 2 * l + j + 1))
                        src = bank("conv", s, l, j)[:].rearrange("p (h j v e) -> p h j v e", h=HALF, j=J, v=2)
                        act.activation(vc[s][:].rearrange("p j (h e) -> p h j e", h=HEADS)[:, HALF * j:HALF * j + HALF],
                                       src[:, :, :, 1, :], ACT.Copy).then_inc(vc_made[s].sem, 1)

                    elif step == "turn_v":
                        act.wait_ge(p_vT[s].sem, p_vT[s].at(t, l + 1))
                        act.activation(vT[s][:], bank("vT", s, l)[:], ACT.Copy).then_inc(vT_made[s].sem, 1)

                    elif step == "norm":
                        act.wait_ge(p_av[s].sem, p_av[s].at(t, J * (l + 1)))
                        act.activation(oT[s][:], bank("av", s, l)[:], ACT.Copy).then_inc(oT_made[s].sem, 1)
                        act.wait_ge(p_norm[s].sem, p_norm[s].at(t, l + 1))
                        act.activation(sq[s][:].rearrange("p a e -> p (a e)"), bank("norm", s, l)[:], ACT.Square)\
                            .then_inc(sq_made[s].sem, 1)

                    elif step == "unit":
                        act.wait_ge(p_unit[s].sem, p_unit[s].at(t, l + 1))
                        act.activation(oTn[s][:], bank("unit", s, l)[:], ACT.Copy).then_inc(oTn_made[s].sem, 1)

                    elif step == "f1":
                        act.wait_ge(p_f1[s].sem, p_f1[s].at(t, FC * l + j + 1))
                        act.activation(gl[s][:, j, :], bank("f1", s, l, j)[:], ACT.Gelu_apprx_tanh,
                                       bias=b_f1[:, l, j:j + 1]).then_inc(gl_made[s].sem, 1)

            turns(act, order, body)

        @block.tensor
        def _(pe):
            pe.wait_ge(loaded, N_ALL)
            pe.wait_ge(prep, 1 + LN + 2 * L)
            for l in range(L):
                pe.matmul(ps[0][:, l:l + 1], raw_q[:, l, :], ln_b[:, 2 * l:2 * l + 1], start=(l == 0), stop=True,
                          skip_group_check=True)
            for l in range(L):
                for f in range(FC):
                    n = L + FC * l + f
                    pe.matmul(ps[0][:, n:n + 1], raw_f1[:, l, P * f:P * f + P], ln_b[:, 2 * l + 1:2 * l + 2],
                              start=False, stop=True, skip_group_check=True)
            for l in range(L):
                pe.matmul(ps[1][:, 2 * D * l:2 * D * l + 2 * D], ln_b_rows[:, 2 * l, :], raw_kv[:, l, :],
                          start=(l == 0), stop=True, skip_group_check=True)
            pe.matmul(ps[2][:, 0:V], ln_b_rows[:, 2 * L, :], raw_head, start=True, stop=True)
            for n in range(4):
                ins = pe.matmul(ps[3 + n][:], flip, delayed[:, 512 * n:512 * n + 512], start=True, stop=True)
            ins.then_inc(ready, 1)
            pe.wait_ge(ready, 2)

            def product(out, lhsT, rhs, start=True, stop=True, **kw):
                pe.matmul(out, lhsT[0], rhs[0], start=start, stop=False, **kw)
                pe.matmul(out, lhsT[0], rhs[1], start=False, stop=False, **kw)
                return pe.matmul(out, lhsT[1], rhs[0], start=False, stop=stop, **kw)

            def body(i, steps):
                def claim(*name):
                    wait(pe, i, banks.last_reads(name, i))
                    return bank(*name)

                for step, s, l, j, ahead in steps:
                    t = i + ahead
                    if step == "ln":
                        pe.wait_ge(xn_made[s].sem, xn_made[s].at(t, l + 1))
                        out = claim("xT", s, l)
                        for j in range(J):
                            ins = pe.transpose(out[:, P * j:P * j + P], xn[s][:, j, :], ident[:])
                        ins.then_inc(p_xT[s].sem, 1)

                    elif step == "q":
                        pe.wait_ge(xT_low[s].sem, xT_low[s].at(t, 2 * l + 1))
                        out = claim("q", s, l)
                        product(out[:], [w[:] for w in w_q[l]], [t[:] for t in xT[s]]).then_inc(p_q[s].sem, 1)

                    elif step == "kv":
                        out = claim("kv", s, l, j)
                        for b in range(NB):
                            c = slice(P * (NB * j + b), P * (NB * j + b) + P)
                            ins = product(out[:, 2 * D * b:2 * D * b + 2 * D], [t[:, c] for t in xT[s]],
                                          [w[:] for w in w_kv[l]])
                        ins.then_inc(p_kv[s].sem, 1)

                    elif step == "conv":
                        pe.wait_ge(kv_made[s].sem, kv_made[s].at(t, 2 * l + 2))
                        out = claim("conv", s, l, j)[:].rearrange("p (h w) -> p h w", h=HALF)
                        w = 2 * HD * NB
                        for h in range(HALF):
                            hh = HALF * j + h
                            src = kv[s][:, hh].rearrange("p c b v e -> p (c b v e)")
                            pe.matmul(out[:, h, :], taps[:, hh, 0:P], src, start=(h == 0), stop=True,
                                      skip_group_check=True)
                            ins = pe.matmul(out[:, h, w:2 * w], taps[:, hh, P:2 * P], src[:, 0:w], start=False,
                                            stop=True, skip_group_check=True)
                        ins.then_inc(p_conv[s].sem, 1)

                    elif step == "turn_v":
                        pe.wait_ge(vc_made[s].sem, vc_made[s].at(t, 2 * l + 2))
                        out = claim("vT", s, l)
                        for j in range(J):
                            ins = pe.transpose(out[:, P * j:P * j + P], vc[s][:, j, :], ident[:])
                        ins.then_inc(p_vT[s].sem, 1)

                    elif step == "gate":
                        pe.wait_ge(vT_made[s].sem, vT_made[s].at(t, l + 1))
                        out = claim("vg", s, l)
                        for j in range(J):
                            ins = pe.matmul(out[:, P * j:P * j + P], vT[s][:, P * j:P * j + P], w_gate[l][:],
                                            start=True, stop=True)
                        ins.then_inc(p_vg[s].sem, 1)

                    elif step == "state":
                        out = claim("state", s, l)
                        pe.wait_ge(gate_step[s].sem, gate_step[s].at(t, 6 * l + 6))
                        for b in range(NB):
                            pe.matmul(out[:, D * b:D * b + D], vc[s][:, b, :], gk_heads[:, b], start=(b == 0),
                                      stop=True, skip_group_check=True)
                        z, w = NB * D, NB * HEADS
                        pe.matmul(out[:, z:z + 2 * w], causal[:], gate[s][:], start=False, stop=False,
                                  skip_group_check=True)
                        pe.matmul(out[:, z + w:z + 2 * w], ones[:], gate[s][:, 0:w], start=False, stop=True,
                                  skip_group_check=True).then_inc(p_state[s].sem, 1)

                    elif step == "qk":
                        if j == 0:
                            pe.wait_ge(q_spread[s].sem, q_spread[s].at(t, Q_DMAS * (l + 1)))
                            pe.wait_ge(v_spread[s].sem, v_spread[s].at(t, V_DMAS * (l + 1)))
                        c = slice(P * j, P * j + P)
                        for n in range(2):
                            out = claim("qk", s, l, j, n)
                            out = out[:].rearrange("p (h t) -> p h t", h=HALF)
                            rows = slice(0, BLOCK * len(V_PARTS))
                            for g in range(HALF // PAIR):
                                pair = HALF // PAIR * n + g
                                ins = pe.matmul(out[:, PAIR * g:PAIR * g + PAIR, :], v_rows[s][rows, pair, c],
                                                q_rows[rows, :, pair, c], start=True, stop=True)
                            ins.then_inc(p_qk[s].sem, 1)

                    elif step == "av":
                        if j == 0:
                            claim("av", s, l)
                        if j == NB:
                            pe.wait_ge(state_step[s].sem, state_step[s].at(t, 3 * l + 3))
                            pe.wait_ge(q_high[s].sem, q_high[s].at(t, 2 * l + 2))
                        out = bank("av", s, l)[:, P * j:P * j + P]
                        if j >= NB:
                            b = j - NB
                            pe.matmul(out, state[s][:, b, :], qT_last[s][:, P * b:P * b + P], start=True, stop=False)
                        for h in range(HEADS):
                            if h % HALF == 0:
                                k = 2 * (J * l + j) + h // HALF + 1
                                pe.wait_ge(att_made[s].sem, att_made[s].at(t, k))
                            ins = pe.matmul(out, gk[:, j, h, :], att[:, j % 2, h, :], start=(h == 0 and j < NB),
                                            stop=(h == HEADS - 1))
                        ins.then_inc(p_av[s].sem, 1)

                    elif step == "norm":
                        pe.wait_ge(oT_made[s].sem, oT_made[s].at(t, l + 1))
                        out = claim("norm", s, l)
                        for j in range(J):
                            ins = pe.transpose(out[:, P * j:P * j + P], oT[s][:, P * j:P * j + P], ident[:])
                        ins.then_inc(p_norm[s].sem, 1)

                    elif step == "unit":
                        pe.wait_ge(norm_step[s].sem, norm_step[s].at(t, NORM * (l + 1)))
                        out = claim("unit", s, l)
                        for j in range(J):
                            o = sq[s][:, HEADS * j:HEADS * j + HEADS, :].rearrange("p h e -> p (h e)")
                            ins = pe.transpose(out[:, P * j:P * j + P], o, ident[:])
                        ins.then_inc(p_unit[s].sem, 1)

                    elif step == "wo":
                        pe.wait_ge(oTn_made[s].sem, oTn_made[s].at(t, l + 1))
                        out = claim("wo", s, l)
                        for j in range(J):
                            ins = pe.matmul(out[:, D * j:D * j + D], oTn[s][:, P * j:P * j + P], w_o[l][:],
                                            start=True, stop=True)
                        ins.then_inc(p_wo[s].sem, 1)

                    elif step == "f1":
                        if j == 0:
                            pe.wait_ge(xT_low[s].sem, xT_low[s].at(t, 2 * l + 2))
                        out = claim("f1", s, l, j)
                        product(out[:], [w[:, P * j:P * j + P] for w in w_f1[l]], [t[:] for t in xT[s]])\
                            .then_inc(p_f1[s].sem, 1)

                    elif step == "f2":
                        out = claim("f2", s, l)
                        for f in range(FC):
                            pe.wait_ge(gl_made[s].sem, gl_made[s].at(t, FC * l + f + 1))
                            for j in range(J):
                                ins = pe.matmul(out[:, D * j:D * j + D], gl[s][:, f, P * j:P * j + P],
                                                w_f2[l][:, f, :], start=(f == 0 and j == 0), stop=(f == FC - 1),
                                                skip_group_check=True)
                        ins.then_inc(p_f2[s].sem, 1)

                    elif step == "head":
                        pe.wait_ge(xT_low[s].sem, xT_low[s].at(t, LN))
                        for n in range(2):
                            out = claim("head", s, n)
                            for b in range(2):
                                c = slice(P * (2 * n + b), P * (2 * n + b) + P)
                                ins = product(out[:, V * b:V * b + V], [t[:, c] for t in xT[s]],
                                              [w[:] for w in w_head])
                            ins.then_inc(p_head[s].sem, 1)

                if i is FIRST:
                    wait(pe, 0, banks.reads_ahead())

            turns(pe, order, body)


DM = V
KC = DM // P
AH, DK = 16, 64
PAIRS = AH * DK // P
HID = 768
HC = HID // P
DEQUANT = 1.0 / 127.0
STAGE = 1024
MLP_AFTER = [2, 3, 3, 4, 4, 4, 5, 5, 5, 5, 6, 7, 8, 8, 8, 9, 10]


def attention_and_mlp(nc, semaphores, a, h_rows, out_rows):
    with ExitStack() as ctx:
        def sb(name, shape, dt=F32):
            return ctx.enter_context(nc.sbuf_tensor(name, shape, dt))

        def pair(name, shape):
            return [sb(name + h, shape, F32R) for h in ("_high", "_low")]

        def each(name, shape, dt=F32):
            return [sb(f"{name}{s}", shape, dt) for s in range(STREAMS)]

        def signals(name, per_turn):
            return [semaphores.counted(f"b_{name}{s}", per_turn) for s in range(STREAMS)]

        def sem(name):
            return semaphores.one(name)

        ident = sb("ident_b", [P, P])
        minus_half = sb("minus_half_b", [P, J])
        wv = pair("wv", [P, KC, AH * DK])
        wk = sb("wk", [P, KC, AH * DK])
        wo = pair("wo", [P, PAIRS, DM])
        wq = pair("wq", [P, PAIRS, DM])
        wg = pair("wg", [P, KC, HID])
        wu = pair("wu", [P, KC, HID])
        wd = pair("wd", [P, HC, DM])

        h = each("h", [P, J, DM])
        xn = each("bxn", [P, J, DM])
        xns = [pair(f"xns{s}", [P, J, DM]) for s in range(STREAMS)]
        xT = [pair(f"bxT{s}", [P, KC, TOK]) for s in range(STREAMS)]
        stats = each("bstats", [P, J, 6])
        mv = each("bmv", [P, J, 2])
        var = each("bvar", [P, J])
        rstd = each("brstd", [P, J])
        gram = [pair(f"gram{b}", [P, KC, DM]) for b in range(NB)]
        t1 = sb("t1", [P, KC, AH * DK])
        kvs = pair("kvs", [P, PAIRS, P])
        r = pair("r", [P, PAIRS, DM])
        m = [pair(f"m{b}", [P, KC, DM]) for b in range(NB)]
        silu = sb("silu", [P, 2, TOK])
        hid = sb("hid", [P, 2, TOK])
        hids = pair("hids", [P, 2, TOK])

        ps = [ctx.enter_context(nc.psum_tensor(f"bps{n}", [P, 512], F32)) for n in range(8)]

        direct, cleared = sem("b_direct"), sem("b_cleared")
        passed = sem("b_passed")
        scaled, split_high, split_low = sem("b_scaled"), sem("b_split_high"), sem("b_split_low")
        h_in = signals("h_in", 16)
        out_sent = signals("out_sent", 16 * NB)
        h_step = signals("h_step", NB + 2)
        ln_step = signals("ln_step", 6)
        ln_rstd = signals("ln_rstd", 2)
        xn_made = signals("xn_made", 2)
        xn_high = signals("xn_high", 1)
        xn_low = signals("xn_low", 1)
        xT_high = signals("xT_high", 2 * KC)
        xT_low = signals("xT_low", 2 * KC)
        gram_high, gram_low = signals("gram_high", NB), signals("gram_low", NB)
        t1_even, t1_odd = signals("t1_even", 2 * NB), signals("t1_odd", 2 * NB)
        kvs_high, kvs_low = signals("kvs_high", 2 * NB), signals("kvs_low", 2 * NB)
        r_high, r_low = signals("r_high", 4 * NB), signals("r_low", 4 * NB)
        m_high, m_low = signals("m_high", NB), signals("m_low", NB)
        silu_made = signals("silu_made", HC)
        hid_made, hid_high, hid_low = signals("hid_made", HC), signals("hid_high", HC), signals("hid_low", HC)
        p_xT = signals("p_xT", 2 * KC)
        p_gram = signals("p_gram", NB)
        p_t1 = signals("p_t1", 4 * NB)
        p_kv = signals("p_kv", 2 * NB)
        p_r = signals("p_r", 4 * NB)
        p_m = signals("p_m", NB)
        p_attn = signals("p_attn", NB)
        p_gate, p_up, p_down = signals("p_gate", HC), signals("p_up", HC), signals("p_down", HC)

        def half(s, o, ahead):
            attention = [("gram", s, 0, ahead), ("gram", s, 1, ahead)]
            for b in range(NB):
                attention += [(step, s, b, ahead) for step in ("t1", "kv", "r", "m", "attn")]
            mlp = [("ln", o, 1, 0), ("up", o, 0, 0)]
            for f in range(1, HC):
                mlp += [("up", o, f, 0), ("down", o, f - 1, 0)]
            mlp += [("down", o, HC - 1, 0), ("add", o, 0, 0), ("load", o, 0, 1), ("stats", o, 0, 1), ("ln", o, 0, 1)]
            out = []
            for n, step in enumerate(attention):
                out.append(step)
                out += [mlp[k] for k in range(len(mlp)) if MLP_AFTER[k] == n]
            return out + [("stats", s, 1, ahead)]

        order = half(1, 0, 0) + half(0, 1, 1)
        products = []
        for step, s, b, ahead in order:
            if step == "ln":
                for k in range(KC):
                    products.append((("xT", s, b, k), None, xT_low[s], KC * b + k + 1, ahead))
            elif step == "gram":
                products.append((("gram", s, b), None, gram_low[s], b + 1, ahead))
            elif step == "t1":
                for n in range(2):
                    products.append((("t1", s, b, n, 0), None, t1_even[s], 2 * b + n + 1, ahead))
                    products.append((("t1", s, b, n, 1), None, t1_odd[s], 2 * b + n + 1, ahead))
            elif step == "kv":
                for n in range(2):
                    products.append((("kv", s, b, n), None, kvs_low[s], 2 * b + n + 1, ahead))
            elif step == "r":
                for n in range(4):
                    products.append((("r", s, b, n), None, r_low[s], 4 * b + n + 1, ahead))
            elif step == "m":
                products.append((("m", s, b), None, m_low[s], b + 1, ahead))
            elif step == "attn":
                products.append((("attn", s, b), None, h_step[s], b + 1, ahead))
            elif step == "up":
                products.append((("gate", s, b), None, silu_made[s], b + 1, ahead))
                products.append((("up", s, b), None, hid_made[s], b + 1, ahead))
            elif step == "down" and b == 0:
                for n in range(2):
                    products.append((("down", s, n), 6 + n, h_step[s], NB + n + 1, ahead))
        banks = Banks(range(6), products)

        def bank(*name):
            return ps[banks.bank[name]]

        stages = [t[:].rearrange("p j d -> p (j d)") for t in (h[0], h[1], xn[0], xn[1])]
        stages += [t1[:, k, :] for k in range(KC)]
        landed = [sem(f"b_landed{n}") for n in range(len(stages))]
        pieces = []
        for w, src, is_int in ((wv, "W_vT", False), (wg, "w_gateT", True), (wu, "w_upT", True),
                               (wo, "W_oT", False), (wq, "W_q", False), (wd, "w_downT", True)):
            K, N = w[0].shape[1], w[0].shape[2]
            per = STAGE // N
            view = a[src].rearrange("(k p) n -> p k n", p=P)
            for k in range(0, K, per):
                pieces.append((w, k, min(per, K - k), N, view, is_int))

        def stage(n, dt=F32):
            _, _, cnt, N, _, _ = pieces[n]
            t = stages[n % len(stages)][:, 0:cnt * N]
            if dt != F32:
                t = t.bitcast(dt)
            return t.rearrange("p (k n) -> p k n", n=N)

        block = ctx.enter_context(nc.Block())

        @block.sync
        def _(sp):
            sp.dma_start(ident[:], a["ident"]).then_inc(direct, 16)
            for n, (w, k, cnt, N, view, is_int) in enumerate(pieces):
                if n >= len(stages):
                    sp.wait_ge(split_low, n - len(stages) + 1)
                sp.dma_start(stage(n, I32 if is_int else F32), view[:, k:k + cnt, :]).then_inc(landed[n % len(stages)], 16)
            sp.dma_start(wk[:], a["W_kT"].rearrange("(k p) n -> p k n", p=P)).then_inc(direct, 16)
            sp.wait_ge(split_low, len(pieces))
            def body(i, steps):
                for step, s, b, ahead in steps:
                    t = i + ahead
                    if step == "load":
                        sp.wait_ge(h_step[s].sem, h_step[s].at(t, 0))
                        sp.sem_inc(passed)
                        sp.dma_start(h[s][:], h_rows[t * STREAMS + s]).then_inc(h_in[s].sem, 16)
                    elif step == "add":
                        sp.wait_ge(h_step[s].sem, h_step[s].at(t, NB + 2))
                        sp.sem_inc(passed)
                        for b in range(NB):
                            sp.dma_start(out_rows[t * STREAMS + s, b], xn[s][:, b::NB, :])\
                                .then_inc(out_sent[s].sem, 16)
            turns(sp, order, body)
            for s in range(STREAMS):
                sp.wait_ge(out_sent[s].sem, out_sent[s].at(BODIES, 0))

        @block.gpsimd
        def _(pool):
            pool.memset(minus_half[:], -0.5)
            pool.memset(kvs[0][:].bitcast(F32), 0.0)
            pool.memset(kvs[1][:].bitcast(F32), 0.0).then_inc(cleared, 1)
            def body(i, steps):
                for step, s, b, ahead in steps:
                    t = i + ahead
                    if step == "stats":
                        pool.wait_ge(ln_step[s].sem, ln_step[s].at(t, 3 * b + 3))
                        pool.tensor_tensor(rstd[s][:], var[s][:], minus_half[:], ALU.pow)\
                            .then_inc(ln_rstd[s].sem, 1)
                    elif step == "ln" and b == 0:
                        pool.wait_ge(xn_made[s].sem, xn_made[s].at(t, 1))
                        pool.sem_inc(passed)
                        pool.tensor_scalar(xns[s][0][:], xn[s][:], 1.0, 0.0, ALU.mult, ALU.add)\
                            .then_inc(xn_high[s].sem, 1)
                    elif step == "up":
                        f = b
                        pool.wait_ge(hid_high[s].sem, hid_high[s].at(t, f + 1))
                        pool.tensor_tensor(hids[1][:, f % 2, :], hid[:, f % 2, :], hids[0][:, f % 2, :].bitcast(F32),
                                           ALU.subtract).then_inc(hid_low[s].sem, 1)
            turns(pool, order, body)

        @block.vector
        def _(dve):
            for n, (w, k, cnt, N, view, is_int) in enumerate(pieces):
                if is_int:
                    dve.wait_ge(landed[n % len(stages)], 16 * (n // len(stages) + 1))
                    dve.tensor_scalar(stage(n), stage(n, I32), DEQUANT, None, ALU.mult).then_inc(scaled, 1)
                dve.wait_ge(split_high, n + 1)
                dve.tensor_tensor(w[1][:, k:k + cnt, :], stage(n), w[0][:, k:k + cnt, :].bitcast(F32),
                                  ALU.subtract).then_inc(split_low, 1)
            dve.wait_ge(split_low, len(pieces))
            dve.wait_ge(cleared, 1)

            def body(i, steps):
                for step, s, b, ahead in steps:
                    t = i + ahead
                    if step == "stats":
                        if b == 0:
                            dve.wait_ge(h_in[s].sem, h_in[s].at(t, 16))
                        else:
                            dve.wait_ge(h_step[s].sem, h_step[s].at(t, NB))
                        for j in range(J):
                            ins = dve.bn_stats(stats[s][:, j, :], h[s][:, j, :])
                        ins.then_inc(ln_step[s].sem, 1)
                        dve.wait_ge(ln_step[s].sem, ln_step[s].at(t, 3 * b + 1))
                        dve.sem_inc(passed)
                        for j in range(J):
                            ins = dve.bn_aggr(mv[s][:, j, :], stats[s][:, j, :])
                        ins.then_inc(ln_step[s].sem, 1)
                        dve.wait_ge(ln_step[s].sem, ln_step[s].at(t, 3 * b + 2))
                        dve.tensor_scalar(var[s][:], mv[s][:, :, 1], EPS_LN_B, None, ALU.add)\
                            .then_inc(ln_step[s].sem, 1)

                    elif step == "ln":
                        if b == 0:
                            dve.wait_ge(out_sent[s].sem, out_sent[s].at(t, 0))
                            dve.sem_inc(passed)
                        dve.wait_ge(ln_rstd[s].sem, ln_rstd[s].at(t, b + 1))
                        for j in range(J):
                            ins = dve.tensor_scalar(xn[s][:, j, :], h[s][:, j, :], mv[s][:, j, 0:1],
                                                    rstd[s][:, j:j + 1], ALU.subtract, ALU.mult)
                        ins.then_inc(xn_made[s].sem, 1)
                        for k in range(KC):
                            dve.wait_ge(xT_high[s].sem, xT_high[s].at(t, KC * b + k + 1))
                            dve.tensor_tensor(xT[s][1][:, k, :], bank("xT", s, b, k)[:],
                                              xT[s][0][:, k, :].bitcast(F32), ALU.subtract)\
                                .then_inc(xT_low[s].sem, 1)
                        if b == 0:
                            dve.wait_ge(xn_high[s].sem, xn_high[s].at(t, 1))
                            dve.tensor_tensor(xns[s][1][:], xn[s][:], xns[s][0][:].bitcast(F32), ALU.subtract)\
                                .then_inc(xn_low[s].sem, 1)

                    elif step == "gram":
                        dve.wait_ge(gram_high[s].sem, gram_high[s].at(t, b + 1))
                        dve.tensor_tensor(gram[b][1][:].rearrange("p k n -> p (k n)"), bank("gram", s, b)[:],
                                          gram[b][0][:].rearrange("p k n -> p (k n)").bitcast(F32), ALU.subtract)\
                            .then_inc(gram_low[s].sem, 1)

                    elif step == "t1":
                        for n in range(2):
                            dve.wait_ge(p_t1[s].sem, p_t1[s].at(t, 4 * b + 2 * n + 2))
                            dve.tensor_copy(t1[:, 1, 512 * n:512 * n + 512], bank("t1", s, b, n, 1)[:])\
                                .then_inc(t1_odd[s].sem, 1)

                    elif step == "kv":
                        for n in range(2):
                            dve.wait_ge(kvs_high[s].sem, kvs_high[s].at(t, 2 * b + n + 1))
                            src = bank("kv", s, b, n)[:].rearrange("p (q d) -> p q d", d=P)
                            for e in range(2):
                                r_, c_ = slice(DK * e, DK * e + DK), slice(DK * e, DK * e + DK)
                                ins = dve.scalar_tensor_tensor(
                                    out=kvs[1][r_, 4 * n:4 * n + 4, c_], in0=src[r_, :, c_], scalar=DK ** -0.5,
                                    in1=kvs[0][r_, 4 * n:4 * n + 4, c_].bitcast(F32), op0=ALU.mult,
                                    op1=ALU.subtract)
                            ins.then_inc(kvs_low[s].sem, 1)

                    elif step == "r":
                        for n in range(4):
                            dve.wait_ge(r_high[s].sem, r_high[s].at(t, 4 * b + n + 1))
                            dve.tensor_tensor(r[1][:, 2 * n:2 * n + 2, :].rearrange("p k n -> p (k n)"),
                                              bank("r", s, b, n)[:],
                                              r[0][:, 2 * n:2 * n + 2, :].rearrange("p k n -> p (k n)").bitcast(F32),
                                              ALU.subtract).then_inc(r_low[s].sem, 1)

                    elif step == "m":
                        dve.wait_ge(m_high[s].sem, m_high[s].at(t, b + 1))
                        dve.tensor_tensor(m[b][1][:].rearrange("p k n -> p (k n)"), bank("m", s, b)[:],
                                          m[b][0][:].rearrange("p k n -> p (k n)").bitcast(F32), ALU.subtract)\
                            .then_inc(m_low[s].sem, 1)

                    elif step == "attn":
                        dve.wait_ge(p_attn[s].sem, p_attn[s].at(t, b + 1))
                        dve.tensor_tensor(h[s][:, b::NB, :], h[s][:, b::NB, :],
                                          bank("attn", s, b)[:].rearrange("p (c n) -> p c n", c=C), ALU.add)\
                            .then_inc(h_step[s].sem, 1)

                    elif step == "up":
                        f = b
                        dve.wait_ge(p_up[s].sem, p_up[s].at(t, f + 1))
                        dve.wait_ge(silu_made[s].sem, silu_made[s].at(t, f + 1))
                        o = 1 - s
                        if f < 2:
                            dve.wait_ge(hid_low[o].sem, hid_low[o].at(t, HC * s))
                        else:
                            dve.wait_ge(hid_low[s].sem, hid_low[s].at(t, f - 1))
                        dve.tensor_tensor(hid[:, f % 2, :], silu[:, f % 2, :], bank("up", s, f)[:], ALU.mult)\
                            .then_inc(hid_made[s].sem, 1)

                    elif step == "add":
                        dve.wait_ge(p_down[s].sem, p_down[s].at(t, HC))
                        for n in range(2):
                            dve.tensor_tensor(xn[s][:, 2 * n:2 * n + 2, :], h[s][:, 2 * n:2 * n + 2, :],
                                              bank("down", s, n)[:].rearrange("p (j n) -> p j n", j=2), ALU.add)\
                                .then_inc(h_step[s].sem, 1)
            turns(dve, order, body)

        @block.scalar
        def _(act):
            n_int = 0
            for n, (w, k, cnt, N, view, is_int) in enumerate(pieces):
                if is_int:
                    n_int += 1
                    act.wait_ge(scaled, n_int)
                else:
                    act.wait_ge(landed[n % len(stages)], 16 * (n // len(stages) + 1))
                act.activation(w[0][:, k:k + cnt, :], stage(n), ACT.Copy).then_inc(split_high, 1)
            act.wait_ge(cleared, 1)
            act.wait_ge(split_low, len(pieces))
            def body(i, steps):
                for step, s, b, ahead in steps:
                    t = i + ahead
                    if step == "ln":
                        for k in range(KC):
                            act.wait_ge(p_xT[s].sem, p_xT[s].at(t, KC * b + k + 1))
                            act.activation(xT[s][0][:, k, :], bank("xT", s, b, k)[:], ACT.Copy)\
                                .then_inc(xT_high[s].sem, 1)

                    elif step == "gram":
                        act.wait_ge(p_gram[s].sem, p_gram[s].at(t, b + 1))
                        act.activation(gram[b][0][:].rearrange("p k n -> p (k n)"), bank("gram", s, b)[:], ACT.Copy)\
                            .then_inc(gram_high[s].sem, 1)

                    elif step == "t1":
                        for n in range(2):
                            act.wait_ge(p_t1[s].sem, p_t1[s].at(t, 4 * b + 2 * n + 1))
                            act.activation(t1[:, 0, 512 * n:512 * n + 512], bank("t1", s, b, n, 0)[:], ACT.Copy)\
                                .then_inc(t1_even[s].sem, 1)

                    elif step == "kv":
                        for n in range(2):
                            act.wait_ge(p_kv[s].sem, p_kv[s].at(t, 2 * b + n + 1))
                            src = bank("kv", s, b, n)[:].rearrange("p (q d) -> p q d", d=P)
                            for e in range(2):
                                r_, c_ = slice(DK * e, DK * e + DK), slice(DK * e, DK * e + DK)
                                ins = act.activation(kvs[0][r_, 4 * n:4 * n + 4, c_], src[r_, :, c_], ACT.Copy,
                                                     scale=DK ** -0.5)
                            ins.then_inc(kvs_high[s].sem, 1)

                    elif step == "r":
                        for n in range(4):
                            act.wait_ge(p_r[s].sem, p_r[s].at(t, 4 * b + n + 1))
                            act.activation(r[0][:, 2 * n:2 * n + 2, :].rearrange("p k n -> p (k n)"),
                                           bank("r", s, b, n)[:], ACT.Copy).then_inc(r_high[s].sem, 1)

                    elif step == "m":
                        act.wait_ge(p_m[s].sem, p_m[s].at(t, b + 1))
                        act.activation(m[b][0][:].rearrange("p k n -> p (k n)"), bank("m", s, b)[:], ACT.Copy)\
                            .then_inc(m_high[s].sem, 1)

                    elif step == "up":
                        f, o = b, 1 - s
                        act.wait_ge(p_gate[s].sem, p_gate[s].at(t, f + 1))
                        if f < 2:
                            act.wait_ge(hid_made[o].sem, hid_made[o].at(t, HC * s))
                        else:
                            act.wait_ge(hid_made[s].sem, hid_made[s].at(t, f - 1))
                        act.activation(silu[:, f % 2, :], bank("gate", s, f)[:], ACT.Silu)\
                            .then_inc(silu_made[s].sem, 1)
                        act.wait_ge(hid_made[s].sem, hid_made[s].at(t, f + 1))
                        if f < 2:
                            act.wait_ge(p_down[o].sem, p_down[o].at(t, HC * s))
                        else:
                            act.wait_ge(p_down[s].sem, p_down[s].at(t, f - 1))
                        act.activation(hids[0][:, f % 2, :], hid[:, f % 2, :], ACT.Copy)\
                            .then_inc(hid_high[s].sem, 1)
            turns(act, order, body)

        @block.tensor
        def _(pe):
            pe.wait_ge(direct, 32)
            pe.wait_ge(split_low, len(pieces))
            pe.wait_ge(cleared, 1)

            def product(out, lhsT, rhs, start=True, stop=True, **kw):
                pe.matmul(out, lhsT[0], rhs[0], start=start, stop=False, **kw)
                pe.matmul(out, lhsT[0], rhs[1], start=False, stop=False, **kw)
                return pe.matmul(out, lhsT[1], rhs[0], start=False, stop=stop, **kw)

            def body(i, steps):
                def claim(*name, inputs=()):
                    wait(pe, i, [*inputs, *banks.last_reads(name, i)])
                    return bank(*name)

                for step, s, b, ahead in steps:
                    t = i + ahead
                    if step == "ln":
                        pe.wait_ge(xn_made[s].sem, xn_made[s].at(t, b + 1))
                        for k in range(KC):
                            out = claim("xT", s, b, k)
                            for j in range(J):
                                ins = pe.transpose(out[:, P * j:P * j + P], xn[s][:, j, P * k:P * k + P], ident[:])
                            ins.then_inc(p_xT[s].sem, 1)

                    elif step == "gram":
                        pe.wait_ge(xn_low[s].sem, xn_low[s].at(t, 1))
                        out = claim("gram", s, b)
                        for k in range(KC):
                            for c in range(C):
                                j = NB * c + b
                                ins = product(out[:, DM * k:DM * k + DM], [t[:, j, P * k:P * k + P] for t in xns[s]],
                                              [t[:, j, :] for t in xns[s]], start=(c == 0), stop=(c == C - 1))
                        ins.then_inc(p_gram[s].sem, 1)

                    elif step == "t1":
                        for n in range(2):
                            for k in range(KC):
                                out = claim("t1", s, b, n, k, inputs=[(gram_low[s], b + 1, ahead)])
                                for q in range(KC):
                                    ins = product(out[:], [t[:, q, P * k:P * k + P] for t in gram[b]],
                                                  [w[:, q, 512 * n:512 * n + 512] for w in wv],
                                                  start=(q == 0), stop=(q == KC - 1))
                                ins.then_inc(p_t1[s].sem, 1)

                    elif step == "kv":
                        for n in range(2):
                            out = claim("kv", s, b, n, inputs=[(t1_even[s], 2 * b + n + 1, ahead), (t1_odd[s], 2 * b + n + 1, ahead)])
                            for q in range(PAIRS // 2):
                                c = slice(P * (4 * n + q), P * (4 * n + q) + P)
                                for k in range(KC):
                                    ins = pe.matmul(out[:, P * q:P * q + P], t1[:, k, c], wk[:, k, c],
                                                    start=(k == 0), stop=(k == KC - 1))
                            ins.then_inc(p_kv[s].sem, 1)

                    elif step == "r":
                        for n in range(4):
                            out = claim("r", s, b, n, inputs=[(kvs_low[s], 2 * b + n // 2 + 1, ahead)])
                            for q in range(2):
                                ins = product(out[:, DM * q:DM * q + DM], [t[:, 2 * n + q, :] for t in kvs],
                                              [w[:, 2 * n + q, :] for w in wo])
                            ins.then_inc(p_r[s].sem, 1)

                    elif step == "m":
                        out = claim("m", s, b, inputs=[(r_low[s], 4 * b + 1, ahead)])
                        for k in range(KC):
                            for q in range(PAIRS):
                                if k == 0 and q % 2 == 0 and q > 0:
                                    pe.wait_ge(r_low[s].sem, r_low[s].at(t, 4 * b + q // 2 + 1))
                                ins = product(out[:, DM * k:DM * k + DM], [w[:, q, P * k:P * k + P] for w in wq],
                                              [t[:, q, :] for t in r], start=(q == 0), stop=(q == PAIRS - 1))
                        ins.then_inc(p_m[s].sem, 1)

                    elif step == "attn":
                        out = claim("attn", s, b, inputs=[(m_low[s], b + 1, ahead), (xT_low[s], KC, ahead)])
                        for c in range(C):
                            j = NB * c + b
                            for k in range(KC):
                                ins = product(out[:, DM * c:DM * c + DM], [t[:, k, P * j:P * j + P] for t in xT[s]],
                                              [t[:, k, :] for t in m[b]], start=(k == 0), stop=(k == KC - 1))
                        ins.then_inc(p_attn[s].sem, 1)

                    elif step == "up":
                        f = b
                        for w, name, sig in ((wg, "gate", p_gate), (wu, "up", p_up)):
                            out = claim(name, s, f, inputs=[(xT_low[s], 2 * KC, ahead)] if f == 0 else [])
                            for k in range(KC):
                                ins = product(out[:], [t[:, k, P * f:P * f + P] for t in w],
                                              [t[:, k, :] for t in xT[s]], start=(k == 0), stop=(k == KC - 1))
                            ins.then_inc(sig[s].sem, 1)

                    elif step == "down":
                        f = b
                        pe.wait_ge(hid_low[s].sem, hid_low[s].at(t, f + 1))
                        for j in range(J):
                            if f == 0 and j % 2 == 0:
                                claim("down", s, j // 2)
                            out = bank("down", s, j // 2)
                            ins = product(out[:, DM * (j % 2):DM * (j % 2) + DM],
                                          [t[:, f % 2, P * j:P * j + P] for t in hids],
                                          [w[:, f, :] for w in wd], start=(f == 0 and j % 2 == 0),
                                          stop=(f == HC - 1), skip_group_check=True)
                        ins.then_inc(p_down[s].sem, 1)

                if i is FIRST:
                    wait(pe, 0, banks.reads_ahead())

            turns(pe, order, body)



def layout(t):
    import numpy as np
    g = {k[len("L0_tok_"):]: np.asarray(v) for k, v in t.items() if k.startswith("L0_tok_")}
    ids = np.asarray(t["x"]).reshape(GROUPS, NB, C, P).transpose(0, 3, 2, 1).reshape(GROUPS, P, J)
    position = np.arange(SEQ)[:, None]
    div = np.exp(np.arange(0, D, 2) * (-np.log(10000.0) / D))
    pe = np.zeros((SEQ, D), np.float32)
    pe[:, 0::2] = np.sin(position * div)
    pe[:, 1::2] = np.cos(position * div)
    r = np.arange(P)
    filters = np.concatenate([np.zeros((HEADS, P - 1), np.float32), g["spectral_basis"].T], 1)
    ln = lambda k: np.stack([g[f"ln1_{k}"][0], g[f"ln2_{k}"][0], g[f"ln1_{k}"][1], g[f"ln2_{k}"][1],
                             g[f"lnf_{k}"]], 1)
    out = {
        "token_ids": np.concatenate([ids, np.zeros((STREAMS, P, J), ids.dtype)]),
        "pos": pe, "ident": np.eye(P, dtype=np.float32), "flip": np.eye(P, dtype=np.float32)[::-1],
        "causal": (r[:, None] <= r[None, :]).astype(np.float32),
        "same_head": (r[:, None] // HD == r[None, :] // HD).astype(np.float32),
        "filters": filters, "ln_s": ln("s"), "ln_b": ln("b"),
        "b_q": g["wq_b"].T, "b_f1": g["ff1_b"].reshape(LAYERS, FC, P).transpose(2, 0, 1),
    }
    for k in ("embed", "wq_k", "wk_k", "wv_k", "wo_k", "wk_b", "wv_b", "wo_b", "gate_k", "gate_b", "ff1_k", "ff2_k",
              "ff2_b", "out_k", "out_b"):
        out[k] = g[k]
    at, ff = "L0_attn_", "L0_ffn_"
    out["W_q"] = np.asarray(t[at + "W_q"])
    for k in ("W_k", "W_v", "W_o"):
        out[k + "T"] = np.asarray(t[at + k]).T
    for k in ("w_gate", "w_up", "w_down"):
        out[k + "T"] = np.asarray(t[ff + k]).T
    return {k: np.ascontiguousarray(v) for k, v in out.items()}


def kernel(**inputs):
    import numpy as np
    import concourse.bacc as bacc
    from concourse.bass_utils import run_bass_kernel_spmd

    arrays = {f"in_{k}": v for k, v in layout(inputs).items()}
    nc = bacc.Bacc("TRN2", target_bir_lowering=False, num_devices=1)
    a = {k[3:]: nc.dram_tensor(k, v.shape, mybir.dt.from_np(v.dtype), kind="ExternalInput").ap()
         for k, v in arrays.items()}
    h_rows = nc.dram_tensor("h_rows", (GROUPS, P, J, V), F32).ap()
    out = nc.dram_tensor("out", (BATCH, SEQ, V), F32, kind="ExternalOutput").ap()
    with ExitStack() as ctx:
        semaphores = Semaphores(ctx, nc)
        token_tower(nc, semaphores, a, h_rows)
        semaphores.retire(BODIES)
        attention_and_mlp(nc, semaphores, a, h_rows, out.rearrange("(g b) (c p) n -> g b p c n", b=NB, p=P))
    r = run_bass_kernel_spmd(nc, [arrays], core_ids=[0])
    return r.results[0]["out"]
```

```python
from contextlib import ExitStack

import concourse.bass as bass
from concourse import mybir

F32 = mybir.dt.float32
F32R = mybir.dt.float32r
I32 = mybir.dt.int32
ALU = mybir.AluOpType
ACT = mybir.ActivationFunctionType
AX_X = mybir.AxisListType.X

P = 128
BATCH, SEQ = 32, 256
C = SEQ // P
NB = 2
J = C * NB
TOK = J * P
GROUPS = BATCH // NB
STREAMS = 2
BODIES = GROUPS // STREAMS
D, V, LAYERS, HEADS = 128, 256, 2, 8
HD = D // HEADS
FF = 4 * D
FC = FF // P
EPS_LN, EPS_LN_B, EPS_NORM, EPS = 1e-6, 1e-5, 1e-5, 1e-5
HALF = HEADS // 2
PAIR = 2
BLOCK = PAIR * HD
PAIRS_A = HEADS // PAIR
Q_PARTS = (0, 1, 0)
ROWS = BLOCK * len(Q_PARTS)
FIRST, LAST = -1, BODIES - 1
AFTER = [[2, 6, 7, 7, 8, 8, 8, 9, 9, 9, 11, 12, 12, 14, 14, 15, 15, 15, 19, 19],
         [0, 2, 4, 4, 4, 5, 6, 6, 7, 8, 8, 8, 9, 9, 9, 10, 10, 12, 12, 12, 14, 14, 18, 19, 19],
         [0, 2, 2, 2, 4, 5, 6, 6, 7, 8, 8, 8, 9, 9, 9, 10, 10, 12, 12, 12, 14, 14, 15, 19, 19],
         [2, 6, 7, 7, 7, 7, 7, 9, 9, 9, 11, 12, 12, 14, 14, 14, 14, 14, 19, 19]]
RSQRT_SEED = float(0x5F3759DF)


class Signal:

    def __init__(self, sem, base, per_turn, ahead):
        self.sem, self.base, self.per_turn, self.ahead = sem, base, per_turn, ahead

    def at(self, i, k):
        return i * self.per_turn + (self.base + k)


class Semaphores:

    def __init__(self, ctx, nc):
        self.ctx, self.nc, self.live, self.retired = ctx, nc, [], []

    def one(self, name):
        return self.ctx.enter_context(self.nc.semaphore(name))

    def counted(self, name, per_turn, ahead=0, base=1):
        sem, base = self.retired.pop() if self.retired else (self.one(name), base)
        sig = Signal(sem, base, per_turn, ahead)
        self.live.append(sig)
        return sig

    def raise_new(self, eng):
        for sig in self.live:
            if sig.base == 1:
                eng.sem_inc(sig.sem)

    def retire(self, turns):
        self.retired = [(sig.sem, sig.at(turns, sig.ahead)) for sig in self.live]
        self.live = []


class Banks:

    def __init__(self, ring, products):
        self.bank, self.position = {}, {}
        self.occupants = {b: [] for b in range(8)}
        n = 0
        for name, fixed, signal, k, ahead in products:
            b = fixed
            if b is None:
                b = ring[n % len(ring)]
                n += 1
            self.bank[name] = b
            self.position[name] = len(self.occupants[b])
            self.occupants[b].append((signal, k, ahead))

    def last_reads(self, name, i):
        occupants, n = self.occupants[self.bank[name]], self.position[name]
        before = [(sig, k, ahead) for sig, k, ahead in occupants[n:]]
        earlier = [(sig, k, 0) if ahead else (sig, 0, 0) for sig, k, ahead in before] + occupants[:n]
        if i is FIRST:
            earlier = [(sig, k, shift) for sig, k, shift in occupants[:n] if shift == 1]
        elif i is LAST:
            earlier = [read for read in earlier if read[2] <= 0]
        return earlier[-1:]

    def reads_ahead(self):
        last = [[(sig, k, 0) for sig, k, ahead in occupants if ahead][-1:] for occupants in self.occupants.values()]
        return [read for reads in last for read in reads]


def wait(eng, i, needs):
    last = {}
    for sig, k, shift in needs:
        last[sig] = max((shift, k), last.get(sig, (shift, k)))
    for sig, (shift, k) in last.items():
        value = sig.at(i, shift * sig.per_turn + k)
        if not (isinstance(value, int) and value <= sig.base):
            eng.wait_ge(sig.sem, value)


def turns(eng, order, body):
    body(FIRST, [step for step in order if step[-1]])
    with eng.Fori(0, LAST) as i:
        body(i, order)
    body(LAST, [step for step in order if not step[-1]])


def token_tower(nc, semaphores, a, h_rows):
    with ExitStack() as ctx:
        def sb(name, shape, dt=F32):
            return ctx.enter_context(nc.sbuf_tensor(name, shape, dt))

        def each(name, shape, dt=F32):
            return [sb(f"{name}{s}", shape, dt) for s in range(STREAMS)]

        def signals(name, per_turn, ahead=0, base=1):
            return [semaphores.counted(f"{name}{s}", per_turn, ahead, base) for s in range(STREAMS)]

        def sem(name):
            return semaphores.one(name)

        ident = sb("ident", [P, P])
        causal = sb("causal", [P, P])
        same_head = sb("same_head", [P, P])
        ones = sb("ones", [P, P])
        pos = sb("pos", [P, C, D])
        taps = sb("taps", [P, HEADS, SEQ])
        w_q = [[sb(f"w_q{l}{h}", [P, D], F32R) for h in "hl"] for l in range(LAYERS)]
        w_kv = [[sb(f"w_kv{l}{h}", [P, 2 * D], F32R) for h in "hl"] for l in range(LAYERS)]
        w_f1 = [[sb(f"w_f1{l}{h}", [P, FF], F32R) for h in "hl"] for l in range(LAYERS)]
        w_head = [sb(f"w_head{h}", [P, V], F32R) for h in "hl"]
        w_o = [sb(f"w_o{l}", [P, D]) for l in range(LAYERS)]
        w_f2 = [sb(f"w_f2{l}", [P, FC, D]) for l in range(LAYERS)]
        w_gate = [sb(f"w_gate{l}", [P, D]) for l in range(LAYERS)]
        b_q = sb("b_q", [P, LAYERS])
        b_kv = sb("b_kv", [P, LAYERS, 2 * D])
        b_f1 = sb("b_f1", [P, LAYERS, FC])
        b_head = sb("b_head", [P, V])
        b_o = sb("b_o", [P, LAYERS, D])
        b_f2 = sb("b_f2", [P, LAYERS, D])
        b_gate = sb("b_gate", [P, LAYERS])
        minus_half = sb("minus_half", [P, J])

        idx = each("idx", [P, J], I32)
        emb = each("emb", [P, J, D])
        x = each("x", [P, J, D])
        xn = each("xn", [P, J, D])
        stats = each("stats", [P, J, 6])
        mv = each("mv", [P, J, 2])
        var = each("var", [P, J])
        rstd = each("rstd", [P, J])
        xT = [[sb(f"xT{s}{h}", [P, TOK], F32R) for h in "hl"] for s in range(STREAMS)]
        qT = each("qT", [P, 2, TOK], F32R)
        qT_last = each("qT_last", [P, NB * P])
        kv = each("kv", [P, HEADS, C, NB, 2, HD])
        vc = each("vc", [P, J, D])
        kc = each("kc", [P, J, D])
        vT = each("vT", [P, TOK])
        v_thrice = each("v_thrice", [P, J, PAIRS_A, len(Q_PARTS), BLOCK])
        v_rows = each("v_rows", [P, HEADS // PAIR, TOK], F32R)
        gate = each("gate", [P, J * HEADS])
        state = each("state", [P, NB, D])
        floor = each("floor", [P, J * HEADS])
        sq = each("sq", [P, J * HEADS, HD])
        m2 = each("m2", [P, J * HEADS])
        mh = each("mh", [P, J * HEADS])
        y = each("y", [P, J * HEADS])
        yy = each("yy", [P, J * HEADS])
        oTn = each("oTn", [P, TOK])
        gl = each("gl", [P, FC, TOK])
        h_out = each("h_out", [P, J, V])
        q_rows = sb("q_rows", [P, PAIR, HEADS // PAIR, TOK], F32R)
        gk = sb("gk", [P, J, HEADS, D])
        att = sb("att", [P, 2, HEADS, P])
        gk_heads = gk[:].rearrange("p j h (g e) -> p j (h g) e", e=HD)[:, :, ::HEADS + 1, :]

        ps = [ctx.enter_context(nc.psum_tensor(f"ps{n}", [P, 512], F32)) for n in range(8)]

        loaded, loaded_late, zeroed = sem("loaded"), sem("loaded_late"), sem("zeroed")
        prep, shifted, scaled, w_high, ready = sem("prep"), sem("shifted"), sem("scaled"), sem("w_high"), sem("ready")
        passed = sem("passed")
        L = LAYERS
        LN = 2 * L + 1
        idx_in = signals("idx_in", 16, ahead=16)
        emb_in = signals("emb_in", 16 * J, ahead=16 * J, base=0)
        Q_DMAS = 16 * len(Q_PARTS) * HEADS
        q_spread = signals("q_spread", Q_DMAS * L)
        h_stored = signals("h_stored", 16)
        x_step = signals("x_step", 1 + 4 * L)
        ln_step = signals("ln_step", 3 * LN)
        ln_rstd = signals("ln_rstd", LN)
        xn_made = signals("xn_made", J * LN)
        xT_low = signals("xT_low", LN)
        q_low = signals("q_low", L)
        kv_made = signals("kv_made", 2 * L)
        v_low = signals("v_low", PAIRS_A * L)
        gate_step = signals("gate_step", 6 * L)
        state_step = signals("state_step", 3 * L)
        att_made = signals("att_made", 2 * J * L)
        NORM = 14
        norm_step = signals("norm_step", NORM * L)
        h_made = signals("h_made", 2)
        xT_high = signals("xT_high", LN)
        q_high = signals("q_high", 2 * L)
        vc_made = signals("vc_made", 2 * L)
        kc_made = signals("kc_made", 2 * L)
        vT_made = signals("vT_made", L)
        v_repeated = signals("v_repeated", PAIRS_A * L)
        v_high = signals("v_high", PAIRS_A * L)
        sq_made = signals("sq_made", L)
        oTn_made = signals("oTn_made", L)
        gl_made = signals("gl_made", FC * L)
        p_xT = signals("p_xT", LN)
        p_q = signals("p_q", L)
        p_kv = signals("p_kv", 2 * L)
        p_conv = signals("p_conv", 2 * L)
        p_vT = signals("p_vT", L)
        p_rows = signals("p_rows", PAIRS_A * L)
        p_vg = signals("p_vg", L)
        p_state = signals("p_state", L)
        p_qk = signals("p_qk", 2 * J * L)
        p_av = signals("p_av", J * L)
        p_unit = signals("p_unit", L)
        p_wo = signals("p_wo", L)
        p_f1 = signals("p_f1", FC * L)
        p_f2 = signals("p_f2", L)
        p_head = signals("p_head", 2)

        def norm(s, u, ahead):
            return [("stats", s, u, 0, ahead), ("ln", s, u, 0, ahead), ("low", s, u, 0, ahead)]

        def front(s, l, ahead):
            return norm(s, 2 * l, ahead) + [(step, s, l, n, ahead) for step, n in (
                ("q", 0), ("kv", 0), ("q_low", 0), ("kv", 1), ("conv", 0), ("repeat", 0), ("conv", 1), ("repeat", 1),
                ("turn_v", 0), ("gate", 0),
                ("rows", 0), ("rows", 1), ("rows", 2), ("rows", 3),
                ("gated", 0), ("state", 0), ("state_low", 0))]

        def back(s, l, ahead):
            steps = [("qk", 0), ("qk", 1), ("av", 0), ("qk", 2), ("av", 1), ("qk", 3), ("av", 2), ("av", 3),
                     ("norm", 0), ("chain", 0), ("unit", 0), ("wo", 0)]
            return [(step, s, l, j, ahead) for step, j in steps] + norm(s, 2 * l + 1, ahead) + \
                [(step, s, l, f, ahead) for step, f in [("f1", f) for f in range(FC)] + [("f2", 0)]]

        def head(s, ahead):
            return norm(s, 2 * L, ahead) + [("head", s, 0, 0, ahead)]

        def woven(long, short, after):
            out = []
            for n, step in enumerate(long):
                out.append(step)
                out += [short[k] for k in range(len(short)) if after[k] == n]
            return out

        def next_turn(s):
            stats, ln, low, out = head(s, 0)
            first = front(s, 0, 1)
            return [stats, ln, ("embed", s, 0, 0, 1), low, first[0], out] + first[1:]

        order = woven(back(0, 1, 0), front(1, 1, 0), AFTER[0])
        order += woven(back(1, 1, 0), next_turn(0), AFTER[1])
        order += woven(back(0, 0, 1), next_turn(1), AFTER[2])
        order += woven(back(1, 0, 1), front(0, 1, 1), AFTER[3])

        products = []
        for step, s, l, j, ahead in order:
            if step == "ln":
                products.append((("xT", s, l), None, xT_low[s], l + 1, ahead))
            elif step == "q":
                products.append((("q", s, l), None, q_low[s], l + 1, ahead))
            elif step == "kv":
                products.append((("kv", s, l, j), None, kv_made[s], 2 * l + j + 1, ahead))
            elif step == "conv":
                products.append((("conv", s, l, j), None, kc_made[s], 2 * l + j + 1, ahead))
            elif step == "turn_v":
                products.append((("vT", s, l), None, vT_made[s], l + 1, ahead))
            elif step == "rows":
                products.append((("rows", s, l, j), None, v_low[s], PAIRS_A * l + j + 1, ahead))
            elif step == "gate":
                products.append((("vg", s, l), None, gate_step[s], 6 * l + 1, ahead))
            elif step == "state":
                products.append((("state", s, l), None, state_step[s], 3 * l + 3, ahead))
            elif step == "qk":
                for n in range(2):
                    products.append((("qk", s, l, j, n), None, att_made[s], 2 * (J * l + j) + n + 1, ahead))
            elif step == "av" and j == 0:
                products.append((("av", s, l), 7, norm_step[s], NORM * (l + 1), ahead))
            elif step == "unit":
                products.append((("unit", s, l), 7, oTn_made[s], l + 1, ahead))
            elif step == "wo":
                products.append((("wo", s, l), 7, x_step[s], 4 * l + 3, ahead))
            elif step == "f1":
                products.append((("f1", s, l, j), None, gl_made[s], FC * l + j + 1, ahead))
            elif step == "f2":
                products.append((("f2", s, l), None, x_step[s], 4 * l + 5, ahead))
            elif step == "head":
                for n in range(2):
                    products.append((("head", s, n), None, h_made[s], n + 1, ahead))
        banks = Banks(range(7), products)

        def bank(*name):
            return ps[banks.bank[name]]

        raw_q = xn[0][:].rearrange("p j d -> p (j d)")[:, 0:L * D].rearrange("p (l d) -> p l d", l=L)
        raw_kv = kv[0][:].rearrange("p h c b v e -> p (h c b v e)")[:, 0:L * 2 * D].rearrange("p (l d) -> p l d", l=L)
        raw_f1 = gl[0][:].rearrange("p f t -> p (f t)")[:, 0:L * FF].rearrange("p (l d) -> p l d", l=L)
        raw_head = sq[0][:].rearrange("p a e -> p (a e)")[:, 0:V]
        ln_s = sb("ln_s", [P, LN])
        ln_b = sb("ln_b", [P, LN])
        ln_b_rows = sb("ln_b_rows", [P, LN, P])

        block = ctx.enter_context(nc.Block())
        loads = [(ln_s[:], a["ln_s"]), (ln_b[:], a["ln_b"]),
                 (raw_q, a["wq_k"].rearrange("l c n -> c l n")),
                 (raw_kv[:, :, 0:D], a["wk_k"].rearrange("l c n -> c l n")),
                 (raw_kv[:, :, D:2 * D], a["wv_k"].rearrange("l c n -> c l n")),
                 (raw_f1, a["ff1_k"].rearrange("l c n -> c l n")),
                 (raw_head, a["out_k"]), (b_q[:], a["b_q"]), (b_f1[:], a["b_f1"])]
        late = [(ident[:], a["ident"]), (causal[:], a["causal"]), (same_head[:], a["same_head"]),
                (pos[:], a["pos"].rearrange("(c p) d -> p c d", p=P))]
        for l in range(L):
            late += [(w_o[l][:], a["wo_k"][l]),
                     (w_f2[l][:], a["ff2_k"][l].rearrange("(f p) n -> p f n", p=P))]
        for to, out, src in ((loads, b_kv[:, :, 0:D], a["wk_b"]), (loads, b_kv[:, :, D:2 * D], a["wv_b"]),
                             (late, b_o[:], a["wo_b"]), (late, b_f2[:], a["ff2_b"])):
            to.append((out, src.unsqueeze(0).to_broadcast([P, L, D])))
        loads.append((b_head[:], a["out_b"].unsqueeze(0).to_broadcast([P, V])))
        late.append((b_gate[:], a["gate_b"].rearrange("l o -> o l").to_broadcast([P, L])))
        flt = a["filters"]
        delayed = att[:].rearrange("p n h t -> p (n h t)")
        flip = oTn[0][:, 0:P]
        loads.append((delayed.rearrange("p (h t) -> p h t", h=HEADS),
                      bass.AP(tensor=flt.tensor, offset=flt.offset,
                              ap=[[1, P], [P - 1 + SEQ, HEADS], [1, SEQ]])))
        loads.append((flip, a["flip"]))
        gate_loads = [(w_gate[l][HD * h:HD * h + HD, HD * h:HD * h + HD],
                       a["gate_k"][l].rearrange("(d e) o -> d (e o)", e=HD))
                      for l in range(L) for h in range(HEADS)]

        @block.sync
        def _(sp):
            semaphores.raise_new(sp)
            for out, src in loads:
                sp.dma_start(out, src).then_inc(loaded, 16)
            for out, src in late:
                sp.dma_start(out, src).then_inc(loaded_late, 16)
            for s in range(STREAMS):
                sp.dma_start(idx[s][:], a["token_ids"][s]).then_inc(idx_in[s].sem, 16)
            sp.wait_ge(zeroed, 1)
            for out, src in gate_loads:
                sp.dma_start(out, src).then_inc(loaded_late, 16)
            def body(i, steps):
                for step, s, l, j, ahead in steps:
                    t = i + ahead
                    if step == "embed":
                        sp.wait_ge(emb_in[s].sem, emb_in[s].at(t, 16 * J))
                        sp.sem_inc(passed)
                        sp.dma_start(idx[s][:], a["token_ids"][t * STREAMS + (STREAMS + s)])\
                            .then_inc(idx_in[s].sem, 16)
                    elif step == "q_low":
                        sp.wait_ge(q_low[s].sem, q_low[s].at(t, l + 1))
                        sp.sem_inc(passed)
                        o = 1 - s
                        used = J * 2 * (l + 1 if s else l)
                        wait(sp, t, [(p_qk[o], used, 0)])
                        sp.sem_inc(passed)
                        for h in range(HEADS):
                            src = slice(HD * h, HD * h + HD)
                            for n, part in enumerate(Q_PARTS):
                                r = BLOCK * n + HD * (h % PAIR)
                                sp.dma_start(q_rows[r:r + HD, h % PAIR, h // PAIR, :].bitcast(F32),
                                             qT[s][src, part, :].bitcast(F32)).then_inc(q_spread[s].sem, 16)
                    elif step == "head":
                        sp.wait_ge(h_made[s].sem, h_made[s].at(t, 2))
                        sp.sem_inc(passed)
                        sp.dma_start(h_rows[t * STREAMS + s], h_out[s][:]).then_inc(h_stored[s].sem, 16)
            turns(sp, order, body)
            for s in range(STREAMS):
                sp.wait_ge(h_stored[s].sem, h_stored[s].at(BODIES, 0))
                sp.wait_ge(idx_in[s].sem, idx_in[s].at(BODIES, 16))

        split = [(raw[:, l, :], pair, u) for l in range(L) for raw, pair, u in (
            (raw_q, w_q[l], 2 * l), (raw_kv, w_kv[l], 2 * l), (raw_f1, w_f1[l], 2 * l + 1))]
        split.append((raw_head, w_head, 2 * L))
        TAPS = 4

        @block.gpsimd
        def _(pool):
            for l in range(L):
                ins = pool.memset(w_gate[l][:], 0.0)
            ins.then_inc(zeroed, 1)
            pool.memset(ones[:], 1.0)
            pool.memset(minus_half[:], -0.5)
            pool.memset(gk[:], 0.0)
            pool.memset(q_rows[:].bitcast(F32), 0.0).then_inc(zeroed, 1)

            def gather(s):
                for j in range(J):
                    pool.indirect_dma_start(emb[s][:, j, :], None, a["embed"],
                                            bass.IndirectOffsetOnAxis(ap=idx[s][:, j:j + 1], axis=0))\
                        .then_inc(emb_in[s].sem, 16)

            for s in range(STREAMS):
                pool.wait_ge(idx_in[s].sem, idx_in[s].at(0, 16))
                gather(s)
            pool.wait_ge(ready, 1)
            def body(i, steps):
                for step, s, l, j, ahead in steps:
                    t = i + ahead
                    if step == "embed":
                        pool.wait_ge(emb_in[s].sem, emb_in[s].at(t, 16 * J))
                        pool.wait_ge(xn_made[s].sem, xn_made[s].at(t, 0))
                        for c in range(C):
                            ins = pool.tensor_tensor(x[s][:, NB * c:NB * c + NB, :], emb[s][:, NB * c:NB * c + NB, :],
                                                    pos[:, c, :].unsqueeze(1).to_broadcast([P, NB, D]), ALU.add)
                        ins.then_inc(x_step[s].sem, 1)
                    elif step == "stats":
                        pool.wait_ge(ln_step[s].sem, ln_step[s].at(t, 3 * l + 3))
                        pool.tensor_tensor(rstd[s][:], var[s][:], minus_half[:], ALU.pow)\
                            .then_inc(ln_rstd[s].sem, 1)
                    elif step == "ln" and l < 2 * L:
                        pool.wait_ge(xn_made[s].sem, xn_made[s].at(t, J * (l + 1)))
                        bias = (b_f2 if l % 2 else b_o)[:, l // 2, :]
                        pool.tensor_tensor(x[s][:], x[s][:], bias.unsqueeze(1).to_broadcast([P, J, D]),
                                           ALU.add).then_inc(x_step[s].sem, 1)
                    elif step == "f2" and l == 0:
                        pool.wait_ge(idx_in[s].sem, idx_in[s].at(t, 32))
                        pool.wait_ge(x_step[s].sem, x_step[s].at(t, 1))
                        pool.sem_inc(passed)
                        gather(s)
            turns(pool, order, body)
            for s in range(STREAMS):
                pool.wait_ge(emb_in[s].sem, emb_in[s].at(BODIES, 16 * J))

        @block.vector
        def _(dve):
            dve.wait_ge(loaded, 16 * len(loads))
            for u in range(LN):
                dve.tensor_copy(ln_b_rows[:, u, :], ln_b[:, u:u + 1].to_broadcast([P, P])).then_inc(prep, 1)
            for l in range(L):
                for k in (raw_kv[:, l, 0:D], b_kv[:, l, 0:D]):
                    dve.tensor_scalar(k, k, HD ** -0.5, None, ALU.mult).then_inc(prep, 1)
            n_prep = LN + 2 * L
            dve.wait_ge(prep, n_prep)
            dve.wait_ge(shifted, 1)
            for raw, pair, u in split:
                dve.tensor_scalar(raw, raw, ln_s[:, u:u + 1], None, ALU.mult).then_inc(scaled, 1)
            for bias, shift in ((b_q[:], ps[0][:, 0:L]),
                                (b_f1[:], ps[0][:, L:L + L * FC].rearrange("p (l f) -> p l f", l=L)),
                                (b_kv[:], ps[1][:].rearrange("p (l d) -> p l d", l=L)),
                                (b_head[:], ps[2][:, 0:V])):
                dve.tensor_tensor(bias, bias, shift, ALU.add).then_inc(prep, 1)
                n_prep += 1
            for n, (raw, pair, u) in enumerate(split):
                dve.wait_ge(w_high, n + 1)
                dve.tensor_tensor(pair[1][:], raw, pair[0][:].bitcast(F32), ALU.subtract).then_inc(prep, 1)
                n_prep += 1
            dve.wait_ge(prep, n_prep)
            dve.wait_ge(w_high, len(split) + TAPS)
            dve.wait_ge(loaded_late, 16 * (len(late) + len(gate_loads)))
            dve.wait_ge(zeroed, 2)
            dve.sem_inc(ready)

            def body(i, steps):
                for step, s, l, j, ahead in steps:
                    t = i + ahead
                    if step == "stats":
                        dve.wait_ge(x_step[s].sem, x_step[s].at(t, 2 * l + 1))
                        for j in range(J):
                            ins = dve.bn_stats(stats[s][:, j, :], x[s][:, j, :])
                        ins.then_inc(ln_step[s].sem, 1)
                        dve.wait_ge(ln_step[s].sem, ln_step[s].at(t, 3 * l + 1))
                        dve.sem_inc(passed)
                        for j in range(J):
                            ins = dve.bn_aggr(mv[s][:, j, :], stats[s][:, j, :])
                        ins.then_inc(ln_step[s].sem, 1)
                        dve.wait_ge(ln_step[s].sem, ln_step[s].at(t, 3 * l + 2))
                        dve.tensor_scalar(var[s][:], mv[s][:, :, 1], EPS_LN, None, ALU.add)\
                            .then_inc(ln_step[s].sem, 1)

                    elif step == "ln":
                        dve.wait_ge(ln_rstd[s].sem, ln_rstd[s].at(t, l + 1))
                        for j in range(J):
                            ins = dve.tensor_scalar(xn[s][:, j, :], x[s][:, j, :], mv[s][:, j, 0:1],
                                                    rstd[s][:, j:j + 1], ALU.subtract, ALU.mult)
                            ins.then_inc(xn_made[s].sem, 1)

                    elif step == "low":
                        dve.wait_ge(p_xT[s].sem, p_xT[s].at(t, l + 1))
                        dve.wait_ge(xT_high[s].sem, xT_high[s].at(t, l + 1))
                        dve.tensor_tensor(xT[s][1][:], bank("xT", s, l)[:], xT[s][0][:].bitcast(F32), ALU.subtract)\
                            .then_inc(xT_low[s].sem, 1)

                    elif step == "q_low":
                        dve.wait_ge(q_high[s].sem, q_high[s].at(t, 2 * l + 2))
                        dve.scalar_tensor_tensor(out=qT[s][:, 1, :], in0=bank("q", s, l)[:], scalar=b_q[:, l:l + 1],
                                                 in1=qT[s][:, 0, :].bitcast(F32), op0=ALU.add, op1=ALU.subtract)\
                            .then_inc(q_low[s].sem, 1)

                    elif step == "kv":
                        dve.wait_ge(p_kv[s].sem, p_kv[s].at(t, 2 * l + j + 1))
                        for b in range(NB):
                            ins = dve.tensor_tensor(
                                kv[s][:, :, j, b, :, :],
                                bank("kv", s, l, j)[:, 2 * D * b:2 * D * b + 2 * D].rearrange(
                                    "p (v h e) -> p h v e", v=2, h=HEADS),
                                b_kv[:, l, :].rearrange("p (v h e) -> p h v e", v=2, h=HEADS), ALU.add)
                        ins.then_inc(kv_made[s].sem, 1)

                    elif step == "rows":
                        k = PAIRS_A * l + j + 1
                        dve.wait_ge(v_high[s].sem, v_high[s].at(t, k))
                        r = slice(ROWS - BLOCK, ROWS)
                        dve.tensor_tensor(v_rows[s][r, j, :], bank("rows", s, l, j)[r, :],
                                          v_rows[s][r, j, :].bitcast(F32), ALU.subtract).then_inc(v_low[s].sem, 1)

                    elif step == "gate":
                        k = 6 * l
                        g = gate_step[s]
                        dve.wait_ge(p_vg[s].sem, p_vg[s].at(t, l + 1))
                        dve.wait_ge(kc_made[s].sem, kc_made[s].at(t, 2 * l + 2))
                        dve.tensor_tensor(sq[s][:].rearrange("p a e -> p (a e)"), bank("vg", s, l)[:],
                                          kc[s][:].rearrange("p j d -> p (j d)"), ALU.mult).then_inc(g.sem, 1)

                    elif step == "gated":
                        k = 6 * l
                        g = gate_step[s]
                        dve.wait_ge(g.sem, g.at(t, k + 1))
                        dve.tensor_reduce(gate[s][:], sq[s][:], AX_X, ALU.add).then_inc(g.sem, 1)
                        dve.wait_ge(g.sem, g.at(t, k + 2))
                        dve.tensor_scalar(gate[s][:], gate[s][:], b_gate[:, l:l + 1], 0.0, ALU.add, ALU.max)\
                            .then_inc(g.sem, 1)
                        dve.wait_ge(g.sem, g.at(t, k + 3))
                        dve.tensor_tensor(gate[s][:], gate[s][:], gate[s][:], ALU.mult).then_inc(g.sem, 1)
                        dve.wait_ge(g.sem, g.at(t, k + 4))
                        dve.tensor_scalar(gate[s][:], gate[s][:], EPS, None, ALU.add).then_inc(g.sem, 1)
                        dve.wait_ge(g.sem, g.at(t, k + 5))
                        o = 1 - s
                        wait(dve, t, [(p_av[o], J * (l + 1 if s else l), 0)])
                        dve.tensor_tensor(gk_heads, kc[s][:].rearrange("p j (h e) -> p j h e", h=HEADS),
                                          gate[s][:].rearrange("p (j h) -> p j h", h=HEADS).unsqueeze(3)
                                          .to_broadcast([P, J, HEADS, HD]), ALU.mult).then_inc(g.sem, 1)

                    elif step == "state_low":
                        g = state_step[s]
                        dve.wait_ge(p_state[s].sem, p_state[s].at(t, l + 1))
                        dve.tensor_scalar(floor[s][:], bank("state", s, l)[:, NB * D:NB * D + J * HEADS], EPS,
                                          EPS_NORM, ALU.add, ALU.mult).then_inc(g.sem, 1)
                        dve.wait_ge(g.sem, g.at(t, 3 * l + 1))
                        dve.tensor_tensor(floor[s][:], floor[s][:], floor[s][:], ALU.mult).then_inc(g.sem, 1)
                        dve.tensor_tensor(state[s][:], bank("state", s, l)[:, 0:NB * D].rearrange(
                            "p (b d) -> p b d", b=NB), same_head[:].unsqueeze(1).to_broadcast([P, NB, D]),
                            ALU.mult).then_inc(g.sem, 1)

                    elif step == "qk":
                        if j < 2:
                            o = 1 - s
                            wait(dve, t, [(p_av[o], J * (l + 1 if s else l), 0)])
                        else:
                            dve.wait_ge(p_av[s].sem, p_av[s].at(t, J * l + j - 1))
                        for n in range(2):
                            k = 2 * (J * l + j) + n + 1
                            dve.wait_ge(p_qk[s].sem, p_qk[s].at(t, k))
                            dve.tensor_tensor(att[:, j % 2, HALF * n:HALF * n + HALF, :],
                                              bank("qk", s, l, j, n)[:].rearrange("p (h t) -> p h t", h=HALF),
                                              causal[:].unsqueeze(1).to_broadcast([P, HALF, P]), ALU.mult)\
                                .then_inc(att_made[s].sem, 1)

                    elif step == "chain":
                        g, k = norm_step[s], NORM * l
                        dve.wait_ge(sq_made[s].sem, sq_made[s].at(t, l + 1))
                        dve.tensor_reduce(m2[s][:], sq[s][:], AX_X, ALU.add).then_inc(g.sem, 1)
                        dve.wait_ge(g.sem, g.at(t, k + 1))
                        dve.tensor_tensor(m2[s][:], m2[s][:], floor[s][:], ALU.max).then_inc(g.sem, 1)
                        dve.wait_ge(g.sem, g.at(t, k + 2))
                        dve.tensor_scalar(mh[s][:], m2[s][:], -0.5, None, ALU.mult).then_inc(g.sem, 1)
                        dve.tensor_scalar(y[s][:].bitcast(I32), m2[s][:].bitcast(I32), -0.5, RSQRT_SEED,
                                          ALU.mult, ALU.add).then_inc(g.sem, 1)
                        for n in range(3):
                            dve.wait_ge(g.sem, g.at(t, k + 4 + 3 * n))
                            dve.tensor_tensor(yy[s][:], y[s][:], y[s][:], ALU.mult).then_inc(g.sem, 1)
                            dve.wait_ge(g.sem, g.at(t, k + 5 + 3 * n))
                            dve.tensor_tensor(yy[s][:], yy[s][:], mh[s][:], ALU.mult).then_inc(g.sem, 1)
                            dve.wait_ge(g.sem, g.at(t, k + 6 + 3 * n))
                            dve.scalar_tensor_tensor(out=y[s][:], in0=yy[s][:], scalar=1.5, in1=y[s][:],
                                                     op0=ALU.add, op1=ALU.mult).then_inc(g.sem, 1)
                        dve.wait_ge(g.sem, g.at(t, k + 13))
                        dve.tensor_tensor(sq[s][:], bank("av", s, l)[:].rearrange("p (a e) -> p a e", e=HD),
                                          y[s][:].unsqueeze(2).to_broadcast([P, J * HEADS, HD]), ALU.mult)\
                            .then_inc(g.sem, 1)

                    elif step == "wo":
                        dve.wait_ge(p_wo[s].sem, p_wo[s].at(t, l + 1))
                        dve.wait_ge(x_step[s].sem, x_step[s].at(t, 4 * l + 2))
                        dve.tensor_tensor(x[s][:], x[s][:], bank("wo", s, l)[:].rearrange("p (j d) -> p j d", j=J),
                                          ALU.add).then_inc(x_step[s].sem, 1)

                    elif step == "f2":
                        dve.wait_ge(p_f2[s].sem, p_f2[s].at(t, l + 1))
                        dve.wait_ge(x_step[s].sem, x_step[s].at(t, 4 * l + 4))
                        dve.tensor_tensor(x[s][:], x[s][:], bank("f2", s, l)[:].rearrange("p (j d) -> p j d", j=J),
                                          ALU.add).then_inc(x_step[s].sem, 1)

                    elif step == "head":
                        wait(dve, t, [(h_stored[s], 0, 0)])
                        for n in range(2):
                            dve.wait_ge(p_head[s].sem, p_head[s].at(t, n + 1))
                            dve.tensor_tensor(h_out[s][:, 2 * n:2 * n + 2, :],
                                              bank("head", s, n)[:].rearrange("p (j v) -> p j v", j=2),
                                              b_head[:].unsqueeze(1).to_broadcast([P, 2, V]), ALU.add)\
                                .then_inc(h_made[s].sem, 1)

            turns(dve, order, body)

        @block.scalar
        def _(act):
            for n, (raw, pair, u) in enumerate(split):
                act.wait_ge(scaled, n + 1)
                act.activation(pair[0][:], raw, ACT.Copy).then_inc(w_high, 1)
            act.wait_ge(shifted, 1)
            for n in range(TAPS):
                act.activation(taps[:].rearrange("p h t -> p (h t)")[:, 512 * n:512 * n + 512], ps[3 + n][:],
                               ACT.Copy).then_inc(w_high, 1)
            act.wait_ge(ready, 1)
            def body(i, steps):
                for step, s, l, j, ahead in steps:
                    t = i + ahead
                    if step == "ln":
                        act.wait_ge(p_xT[s].sem, p_xT[s].at(t, l + 1))
                        act.activation(xT[s][0][:], bank("xT", s, l)[:], ACT.Copy).then_inc(xT_high[s].sem, 1)

                    elif step == "q":
                        act.wait_ge(p_q[s].sem, p_q[s].at(t, l + 1))
                        wait(act, t, [(q_spread[s], Q_DMAS * l, 0)])
                        act.activation(qT[s][:, 0, :], bank("q", s, l)[:], ACT.Identity, bias=b_q[:, l:l + 1])\
                            .then_inc(q_high[s].sem, 1)
                        act.activation(qT_last[s][:], bank("q", s, l)[:, NB * P:J * P], ACT.Identity,
                                       bias=b_q[:, l:l + 1]).then_inc(q_high[s].sem, 1)

                    elif step == "conv":
                        act.wait_ge(p_conv[s].sem, p_conv[s].at(t, 2 * l + j + 1))
                        src = bank("conv", s, l, j)[:].rearrange("p (h j v e) -> p h j v e", h=HALF, j=J, v=2)
                        act.activation(vc[s][:].rearrange("p j (h e) -> p h j e", h=HEADS)[:, HALF * j:HALF * j + HALF],
                                       src[:, :, :, 1, :], ACT.Copy).then_inc(vc_made[s].sem, 1)
                        act.activation(kc[s][:].rearrange("p j (h e) -> p h j e", h=HEADS)[:, HALF * j:HALF * j + HALF],
                                       src[:, :, :, 0, :], ACT.Copy).then_inc(kc_made[s].sem, 1)

                    elif step == "turn_v":
                        act.wait_ge(p_vT[s].sem, p_vT[s].at(t, l + 1))
                        act.activation(vT[s][:], bank("vT", s, l)[:], ACT.Copy).then_inc(vT_made[s].sem, 1)

                    elif step == "repeat":
                        act.wait_ge(vc_made[s].sem, vc_made[s].at(t, 2 * l + j + 1))
                        for g in range(PAIRS_A // 2 * j, PAIRS_A // 2 * j + PAIRS_A // 2):
                            v = vc[s][:, :, BLOCK * g:BLOCK * g + BLOCK].unsqueeze(2)
                            act.activation(v_thrice[s][:, :, g, :, :],
                                           v.to_broadcast([P, J, len(Q_PARTS), BLOCK]), ACT.Copy)\
                                .then_inc(v_repeated[s].sem, 1)

                    elif step == "rows":
                        k = PAIRS_A * l + j + 1
                        act.wait_ge(p_rows[s].sem, p_rows[s].at(t, k))
                        act.activation(v_rows[s][0:ROWS, j, :], bank("rows", s, l, j)[0:ROWS, :], ACT.Copy)\
                            .then_inc(v_high[s].sem, 1)

                    elif step == "norm":
                        act.wait_ge(p_av[s].sem, p_av[s].at(t, J * (l + 1)))
                        act.activation(sq[s][:].rearrange("p a e -> p (a e)"), bank("av", s, l)[:], ACT.Square)\
                            .then_inc(sq_made[s].sem, 1)

                    elif step == "unit":
                        act.wait_ge(p_unit[s].sem, p_unit[s].at(t, l + 1))
                        act.activation(oTn[s][:], bank("unit", s, l)[:], ACT.Copy).then_inc(oTn_made[s].sem, 1)

                    elif step == "f1":
                        act.wait_ge(p_f1[s].sem, p_f1[s].at(t, FC * l + j + 1))
                        act.activation(gl[s][:, j, :], bank("f1", s, l, j)[:], ACT.Gelu_apprx_tanh,
                                       bias=b_f1[:, l, j:j + 1]).then_inc(gl_made[s].sem, 1)

            turns(act, order, body)

        @block.tensor
        def _(pe):
            pe.wait_ge(loaded, 16 * len(loads))
            pe.wait_ge(prep, LN + 2 * L)
            for l in range(L):
                pe.matmul(ps[0][:, l:l + 1], raw_q[:, l, :], ln_b[:, 2 * l:2 * l + 1], start=(l == 0), stop=True,
                          skip_group_check=True)
            for l in range(L):
                for f in range(FC):
                    n = L + FC * l + f
                    pe.matmul(ps[0][:, n:n + 1], raw_f1[:, l, P * f:P * f + P], ln_b[:, 2 * l + 1:2 * l + 2],
                              start=False, stop=True, skip_group_check=True)
            for l in range(L):
                pe.matmul(ps[1][:, 2 * D * l:2 * D * l + 2 * D], ln_b_rows[:, 2 * l, :], raw_kv[:, l, :],
                          start=(l == 0), stop=True, skip_group_check=True)
            pe.matmul(ps[2][:, 0:V], ln_b_rows[:, 2 * L, :], raw_head, start=True, stop=True)
            for n in range(TAPS):
                ins = pe.matmul(ps[3 + n][:], flip, delayed[:, 512 * n:512 * n + 512], start=True, stop=True)
            ins.then_inc(shifted, 1)
            pe.wait_ge(ready, 1)

            def product(out, lhsT, rhs, start=True, stop=True, **kw):
                pe.matmul(out, lhsT[0], rhs[0], start=start, stop=False, **kw)
                pe.matmul(out, lhsT[0], rhs[1], start=False, stop=False, **kw)
                return pe.matmul(out, lhsT[1], rhs[0], start=False, stop=stop, **kw)

            def body(i, steps):
                def claim(*name, inputs=()):
                    wait(pe, i, [(sig, k, ahead) for sig, k in inputs] + banks.last_reads(name, i))
                    return bank(*name)

                for step, s, l, j, ahead in steps:
                    t = i + ahead
                    if step == "ln":
                        out = claim("xT", s, l)
                        for j in range(J):
                            pe.wait_ge(xn_made[s].sem, xn_made[s].at(t, J * l + j + 1))
                            ins = pe.transpose(out[:, P * j:P * j + P], xn[s][:, j, :], ident[:])
                        ins.then_inc(p_xT[s].sem, 1)

                    elif step == "q":
                        out = claim("q", s, l, inputs=[(xT_low[s], 2 * l + 1)])
                        product(out[:], [w[:] for w in w_q[l]], [t[:] for t in xT[s]]).then_inc(p_q[s].sem, 1)

                    elif step == "kv":
                        out = claim("kv", s, l, j)
                        for b in range(NB):
                            c = slice(P * (NB * j + b), P * (NB * j + b) + P)
                            ins = product(out[:, 2 * D * b:2 * D * b + 2 * D], [t[:, c] for t in xT[s]],
                                          [w[:] for w in w_kv[l]])
                        ins.then_inc(p_kv[s].sem, 1)

                    elif step == "conv":
                        out = claim("conv", s, l, j, inputs=[(kv_made[s], 2 * l + 2)])[:].rearrange("p (h w) -> p h w", h=HALF)
                        w = 2 * HD * NB
                        for h in range(HALF):
                            hh = HALF * j + h
                            src = kv[s][:, hh].rearrange("p c b v e -> p (c b v e)")
                            pe.matmul(out[:, h, :], taps[:, hh, 0:P], src, start=(h == 0), stop=True,
                                      skip_group_check=True)
                            ins = pe.matmul(out[:, h, w:2 * w], taps[:, hh, P:2 * P], src[:, 0:w], start=False,
                                            stop=True, skip_group_check=True)
                        ins.then_inc(p_conv[s].sem, 1)

                    elif step == "turn_v":
                        pe.wait_ge(vc_made[s].sem, vc_made[s].at(t, 2 * l + 2))
                        out = claim("vT", s, l)
                        for j in range(J):
                            ins = pe.transpose(out[:, P * j:P * j + P], vc[s][:, j, :], ident[:])
                        ins.then_inc(p_vT[s].sem, 1)

                    elif step == "rows":
                        pe.wait_ge(v_repeated[s].sem, v_repeated[s].at(t, PAIRS_A * l + j + 1))
                        out = claim("rows", s, l, j)
                        for c in range(J):
                            v = v_thrice[s][:, c, j, :, :].rearrange("p n e -> p (n e)")
                            ins = pe.transpose(out[0:ROWS, P * c:P * c + P], v, ident[:])
                        ins.then_inc(p_rows[s].sem, 1)

                    elif step == "gate":
                        out = claim("vg", s, l, inputs=[(vT_made[s], l + 1)])
                        for j in range(J):
                            ins = pe.matmul(out[:, P * j:P * j + P], vT[s][:, P * j:P * j + P], w_gate[l][:],
                                            start=True, stop=True)
                        ins.then_inc(p_vg[s].sem, 1)

                    elif step == "state":
                        out = claim("state", s, l, inputs=[(gate_step[s], 6 * l + 6)])
                        for b in range(NB):
                            pe.matmul(out[:, D * b:D * b + D], vc[s][:, b, :], gk_heads[:, b], start=(b == 0),
                                      stop=True, skip_group_check=True)
                        z, w = NB * D, NB * HEADS
                        pe.matmul(out[:, z:z + 2 * w], causal[:], gate[s][:], start=False, stop=False,
                                  skip_group_check=True)
                        pe.matmul(out[:, z + w:z + 2 * w], ones[:], gate[s][:, 0:w], start=False, stop=True,
                                  skip_group_check=True).then_inc(p_state[s].sem, 1)

                    elif step == "qk":
                        if j == 0:
                            pe.wait_ge(q_spread[s].sem, q_spread[s].at(t, Q_DMAS * (l + 1)))
                        c = slice(P * j, P * j + P)
                        for n in range(2):
                            first = j == 0 and n == 0
                            out = claim("qk", s, l, j, n, inputs=[(v_low[s], PAIRS_A * (l + 1))] if first else [])
                            out = out[:].rearrange("p (h t) -> p h t", h=HALF)
                            rows = slice(0, ROWS)
                            for g in range(HALF // PAIR):
                                pair = HALF // PAIR * n + g
                                ins = pe.matmul(out[:, PAIR * g:PAIR * g + PAIR, :], v_rows[s][rows, pair, c],
                                                q_rows[rows, :, pair, c], start=True, stop=True)
                            ins.then_inc(p_qk[s].sem, 1)

                    elif step == "av":
                        if j == 0:
                            claim("av", s, l)
                        if j == NB:
                            pe.wait_ge(state_step[s].sem, state_step[s].at(t, 3 * l + 3))
                            pe.wait_ge(q_high[s].sem, q_high[s].at(t, 2 * l + 2))
                        out = bank("av", s, l)[:, P * j:P * j + P]
                        if j >= NB:
                            b = j - NB
                            pe.matmul(out, qT_last[s][:, P * b:P * b + P], state[s][:, b, :], start=True, stop=False)
                        for h in range(HEADS):
                            if h % HALF == 0:
                                k = 2 * (J * l + j) + h // HALF + 1
                                pe.wait_ge(att_made[s].sem, att_made[s].at(t, k))
                            ins = pe.matmul(out, att[:, j % 2, h, :], gk[:, j, h, :], start=(h == 0 and j < NB),
                                            stop=(h == HEADS - 1))
                        ins.then_inc(p_av[s].sem, 1)

                    elif step == "unit":
                        out = claim("unit", s, l, inputs=[(norm_step[s], NORM * (l + 1))])
                        for j in range(J):
                            o = sq[s][:, HEADS * j:HEADS * j + HEADS, :].rearrange("p h e -> p (h e)")
                            ins = pe.transpose(out[:, P * j:P * j + P], o, ident[:])
                        ins.then_inc(p_unit[s].sem, 1)

                    elif step == "wo":
                        pe.wait_ge(oTn_made[s].sem, oTn_made[s].at(t, l + 1))
                        out = claim("wo", s, l)
                        for j in range(J):
                            ins = pe.matmul(out[:, D * j:D * j + D], oTn[s][:, P * j:P * j + P], w_o[l][:],
                                            start=True, stop=True)
                        ins.then_inc(p_wo[s].sem, 1)

                    elif step == "f1":
                        out = claim("f1", s, l, j, inputs=[(xT_low[s], 2 * l + 2)] if j == 0 else [])
                        product(out[:], [w[:, P * j:P * j + P] for w in w_f1[l]], [t[:] for t in xT[s]])\
                            .then_inc(p_f1[s].sem, 1)

                    elif step == "f2":
                        out = claim("f2", s, l, inputs=[(gl_made[s], FC * l + 1)])
                        for f in range(FC):
                            if f > 0:
                                pe.wait_ge(gl_made[s].sem, gl_made[s].at(t, FC * l + f + 1))
                            for j in range(J):
                                ins = pe.matmul(out[:, D * j:D * j + D], gl[s][:, f, P * j:P * j + P],
                                                w_f2[l][:, f, :], start=(f == 0 and j == 0), stop=(f == FC - 1),
                                                skip_group_check=True)
                        ins.then_inc(p_f2[s].sem, 1)

                    elif step == "head":
                        for n in range(2):
                            out = claim("head", s, n, inputs=[(xT_low[s], LN)] if n == 0 else [])
                            for b in range(2):
                                c = slice(P * (2 * n + b), P * (2 * n + b) + P)
                                ins = product(out[:, V * b:V * b + V], [t[:, c] for t in xT[s]],
                                              [w[:] for w in w_head])
                            ins.then_inc(p_head[s].sem, 1)

                if i is FIRST:
                    wait(pe, 0, banks.reads_ahead())

            turns(pe, order, body)


DM = V
KC = DM // P
AH, DK = 16, 64
PAIRS = AH * DK // P
HID = 768
HC = HID // P
DEQUANT = 1.0 / 127.0
STAGE = 1024
MLP_AFTER = [1, 2, 3, 3, 4, 4, 4, 4, 4, 5, 5, 6, 6, 7, 7, 8, 9, 9, 10]


def attention_and_mlp(nc, semaphores, a, h_rows, out_rows):
    with ExitStack() as ctx:
        def sb(name, shape, dt=F32):
            return ctx.enter_context(nc.sbuf_tensor(name, shape, dt))

        def pair(name, shape):
            return [sb(name + h, shape, F32R) for h in ("_high", "_low")]

        def each(name, shape, dt=F32):
            return [sb(f"{name}{s}", shape, dt) for s in range(STREAMS)]

        def signals(name, per_turn):
            return [semaphores.counted(f"b_{name}{s}", per_turn) for s in range(STREAMS)]

        def sem(name):
            return semaphores.one(name)

        ident = sb("ident_b", [P, P])
        minus_half = sb("minus_half_b", [P, J])
        wv = pair("wv", [P, KC, AH * DK])
        wk = sb("wk", [P, KC, AH * DK])
        wo = pair("wo", [P, PAIRS, DM])
        wq = pair("wq", [P, PAIRS, DM])
        wg = pair("wg", [P, KC, HID])
        wu = pair("wu", [P, KC, HID])
        wd = pair("wd", [P, HC, DM])

        h = each("h", [P, J, DM])
        xn = each("bxn", [P, J, DM])
        xns = [pair(f"xns{s}", [P, J, DM]) for s in range(STREAMS)]
        xT = [pair(f"bxT{s}", [P, KC, TOK]) for s in range(STREAMS)]
        stats = each("bstats", [P, J, 6])
        mv = each("bmv", [P, J, 2])
        var = each("bvar", [P, J])
        rstd = each("brstd", [P, J])
        gram = [pair(f"gram{b}", [P, KC, DM]) for b in range(NB)]
        t1 = sb("t1", [P, KC, AH * DK])
        kvs = pair("kvs", [P, PAIRS, P])
        r = pair("r", [P, PAIRS, DM])
        m = [pair(f"m{b}", [P, KC, DM]) for b in range(NB)]
        silu = sb("silu", [P, 2, TOK])
        hid = sb("hid", [P, 2, TOK])
        hids = pair("hids", [P, 2, TOK])

        ps = [ctx.enter_context(nc.psum_tensor(f"bps{n}", [P, 512], F32)) for n in range(8)]

        ident_in, wk_in, cleared = sem("b_ident_in"), sem("b_wk_in"), sem("b_cleared")
        passed = sem("b_passed")
        scaled, split_high, split_low = sem("b_scaled"), sem("b_split_high"), sem("b_split_low")
        h_in = signals("h_in", 16)
        out_sent = signals("out_sent", 16 * NB)
        h_step = signals("h_step", NB + 2)
        ln_step = signals("ln_step", 6)
        ln_rstd = signals("ln_rstd", 2)
        xn_made = signals("xn_made", 2)
        xn_high = signals("xn_high", 1)
        xn_low = signals("xn_low", 1)
        xT_high = signals("xT_high", 2 * KC)
        xT_low = signals("xT_low", 2 * KC)
        gram_high, gram_low = signals("gram_high", NB), signals("gram_low", NB)
        t1_even, t1_odd = signals("t1_even", 2 * NB), signals("t1_odd", 2 * NB)
        kvs_high, kvs_low = signals("kvs_high", 2 * NB), signals("kvs_low", 2 * NB)
        r_high, r_low = signals("r_high", 4 * NB), signals("r_low", 4 * NB)
        m_high, m_low = signals("m_high", NB), signals("m_low", NB)
        silu_made = signals("silu_made", HC)
        hid_made, hid_high, hid_low = signals("hid_made", HC), signals("hid_high", HC), signals("hid_low", HC)
        p_xT = signals("p_xT", 2 * KC)
        p_gram = signals("p_gram", NB)
        p_t1 = signals("p_t1", 4 * NB)
        p_kv = signals("p_kv", 2 * NB)
        p_r = signals("p_r", 4 * NB)
        p_m = signals("p_m", NB)
        p_attn = signals("p_attn", NB)
        p_gate, p_up, p_down = signals("p_gate", HC), signals("p_up", HC), signals("p_down", HC)

        def half(s, o, ahead):
            attention = [("gram", s, 0, ahead), ("gram", s, 1, ahead)]
            for b in range(NB):
                attention += [(step, s, b, ahead) for step in ("t1", "kv", "r", "m", "attn")]
            mlp = [("scale", o, 1, 0), ("ln", o, 1, 0), ("up", o, 0, 0)]
            for f in range(1, HC):
                mlp += [("up", o, f, 0), ("down", o, f - 1, 0)]
            mlp += [("down", o, HC - 1, 0), ("add", o, 0, 0), ("load", o, 0, 1), ("stats", o, 0, 1), ("scale", o, 0, 1),
                    ("ln", o, 0, 1)]
            out = []
            for n, step in enumerate(attention):
                out.append(step)
                out += [mlp[k] for k in range(len(mlp)) if MLP_AFTER[k] == n]
            return out + [("stats", s, 1, ahead)]

        order = half(1, 0, 0) + half(0, 1, 1)
        products = []
        for step, s, b, ahead in order:
            if step == "ln":
                for k in range(KC):
                    products.append((("xT", s, b, k), None, xT_low[s], KC * b + k + 1, ahead))
            elif step == "gram":
                products.append((("gram", s, b), None, gram_low[s], b + 1, ahead))
            elif step == "t1":
                for n in range(2):
                    products.append((("t1", s, b, n, 0), None, t1_even[s], 2 * b + n + 1, ahead))
                    products.append((("t1", s, b, n, 1), None, t1_odd[s], 2 * b + n + 1, ahead))
            elif step == "kv":
                for n in range(2):
                    products.append((("kv", s, b, n), None, kvs_low[s], 2 * b + n + 1, ahead))
            elif step == "r":
                for n in range(4):
                    products.append((("r", s, b, n), None, r_low[s], 4 * b + n + 1, ahead))
            elif step == "m":
                products.append((("m", s, b), None, m_low[s], b + 1, ahead))
            elif step == "attn":
                products.append((("attn", s, b), None, h_step[s], b + 1, ahead))
            elif step == "up":
                products.append((("gate", s, b), None, silu_made[s], b + 1, ahead))
                products.append((("up", s, b), None, hid_made[s], b + 1, ahead))
            elif step == "down" and b == 0:
                for n in range(2):
                    products.append((("down", s, n), 6 + n, h_step[s], NB + n + 1, ahead))
        banks = Banks(range(6), products)

        def bank(*name):
            return ps[banks.bank[name]]

        stages = [t[:].rearrange("p n t -> p (n t)") for t in (silu, hid, h[1], xn[1])]
        landed = [sem(f"b_landed{n}") for n in range(len(stages))]
        pieces = []
        for w, src, is_int in ((wv, "W_vT", False), (wo, "W_oT", False), (wq, "W_q", False),
                               (wg, "w_gateT", True), (wu, "w_upT", True), (wd, "w_downT", True)):
            K, N = w[0].shape[1], w[0].shape[2]
            per = STAGE // N
            view = a[src].rearrange("(k p) n -> p k n", p=P)
            for k in range(0, K, per):
                pieces.append((w, k, min(per, K - k), N, view, is_int))

        integers = [n for n, piece in enumerate(pieces) if piece[-1]]
        due = {step: [n for n, piece in enumerate(pieces) if piece[0] is w] for step, w in (
            (("t1", 0), wv), (("r", 0), wo), (("m", 0), wq), (("attn", 0), wg), (("t1", 1), wu), (("kv", 1), wd))}

        def stage(n, dt=F32):
            _, _, cnt, N, _, _ = pieces[n]
            t = stages[n % len(stages)][:, 0:cnt * N]
            if dt != F32:
                t = t.bitcast(dt)
            return t.rearrange("p (k n) -> p k n", n=N)

        block = ctx.enter_context(nc.Block())

        @block.sync
        def _(sp):
            sp.dma_start(ident[:], a["ident"]).then_inc(ident_in, 16)

            def load_weights():
                for n, (w, k, cnt, N, view, is_int) in enumerate(pieces):
                    if n >= len(stages):
                        sp.wait_ge(split_low, n - len(stages) + 1)
                    sp.dma_start(stage(n, I32 if is_int else F32), view[:, k:k + cnt, :])\
                        .then_inc(landed[n % len(stages)], 16)
                    if n == len(due["t1", 0]) - 1:
                        sp.dma_start(wk[:], a["W_kT"].rearrange("(k p) n -> p k n", p=P)).then_inc(wk_in, 16)
                sp.wait_ge(split_low, len(pieces))

            def body(i, steps):
                for step, s, b, ahead in steps:
                    t = i + ahead
                    if step == "load":
                        sp.wait_ge(h_step[s].sem, h_step[s].at(t, 0))
                        sp.sem_inc(passed)
                        sp.dma_start(h[s][:], h_rows[t * STREAMS + s]).then_inc(h_in[s].sem, 16)
                        if i is FIRST and s == 0:
                            load_weights()
                    elif step == "add":
                        sp.wait_ge(h_step[s].sem, h_step[s].at(t, NB + 2))
                        sp.sem_inc(passed)
                        for b in range(NB):
                            sp.dma_start(out_rows[t * STREAMS + s, b], xn[s][:, b::NB, :])\
                                .then_inc(out_sent[s].sem, 16)
            turns(sp, order, body)
            for s in range(STREAMS):
                sp.wait_ge(out_sent[s].sem, out_sent[s].at(BODIES, 0))

        @block.gpsimd
        def _(pool):
            pool.memset(minus_half[:], -0.5)
            pool.memset(kvs[0][:].bitcast(F32), 0.0)
            pool.memset(kvs[1][:].bitcast(F32), 0.0).then_inc(cleared, 1)
            def body(i, steps):
                for step, s, b, ahead in steps:
                    t = i + ahead
                    if step == "stats":
                        pool.wait_ge(ln_step[s].sem, ln_step[s].at(t, 3 * b + 3))
                        pool.tensor_tensor(rstd[s][:], var[s][:], minus_half[:], ALU.pow)\
                            .then_inc(ln_rstd[s].sem, 1)
                    elif step == "scale" and b == 0:
                        pool.wait_ge(xn_made[s].sem, xn_made[s].at(t, 1))
                        pool.sem_inc(passed)
                        pool.tensor_scalar(xns[s][0][:], xn[s][:], 1.0, 0.0, ALU.mult, ALU.add)\
                            .then_inc(xn_high[s].sem, 1)
                    elif step == "up":
                        f = b
                        pool.wait_ge(hid_high[s].sem, hid_high[s].at(t, f + 1))
                        pool.tensor_tensor(hids[1][:, f % 2, :], hid[:, f % 2, :], hids[0][:, f % 2, :].bitcast(F32),
                                           ALU.subtract).then_inc(hid_low[s].sem, 1)
            turns(pool, order, body)

        @block.vector
        def _(dve):
            def prepare(numbers):
                for n in numbers:
                    if n in integers:
                        dve.wait_ge(landed[n % len(stages)], 16 * (n // len(stages) + 1))
                        dve.tensor_scalar(stage(n), stage(n, I32), DEQUANT, None, ALU.mult).then_inc(scaled, 1)
                for n in numbers:
                    w, k, cnt = pieces[n][:3]
                    dve.wait_ge(split_high, n + 1)
                    dve.tensor_tensor(w[1][:, k:k + cnt, :], stage(n), w[0][:, k:k + cnt, :].bitcast(F32),
                                      ALU.subtract).then_inc(split_low, 1)

            dve.wait_ge(cleared, 1)

            def body(i, steps):
                for step, s, b, ahead in steps:
                    t = i + ahead
                    if i is FIRST and (step, b) in due:
                        prepare(due[step, b])
                    if step == "stats":
                        if b == 0:
                            dve.wait_ge(h_in[s].sem, h_in[s].at(t, 16))
                        else:
                            dve.wait_ge(h_step[s].sem, h_step[s].at(t, NB))
                        for j in range(J):
                            ins = dve.bn_stats(stats[s][:, j, :], h[s][:, j, :])
                        ins.then_inc(ln_step[s].sem, 1)
                        dve.wait_ge(ln_step[s].sem, ln_step[s].at(t, 3 * b + 1))
                        dve.sem_inc(passed)
                        for j in range(J):
                            ins = dve.bn_aggr(mv[s][:, j, :], stats[s][:, j, :])
                        ins.then_inc(ln_step[s].sem, 1)
                        dve.wait_ge(ln_step[s].sem, ln_step[s].at(t, 3 * b + 2))
                        dve.tensor_scalar(var[s][:], mv[s][:, :, 1], EPS_LN_B, None, ALU.add)\
                            .then_inc(ln_step[s].sem, 1)

                    elif step == "scale":
                        if b == 0:
                            dve.wait_ge(out_sent[s].sem, out_sent[s].at(t, 0))
                            dve.sem_inc(passed)
                        dve.wait_ge(ln_rstd[s].sem, ln_rstd[s].at(t, b + 1))
                        for j in range(J):
                            ins = dve.tensor_scalar(xn[s][:, j, :], h[s][:, j, :], mv[s][:, j, 0:1],
                                                    rstd[s][:, j:j + 1], ALU.subtract, ALU.mult)
                        ins.then_inc(xn_made[s].sem, 1)

                    elif step == "ln":
                        for k in range(KC):
                            dve.wait_ge(xT_high[s].sem, xT_high[s].at(t, KC * b + k + 1))
                            dve.tensor_tensor(xT[s][1][:, k, :], bank("xT", s, b, k)[:],
                                              xT[s][0][:, k, :].bitcast(F32), ALU.subtract)\
                                .then_inc(xT_low[s].sem, 1)
                        if b == 0:
                            dve.wait_ge(xn_high[s].sem, xn_high[s].at(t, 1))
                            dve.tensor_tensor(xns[s][1][:], xn[s][:], xns[s][0][:].bitcast(F32), ALU.subtract)\
                                .then_inc(xn_low[s].sem, 1)

                    elif step == "gram":
                        dve.wait_ge(gram_high[s].sem, gram_high[s].at(t, b + 1))
                        dve.tensor_tensor(gram[b][1][:].rearrange("p k n -> p (k n)"), bank("gram", s, b)[:],
                                          gram[b][0][:].rearrange("p k n -> p (k n)").bitcast(F32), ALU.subtract)\
                            .then_inc(gram_low[s].sem, 1)

                    elif step == "t1":
                        for n in range(2):
                            dve.wait_ge(p_t1[s].sem, p_t1[s].at(t, 4 * b + 2 * n + 2))
                            dve.tensor_copy(t1[:, 1, 512 * n:512 * n + 512], bank("t1", s, b, n, 1)[:])\
                                .then_inc(t1_odd[s].sem, 1)

                    elif step == "kv":
                        for n in range(2):
                            dve.wait_ge(kvs_high[s].sem, kvs_high[s].at(t, 2 * b + n + 1))
                            src = bank("kv", s, b, n)[:].rearrange("p (q d) -> p q d", d=P)
                            for e in range(2):
                                r_, c_ = slice(DK * e, DK * e + DK), slice(DK * e, DK * e + DK)
                                ins = dve.scalar_tensor_tensor(
                                    out=kvs[1][r_, 4 * n:4 * n + 4, c_], in0=src[r_, :, c_], scalar=DK ** -0.5,
                                    in1=kvs[0][r_, 4 * n:4 * n + 4, c_].bitcast(F32), op0=ALU.mult,
                                    op1=ALU.subtract)
                            ins.then_inc(kvs_low[s].sem, 1)

                    elif step == "r":
                        for n in range(4):
                            dve.wait_ge(r_high[s].sem, r_high[s].at(t, 4 * b + n + 1))
                            dve.tensor_tensor(r[1][:, 2 * n:2 * n + 2, :].rearrange("p k n -> p (k n)"),
                                              bank("r", s, b, n)[:],
                                              r[0][:, 2 * n:2 * n + 2, :].rearrange("p k n -> p (k n)").bitcast(F32),
                                              ALU.subtract).then_inc(r_low[s].sem, 1)

                    elif step == "m":
                        dve.wait_ge(m_high[s].sem, m_high[s].at(t, b + 1))
                        dve.tensor_tensor(m[b][1][:].rearrange("p k n -> p (k n)"), bank("m", s, b)[:],
                                          m[b][0][:].rearrange("p k n -> p (k n)").bitcast(F32), ALU.subtract)\
                            .then_inc(m_low[s].sem, 1)

                    elif step == "attn":
                        dve.wait_ge(p_attn[s].sem, p_attn[s].at(t, b + 1))
                        dve.tensor_tensor(h[s][:, b::NB, :], h[s][:, b::NB, :],
                                          bank("attn", s, b)[:].rearrange("p (c n) -> p c n", c=C), ALU.add)\
                            .then_inc(h_step[s].sem, 1)

                    elif step == "up":
                        f = b
                        dve.wait_ge(p_up[s].sem, p_up[s].at(t, f + 1))
                        dve.wait_ge(silu_made[s].sem, silu_made[s].at(t, f + 1))
                        o = 1 - s
                        if f < 2:
                            dve.wait_ge(hid_low[o].sem, hid_low[o].at(t, HC * s))
                        else:
                            dve.wait_ge(hid_low[s].sem, hid_low[s].at(t, f - 1))
                        dve.tensor_tensor(hid[:, f % 2, :], silu[:, f % 2, :], bank("up", s, f)[:], ALU.mult)\
                            .then_inc(hid_made[s].sem, 1)

                    elif step == "add":
                        dve.wait_ge(p_down[s].sem, p_down[s].at(t, HC))
                        for n in range(2):
                            dve.tensor_tensor(xn[s][:, 2 * n:2 * n + 2, :], h[s][:, 2 * n:2 * n + 2, :],
                                              bank("down", s, n)[:].rearrange("p (j n) -> p j n", j=2), ALU.add)\
                                .then_inc(h_step[s].sem, 1)
            turns(dve, order, body)

        @block.scalar
        def _(act):
            def prepare(numbers):
                for n in numbers:
                    w, k, cnt = pieces[n][:3]
                    if n in integers:
                        act.wait_ge(scaled, integers.index(n) + 1)
                    else:
                        act.wait_ge(landed[n % len(stages)], 16 * (n // len(stages) + 1))
                    act.activation(w[0][:, k:k + cnt, :], stage(n), ACT.Copy).then_inc(split_high, 1)

            act.wait_ge(cleared, 1)

            def body(i, steps):
                for step, s, b, ahead in steps:
                    t = i + ahead
                    if i is FIRST and (step, b) in due:
                        prepare(due[step, b])
                    if step == "ln":
                        for k in range(KC):
                            act.wait_ge(p_xT[s].sem, p_xT[s].at(t, KC * b + k + 1))
                            act.activation(xT[s][0][:, k, :], bank("xT", s, b, k)[:], ACT.Copy)\
                                .then_inc(xT_high[s].sem, 1)

                    elif step == "gram":
                        act.wait_ge(p_gram[s].sem, p_gram[s].at(t, b + 1))
                        act.activation(gram[b][0][:].rearrange("p k n -> p (k n)"), bank("gram", s, b)[:], ACT.Copy)\
                            .then_inc(gram_high[s].sem, 1)

                    elif step == "t1":
                        for n in range(2):
                            act.wait_ge(p_t1[s].sem, p_t1[s].at(t, 4 * b + 2 * n + 1))
                            act.activation(t1[:, 0, 512 * n:512 * n + 512], bank("t1", s, b, n, 0)[:], ACT.Copy)\
                                .then_inc(t1_even[s].sem, 1)

                    elif step == "kv":
                        for n in range(2):
                            act.wait_ge(p_kv[s].sem, p_kv[s].at(t, 2 * b + n + 1))
                            src = bank("kv", s, b, n)[:].rearrange("p (q d) -> p q d", d=P)
                            for e in range(2):
                                r_, c_ = slice(DK * e, DK * e + DK), slice(DK * e, DK * e + DK)
                                ins = act.activation(kvs[0][r_, 4 * n:4 * n + 4, c_], src[r_, :, c_], ACT.Copy,
                                                     scale=DK ** -0.5)
                            ins.then_inc(kvs_high[s].sem, 1)

                    elif step == "r":
                        for n in range(4):
                            act.wait_ge(p_r[s].sem, p_r[s].at(t, 4 * b + n + 1))
                            act.activation(r[0][:, 2 * n:2 * n + 2, :].rearrange("p k n -> p (k n)"),
                                           bank("r", s, b, n)[:], ACT.Copy).then_inc(r_high[s].sem, 1)

                    elif step == "m":
                        act.wait_ge(p_m[s].sem, p_m[s].at(t, b + 1))
                        act.activation(m[b][0][:].rearrange("p k n -> p (k n)"), bank("m", s, b)[:], ACT.Copy)\
                            .then_inc(m_high[s].sem, 1)

                    elif step == "up":
                        f, o = b, 1 - s
                        act.wait_ge(p_gate[s].sem, p_gate[s].at(t, f + 1))
                        if f < 2:
                            act.wait_ge(hid_made[o].sem, hid_made[o].at(t, HC * s))
                        else:
                            act.wait_ge(hid_made[s].sem, hid_made[s].at(t, f - 1))
                        act.activation(silu[:, f % 2, :], bank("gate", s, f)[:], ACT.Silu)\
                            .then_inc(silu_made[s].sem, 1)
                        act.wait_ge(hid_made[s].sem, hid_made[s].at(t, f + 1))
                        if f < 2:
                            act.wait_ge(p_down[o].sem, p_down[o].at(t, HC * s))
                        else:
                            act.wait_ge(p_down[s].sem, p_down[s].at(t, f - 1))
                        act.activation(hids[0][:, f % 2, :], hid[:, f % 2, :], ACT.Copy)\
                            .then_inc(hid_high[s].sem, 1)
            turns(act, order, body)

        @block.tensor
        def _(pe):
            pe.wait_ge(ident_in, 16)
            pe.wait_ge(cleared, 1)

            def product(out, lhsT, rhs, start=True, stop=True, **kw):
                pe.matmul(out, lhsT[0], rhs[0], start=start, stop=False, **kw)
                pe.matmul(out, lhsT[0], rhs[1], start=False, stop=False, **kw)
                return pe.matmul(out, lhsT[1], rhs[0], start=False, stop=stop, **kw)

            def body(i, steps):
                def claim(*name, inputs=()):
                    wait(pe, i, [*inputs, *banks.last_reads(name, i)])
                    return bank(*name)

                for step, s, b, ahead in steps:
                    t = i + ahead
                    if i is FIRST and step in ("t1", "r", "m") and b == 0:
                        pe.wait_ge(split_low, due[step, b][-1] + 1)
                    if i is FIRST and step == "kv" and b == 0:
                        pe.wait_ge(wk_in, 16)
                    if step == "ln":
                        pe.wait_ge(xn_made[s].sem, xn_made[s].at(t, b + 1))
                        for k in range(KC):
                            out = claim("xT", s, b, k)
                            for j in range(J):
                                ins = pe.transpose(out[:, P * j:P * j + P], xn[s][:, j, P * k:P * k + P], ident[:])
                            ins.then_inc(p_xT[s].sem, 1)

                    elif step == "gram":
                        pe.wait_ge(xn_low[s].sem, xn_low[s].at(t, 1))
                        out = claim("gram", s, b)
                        for k in range(KC):
                            for c in range(C):
                                j = NB * c + b
                                ins = product(out[:, DM * k:DM * k + DM], [t[:, j, P * k:P * k + P] for t in xns[s]],
                                              [t[:, j, :] for t in xns[s]], start=(c == 0), stop=(c == C - 1))
                        ins.then_inc(p_gram[s].sem, 1)

                    elif step == "t1":
                        for n in range(2):
                            for k in range(KC):
                                out = claim("t1", s, b, n, k, inputs=[(gram_low[s], b + 1, ahead)])
                                for q in range(KC):
                                    ins = product(out[:], [t[:, q, P * k:P * k + P] for t in gram[b]],
                                                  [w[:, q, 512 * n:512 * n + 512] for w in wv],
                                                  start=(q == 0), stop=(q == KC - 1))
                                ins.then_inc(p_t1[s].sem, 1)

                    elif step == "kv":
                        for n in range(2):
                            out = claim("kv", s, b, n, inputs=[(t1_even[s], 2 * b + n + 1, ahead), (t1_odd[s], 2 * b + n + 1, ahead)])
                            for q in range(PAIRS // 2):
                                c = slice(P * (4 * n + q), P * (4 * n + q) + P)
                                for k in range(KC):
                                    ins = pe.matmul(out[:, P * q:P * q + P], t1[:, k, c], wk[:, k, c],
                                                    start=(k == 0), stop=(k == KC - 1))
                            ins.then_inc(p_kv[s].sem, 1)

                    elif step == "r":
                        for n in range(4):
                            out = claim("r", s, b, n, inputs=[(kvs_low[s], 2 * b + n // 2 + 1, ahead)])
                            for q in range(2):
                                ins = product(out[:, DM * q:DM * q + DM], [t[:, 2 * n + q, :] for t in kvs],
                                              [w[:, 2 * n + q, :] for w in wo])
                            ins.then_inc(p_r[s].sem, 1)

                    elif step == "m":
                        out = claim("m", s, b, inputs=[(r_low[s], 4 * b + 1, ahead)])
                        for k in range(KC):
                            for q in range(PAIRS):
                                if k == 0 and q % 2 == 0 and q > 0:
                                    pe.wait_ge(r_low[s].sem, r_low[s].at(t, 4 * b + q // 2 + 1))
                                ins = product(out[:, DM * k:DM * k + DM], [w[:, q, P * k:P * k + P] for w in wq],
                                              [t[:, q, :] for t in r], start=(q == 0), stop=(q == PAIRS - 1))
                        ins.then_inc(p_m[s].sem, 1)

                    elif step == "attn":
                        out = claim("attn", s, b, inputs=[(m_low[s], b + 1, ahead), (xT_low[s], KC, ahead)])
                        for c in range(C):
                            j = NB * c + b
                            for k in range(KC):
                                ins = product(out[:, DM * c:DM * c + DM], [t[:, k, P * j:P * j + P] for t in xT[s]],
                                              [t[:, k, :] for t in m[b]], start=(k == 0), stop=(k == KC - 1))
                        ins.then_inc(p_attn[s].sem, 1)

                    elif step == "up":
                        f = b
                        for w, name, sig in ((wg, "gate", p_gate), (wu, "up", p_up)):
                            out = claim(name, s, f, inputs=[(xT_low[s], 2 * KC, ahead)] if f == 0 else [])
                            for k in range(KC):
                                ins = product(out[:], [t[:, k, P * f:P * f + P] for t in w],
                                              [t[:, k, :] for t in xT[s]], start=(k == 0), stop=(k == KC - 1))
                            ins.then_inc(sig[s].sem, 1)

                    elif step == "down":
                        f = b
                        pe.wait_ge(hid_low[s].sem, hid_low[s].at(t, f + 1))
                        for j in range(J):
                            if f == 0 and j % 2 == 0:
                                claim("down", s, j // 2)
                            out = bank("down", s, j // 2)
                            ins = product(out[:, DM * (j % 2):DM * (j % 2) + DM],
                                          [t[:, f % 2, P * j:P * j + P] for t in hids],
                                          [w[:, f, :] for w in wd], start=(f == 0 and j % 2 == 0),
                                          stop=(f == HC - 1), skip_group_check=True)
                        ins.then_inc(p_down[s].sem, 1)

                if i is FIRST:
                    pe.wait_ge(split_low, len(pieces))
                    wait(pe, 0, banks.reads_ahead())

            turns(pe, order, body)



def layout(t):
    import numpy as np
    g = {k[len("L0_tok_"):]: np.asarray(v) for k, v in t.items() if k.startswith("L0_tok_")}
    ids = np.asarray(t["x"]).reshape(GROUPS, NB, C, P).transpose(0, 3, 2, 1).reshape(GROUPS, P, J)
    position = np.arange(SEQ)[:, None]
    div = np.exp(np.arange(0, D, 2) * (-np.log(10000.0) / D))
    pe = np.zeros((SEQ, D), np.float32)
    pe[:, 0::2] = np.sin(position * div)
    pe[:, 1::2] = np.cos(position * div)
    r = np.arange(P)
    filters = np.concatenate([np.zeros((HEADS, P - 1), np.float32), g["spectral_basis"].T], 1)
    ln = lambda k: np.stack([g[f"ln1_{k}"][0], g[f"ln2_{k}"][0], g[f"ln1_{k}"][1], g[f"ln2_{k}"][1],
                             g[f"lnf_{k}"]], 1)
    out = {
        "token_ids": np.concatenate([ids, np.zeros((STREAMS, P, J), ids.dtype)]),
        "pos": pe, "ident": np.eye(P, dtype=np.float32), "flip": np.eye(P, dtype=np.float32)[::-1],
        "causal": (r[:, None] <= r[None, :]).astype(np.float32),
        "same_head": (r[:, None] // HD == r[None, :] // HD).astype(np.float32),
        "filters": filters, "ln_s": ln("s"), "ln_b": ln("b"),
        "b_q": g["wq_b"].T, "b_f1": g["ff1_b"].reshape(LAYERS, FC, P).transpose(2, 0, 1),
    }
    for k in ("embed", "wq_k", "wk_k", "wv_k", "wo_k", "wk_b", "wv_b", "wo_b", "gate_k", "gate_b", "ff1_k", "ff2_k",
              "ff2_b", "out_k", "out_b"):
        out[k] = g[k]
    at, ff = "L0_attn_", "L0_ffn_"
    out["W_q"] = np.asarray(t[at + "W_q"])
    for k in ("W_k", "W_v", "W_o"):
        out[k + "T"] = np.asarray(t[at + k]).T
    for k in ("w_gate", "w_up", "w_down"):
        out[k + "T"] = np.asarray(t[ff + k]).T
    return {k: np.ascontiguousarray(v) for k, v in out.items()}


def kernel(**inputs):
    import numpy as np
    import concourse.bacc as bacc
    from concourse.bass_utils import run_bass_kernel_spmd

    arrays = {f"in_{k}": v for k, v in layout(inputs).items()}
    nc = bacc.Bacc("TRN2", target_bir_lowering=False, num_devices=1)
    a = {k[3:]: nc.dram_tensor(k, v.shape, mybir.dt.from_np(v.dtype), kind="ExternalInput").ap()
         for k, v in arrays.items()}
    h_rows = nc.dram_tensor("h_rows", (GROUPS, P, J, V), F32).ap()
    out = nc.dram_tensor("out", (BATCH, SEQ, V), F32, kind="ExternalOutput").ap()
    with ExitStack() as ctx:
        semaphores = Semaphores(ctx, nc)
        token_tower(nc, semaphores, a, h_rows)
        semaphores.retire(BODIES)
        attention_and_mlp(nc, semaphores, a, h_rows, out.rearrange("(g b) (c p) n -> g b p c n", b=NB, p=P))
    r = run_bass_kernel_spmd(nc, [arrays], core_ids=[0])
    return r.results[0]["out"]
```
